# Optimizing a Trainium2 kernel written in Bass

```python
import numpy as np
import jax
import jax.numpy as jnp

def _softmax(x, axis=-1):
    return jax.nn.softmax(x, axis=axis)

def _gelu(x):
    return jax.nn.gelu(x, approximate=True)

def _silu(x):
    return jax.nn.silu(x)

def _sigmoid(x):
    return jax.nn.sigmoid(x)

def _layernorm(x, axis=-1, eps=1e-05):
    m = jnp.mean(x, axis=axis, keepdims=True)
    v = jnp.var(x, axis=axis, keepdims=True)
    return (x - m) / jnp.sqrt(v + eps)

def _scatter_add(tgt, idx, src, axis=0):
    return tgt.at[idx].add(src)

def _segment_sum(src, seg, n):
    return jax.ops.segment_sum(src, seg, n)
kernel_name = 'mk_prb_d4_jaxref_r8_b8c64a'

def setup_inputs(seed: int=0):
    np.random.seed(seed)
    _w = jnp.asarray

    def _L0_attn_setup():
        import jax, jax.numpy as jnp
        import numpy as np
        EPS_RMS = 1e-06
        EPS_LN = 1e-05
        ETA_MIN = 1e-06
        B, T, D, F = (8, 64, 128, 64)

        def _rmsnorm(x, w):
            return x * jax.lax.rsqrt(jnp.mean(x * x, axis=-1, keepdims=True) + EPS_RMS) * w

        def _phi(x):
            return jax.nn.elu(x) + 1.0

        def _ln2(M):
            mu = jnp.mean(M, axis=(-2, -1), keepdims=True)
            var = jnp.mean((M - mu) ** 2, axis=(-2, -1), keepdims=True)
            return (M - mu) * jax.lax.rsqrt(var + EPS_LN)

        def _reference_tuple_inner(x, norm_weight, Wk, Wv, Wq, eta, Wout):
            b, t, d = x.shape
            f = Wk.shape[0]
            x_norm = _rmsnorm(x, norm_weight)
            k = _phi(jnp.einsum('btd,fd->btf', x_norm, Wk))
            v = jnp.einsum('btd,ed->bte', x_norm, Wv)
            eta_c = jnp.maximum(jnp.abs(eta), ETA_MIN)

            def step(M, kv):
                k_t, v_t = kv
                v_pred = jnp.einsum('bf,bfd->bd', k_t, M)
                surprise = jnp.linalg.norm(v_t - v_pred, axis=-1, keepdims=True)
                delta = k_t[:, :, None] * v_t[:, None, :]
                M = M + eta_c[None, :, None] * surprise[:, :, None] * delta
                return (_ln2(M), None)
            M0 = jnp.zeros((b, f, d), dtype=x.dtype)
            kT = jnp.transpose(k, (1, 0, 2))
            vT = jnp.transpose(v, (1, 0, 2))
            M, _ = jax.lax.scan(step, M0, (kT, vT))
            q = _phi(jnp.einsum('btd,fd->btf', x_norm, Wq))
            mem_out = jnp.einsum('btf,bfd->btd', q, M)
            out = jnp.einsum('btd,ed->bte', mem_out, Wout)
            output = x + out
            return (output, M)
        key = jax.random.key(seed)
        ks = jax.random.split(key, 5)
        x = jax.random.normal(ks[0], (B, T, D), dtype=jnp.float32)
        norm_weight = jnp.ones((D,), dtype=jnp.float32)
        Wk = jax.random.normal(ks[1], (F, D), dtype=jnp.float32) * 0.02
        Wv = jax.random.normal(ks[2], (D, D), dtype=jnp.float32) * 0.02
        Wq = jax.random.normal(ks[3], (F, D), dtype=jnp.float32) * 0.02
        Wout = jax.random.normal(ks[4], (D, D), dtype=jnp.float32) * 0.02
        eta = jnp.ones((F,), dtype=jnp.float32) * 0.01
        return {'x': x, 'norm_weight': norm_weight, 'Wk': Wk, 'Wv': Wv, 'Wq': Wq, 'eta': eta, 'Wout': Wout}
    _L0_attn_in = _L0_attn_setup()

    def _L0_ffn_setup():
        import jax, jax.numpy as jnp
        import numpy as np
        EPS = 1e-05

        def _quantize(W):
            gamma = jnp.mean(jnp.abs(W))
            return jnp.clip(jnp.round(W / (gamma + EPS)), -1.0, 1.0)
        key = jax.random.key(seed)
        k_x, k_w1, k_b1, k_w2, k_b2 = jax.random.split(key, 5)
        n_embd = 128
        d_ff = 4 * n_embd
        B, S = (4, 512)
        bound1 = 1.0 / np.sqrt(n_embd)
        bound2 = 1.0 / np.sqrt(d_ff)
        x = jax.random.normal(k_x, (B, S, n_embd), dtype=jnp.float32)
        W1 = jax.random.uniform(k_w1, (d_ff, n_embd), jnp.float32, -bound1, bound1)
        b1 = jax.random.uniform(k_b1, (d_ff,), jnp.float32, -bound1, bound1)
        W2 = jax.random.uniform(k_w2, (n_embd, d_ff), jnp.float32, -bound2, bound2)
        b2 = jax.random.uniform(k_b2, (n_embd,), jnp.float32, -bound2, bound2)
        return {'x': x, 'W1': W1, 'b1': b1, 'W2': W2, 'b2': b2}
    _L0_ffn_in = _L0_ffn_setup()

    def _L1_attn_setup():
        import jax, jax.numpy as jnp
        import numpy as np
        import math
        D_MODEL = 128
        N_HEADS = 16
        EPS_GN = 1e-05

        def channel_group_norm(x, gamma, beta, num_groups, eps=EPS_GN):
            B, T, D = x.shape
            g = num_groups
            xt = x.transpose(0, 2, 1).reshape(B, g, D // g, T)
            mu = xt.mean(axis=(2, 3), keepdims=True)
            var = xt.var(axis=(2, 3), keepdims=True)
            xn = ((xt - mu) / jnp.sqrt(var + eps)).reshape(B, D, T)
            xn = xn * gamma[None, :, None] + beta[None, :, None]
            return xn.transpose(0, 2, 1)

        def l2_normalize(x, eps=1e-12):
            n = jnp.linalg.norm(x, axis=-1, keepdims=True)
            return x / jnp.maximum(n, eps)

        def decay_gammas(num_heads, dtype=jnp.float32):
            return 1.0 - jnp.exp(jnp.linspace(math.log(1.0 / 32.0), math.log(1.0 / 512.0), num_heads)).astype(dtype)
        key = jax.random.key(seed)
        ks = jax.random.split(key, 16)
        B, T, D = (4, 128, D_MODEL)
        s = 1.0 / math.sqrt(D)
        inp = {'x': jax.random.normal(ks[0], (B, T, D), jnp.float32), 'norm_g': jnp.ones((D,), jnp.float32), 'norm_b': jnp.zeros((D,), jnp.float32), 'qw': jax.random.normal(ks[1], (D, D), jnp.float32) * s, 'kw': jax.random.normal(ks[2], (D, D), jnp.float32) * s, 'vw': jax.random.normal(ks[3], (D, D), jnp.float32) * s, 'ow': jax.random.normal(ks[4], (D, D), jnp.float32) * s, 'ob': jnp.zeros((D,), jnp.float32), 'ffn_norm_g': jnp.ones((D,), jnp.float32), 'ffn_norm_b': jnp.zeros((D,), jnp.float32), 'w1': jax.random.normal(ks[5], (2 * D, D), jnp.float32) * s, 'b1': jnp.zeros((2 * D,), jnp.float32), 'w2': jax.random.normal(ks[6], (D, 2 * D), jnp.float32) * (1.0 / math.sqrt(2 * D)), 'b2': jnp.zeros((D,), jnp.float32)}
        return inp
    _L1_attn_in = _L1_attn_setup()

    def _L1_ffn_setup():
        import jax, jax.numpy as jnp
        import numpy as np
        D_MODEL = 128
        E = 4
        MIN_E = 1
        TH_LO = 0.5
        TH_HI = 2.0
        key = jax.random.key(seed)
        ks = jax.random.split(key, 12)
        B, N, D, H = (4, 256, D_MODEL, 2 * D_MODEL)
        s = 0.02
        return {'x': jax.random.normal(ks[0], (B, N, D), dtype=jnp.float32), 'gate_w': jax.random.normal(ks[1], (D, E), dtype=jnp.float32) * s, 'gate_b': jnp.zeros((E,), dtype=jnp.float32), 'dp_w1': jax.random.normal(ks[2], (D, D // 2), dtype=jnp.float32) * s, 'dp_b1': jnp.zeros((D // 2,), dtype=jnp.float32), 'dp_w2': jax.random.normal(ks[3], (D // 2, 1), dtype=jnp.float32) * s, 'dp_b2': jnp.zeros((1,), dtype=jnp.float32), 'ew1': jax.random.normal(ks[4], (E, D, H), dtype=jnp.float32) * s, 'eb1': jnp.zeros((E, H), dtype=jnp.float32), 'ew2': jax.random.normal(ks[5], (E, H, D), dtype=jnp.float32) * s, 'eb2': jnp.zeros((E, D), dtype=jnp.float32)}
    _L1_ffn_in = _L1_ffn_setup()

    def _L2_attn_setup():
        import jax, jax.numpy as jnp
        import numpy as np
        H = 128
        M = 128
        FF = 512
        WIN = 16
        SLOTS = 10
        B, S = (2, 512)
        EPS_LN = 1e-05
        EPS_NORM = 1e-12

        def _layernorm(x, g, b):
            m = jnp.mean(x, axis=-1, keepdims=True)
            v = jnp.var(x, axis=-1, keepdims=True)
            return (x - m) / jnp.sqrt(v + EPS_LN) * g + b
        key = jax.random.key(seed)
        ks = jax.random.split(key, 12)

        def lin_w(k, out_d, in_d):
            return jax.random.normal(k, (out_d, in_d), jnp.float32) / np.sqrt(in_d)
        return {'x': jax.random.normal(ks[0], (B, S, H), jnp.float32), 'mem_W': lin_w(ks[1], M, M), 'mem_b': jnp.zeros((M,), jnp.float32), 'P': jax.random.normal(ks[2], (SLOTS, M), jnp.float32), 'Wi': lin_w(ks[3], M, H), 'bi': jnp.zeros((M,), jnp.float32), 'Wl1': lin_w(ks[4], M, M), 'bl1': jnp.zeros((M,), jnp.float32), 'Wl2': lin_w(ks[5], M, M), 'bl2': jnp.zeros((M,), jnp.float32), 'Wo': lin_w(ks[6], H, M), 'bo': jnp.zeros((H,), jnp.float32), 'fgate': jnp.ones((1,), jnp.float32), 'lrate': jnp.ones((1,), jnp.float32), 'Wg': lin_w(ks[7], H, 2 * H), 'bg': jnp.zeros((H,), jnp.float32), 'W1': lin_w(ks[8], FF, H), 'b1': jnp.zeros((FF,), jnp.float32), 'W2': lin_w(ks[9], H, FF), 'b2': jnp.zeros((H,), jnp.float32), 'g1': jnp.ones((H,), jnp.float32), 'be1': jnp.zeros((H,), jnp.float32), 'g2': jnp.ones((H,), jnp.float32), 'be2': jnp.zeros((H,), jnp.float32), 'g3': jnp.ones((H,), jnp.float32), 'be3': jnp.zeros((H,), jnp.float32)}
    _L2_attn_in = _L2_attn_setup()

    def _L2_ffn_setup():
        import jax, jax.numpy as jnp
        import numpy as np
        NUM_EXPERTS = 8
        CAP_FACTOR = 1.0
        MIN_CAP = 8
        key = jax.random.key(seed)
        ks = jax.random.split(key, 10)
        G, S, D, H, E = (4, 512, 128, 512, NUM_EXPERTS)
        s = 0.02
        return {'x': jax.random.normal(ks[0], (G, S, D), dtype=jnp.float32), 'gate': jax.random.normal(ks[1], (D, E), dtype=jnp.float32) * s, 'W1': jax.random.normal(ks[2], (E, D, H), dtype=jnp.float32) * s, 'b1': jnp.zeros((E, H), dtype=jnp.float32), 'W2': jax.random.normal(ks[3], (E, H, D), dtype=jnp.float32) * s, 'b2': jnp.zeros((E, D), dtype=jnp.float32), 'Ws1': jax.random.normal(ks[4], (D, H), dtype=jnp.float32) * s, 'bs1': jnp.zeros((H,), dtype=jnp.float32), 'Ws2': jax.random.normal(ks[5], (H, D), dtype=jnp.float32) * s, 'bs2': jnp.zeros((D,), dtype=jnp.float32)}
    _L2_ffn_in = _L2_ffn_setup()

    def _L3_attn_setup():
        import jax, jax.numpy as jnp
        import numpy as np
        NUM_HEADS = 16
        SPARSITY_THRESHOLD = 0.1
        key = jax.random.key(seed)
        k1, k2, k3 = jax.random.split(key, 3)
        B, S, D = (2, 256, 128)
        x = jax.random.normal(k1, (B, S, D), dtype=jnp.float32)
        w_qkv = jax.random.normal(k2, (3 * D, D), dtype=jnp.float32) * (1.0 / np.sqrt(D))
        b_qkv = jnp.zeros((3 * D,), dtype=jnp.float32)
        w_out = jax.random.normal(k3, (D, D), dtype=jnp.float32) * (1.0 / np.sqrt(D))
        b_out = jnp.zeros((D,), dtype=jnp.float32)
        return {'x': x, 'w_qkv': w_qkv, 'b_qkv': b_qkv, 'w_out': w_out, 'b_out': b_out}
    _L3_attn_in = _L3_attn_setup()

    def _L3_ffn_setup():
        import jax, jax.numpy as jnp
        import numpy as np
        E, D_MODEL, D_FF = (8, 128, 512)
        B, S = (4, 256)
        key = jax.random.key(seed)
        ks = jax.random.split(key, 7)
        scale_in = 1.0 / np.sqrt(D_MODEL)
        scale_ff = 1.0 / np.sqrt(D_FF)
        return {'x': jax.random.normal(ks[0], (B, S, D_MODEL), dtype=jnp.float32), 'w1': jax.random.normal(ks[1], (E, D_MODEL, D_FF), dtype=jnp.float32) * scale_in, 'b1': jax.random.normal(ks[2], (E, D_FF), dtype=jnp.float32) * 0.01, 'w2': jax.random.normal(ks[3], (E, D_FF, D_MODEL), dtype=jnp.float32) * scale_ff, 'b2': jax.random.normal(ks[4], (E, D_MODEL), dtype=jnp.float32) * 0.01, 'gate_w': jax.random.normal(ks[5], (D_MODEL, E), dtype=jnp.float32) * scale_in, 'gate_b': jax.random.normal(ks[6], (E,), dtype=jnp.float32) * 0.01}
    _L3_ffn_in = _L3_ffn_setup()
    _d = {'L0_attn_x': _L0_attn_in['x'], 'L0_attn_norm_weight': _L0_attn_in['norm_weight'], 'L0_attn_Wk': _L0_attn_in['Wk'], 'L0_attn_Wv': _L0_attn_in['Wv'], 'L0_attn_Wq': _L0_attn_in['Wq'], 'L0_attn_eta': _L0_attn_in['eta'], 'L0_attn_Wout': _L0_attn_in['Wout'], 'L0_ffn_W1': _L0_ffn_in['W1'], 'L0_ffn_b1': _L0_ffn_in['b1'], 'L0_ffn_W2': _L0_ffn_in['W2'], 'L0_ffn_b2': _L0_ffn_in['b2'], 'L1_attn_norm_g': _L1_attn_in['norm_g'], 'L1_attn_norm_b': _L1_attn_in['norm_b'], 'L1_attn_qw': _L1_attn_in['qw'], 'L1_attn_kw': _L1_attn_in['kw'], 'L1_attn_vw': _L1_attn_in['vw'], 'L1_attn_ow': _L1_attn_in['ow'], 'L1_attn_ob': _L1_attn_in['ob'], 'L1_attn_ffn_norm_g': _L1_attn_in['ffn_norm_g'], 'L1_attn_ffn_norm_b': _L1_attn_in['ffn_norm_b'], 'L1_attn_w1': _L1_attn_in['w1'], 'L1_attn_b1': _L1_attn_in['b1'], 'L1_attn_w2': _L1_attn_in['w2'], 'L1_attn_b2': _L1_attn_in['b2'], 'L1_ffn_gate_w': _L1_ffn_in['gate_w'], 'L1_ffn_gate_b': _L1_ffn_in['gate_b'], 'L1_ffn_dp_w1': _L1_ffn_in['dp_w1'], 'L1_ffn_dp_b1': _L1_ffn_in['dp_b1'], 'L1_ffn_dp_w2': _L1_ffn_in['dp_w2'], 'L1_ffn_dp_b2': _L1_ffn_in['dp_b2'], 'L1_ffn_ew1': _L1_ffn_in['ew1'], 'L1_ffn_eb1': _L1_ffn_in['eb1'], 'L1_ffn_ew2': _L1_ffn_in['ew2'], 'L1_ffn_eb2': _L1_ffn_in['eb2'], 'L2_attn_mem_W': _L2_attn_in['mem_W'], 'L2_attn_mem_b': _L2_attn_in['mem_b'], 'L2_attn_P': _L2_attn_in['P'], 'L2_attn_Wi': _L2_attn_in['Wi'], 'L2_attn_bi': _L2_attn_in['bi'], 'L2_attn_Wl1': _L2_attn_in['Wl1'], 'L2_attn_bl1': _L2_attn_in['bl1'], 'L2_attn_Wl2': _L2_attn_in['Wl2'], 'L2_attn_bl2': _L2_attn_in['bl2'], 'L2_attn_Wo': _L2_attn_in['Wo'], 'L2_attn_bo': _L2_attn_in['bo'], 'L2_attn_fgate': _L2_attn_in['fgate'], 'L2_attn_lrate': _L2_attn_in['lrate'], 'L2_attn_Wg': _L2_attn_in['Wg'], 'L2_attn_bg': _L2_attn_in['bg'], 'L2_attn_W1': _L2_attn_in['W1'], 'L2_attn_b1': _L2_attn_in['b1'], 'L2_attn_W2': _L2_attn_in['W2'], 'L2_attn_b2': _L2_attn_in['b2'], 'L2_attn_g1': _L2_attn_in['g1'], 'L2_attn_be1': _L2_attn_in['be1'], 'L2_attn_g2': _L2_attn_in['g2'], 'L2_attn_be2': _L2_attn_in['be2'], 'L2_attn_g3': _L2_attn_in['g3'], 'L2_attn_be3': _L2_attn_in['be3'], 'L2_ffn_gate': _L2_ffn_in['gate'], 'L2_ffn_W1': _L2_ffn_in['W1'], 'L2_ffn_b1': _L2_ffn_in['b1'], 'L2_ffn_W2': _L2_ffn_in['W2'], 'L2_ffn_b2': _L2_ffn_in['b2'], 'L2_ffn_Ws1': _L2_ffn_in['Ws1'], 'L2_ffn_bs1': _L2_ffn_in['bs1'], 'L2_ffn_Ws2': _L2_ffn_in['Ws2'], 'L2_ffn_bs2': _L2_ffn_in['bs2'], 'L3_attn_w_qkv': _L3_attn_in['w_qkv'], 'L3_attn_b_qkv': _L3_attn_in['b_qkv'], 'L3_attn_w_out': _L3_attn_in['w_out'], 'L3_attn_b_out': _L3_attn_in['b_out'], 'L3_ffn_w1': _L3_ffn_in['w1'], 'L3_ffn_b1': _L3_ffn_in['b1'], 'L3_ffn_w2': _L3_ffn_in['w2'], 'L3_ffn_b2': _L3_ffn_in['b2'], 'L3_ffn_gate_w': _L3_ffn_in['gate_w'], 'L3_ffn_gate_b': _L3_ffn_in['gate_b']}
    _x0 = _d['L0_attn_x']
    _d['L0_attn_x'] = jax.random.normal(jax.random.fold_in(jax.random.key(seed), 1), (16, 256, 128), dtype=_x0.dtype)
    del _x0
    return _d

def reference(L0_attn_x, L0_attn_norm_weight, L0_attn_Wk, L0_attn_Wv, L0_attn_Wq, L0_attn_eta, L0_attn_Wout, L0_ffn_W1, L0_ffn_b1, L0_ffn_W2, L0_ffn_b2, L1_attn_norm_g, L1_attn_norm_b, L1_attn_qw, L1_attn_kw, L1_attn_vw, L1_attn_ow, L1_attn_ob, L1_attn_ffn_norm_g, L1_attn_ffn_norm_b, L1_attn_w1, L1_attn_b1, L1_attn_w2, L1_attn_b2, L1_ffn_gate_w, L1_ffn_gate_b, L1_ffn_dp_w1, L1_ffn_dp_b1, L1_ffn_dp_w2, L1_ffn_dp_b2, L1_ffn_ew1, L1_ffn_eb1, L1_ffn_ew2, L1_ffn_eb2, L2_attn_mem_W, L2_attn_mem_b, L2_attn_P, L2_attn_Wi, L2_attn_bi, L2_attn_Wl1, L2_attn_bl1, L2_attn_Wl2, L2_attn_bl2, L2_attn_Wo, L2_attn_bo, L2_attn_fgate, L2_attn_lrate, L2_attn_Wg, L2_attn_bg, L2_attn_W1, L2_attn_b1, L2_attn_W2, L2_attn_b2, L2_attn_g1, L2_attn_be1, L2_attn_g2, L2_attn_be2, L2_attn_g3, L2_attn_be3, L2_ffn_gate, L2_ffn_W1, L2_ffn_b1, L2_ffn_W2, L2_ffn_b2, L2_ffn_Ws1, L2_ffn_bs1, L2_ffn_Ws2, L2_ffn_bs2, L3_attn_w_qkv, L3_attn_b_qkv, L3_attn_w_out, L3_attn_b_out, L3_ffn_w1, L3_ffn_b1, L3_ffn_w2, L3_ffn_b2, L3_ffn_gate_w, L3_ffn_gate_b):

    def _L0_attn_ref(x, norm_weight, Wk, Wv, Wq, eta, Wout):
        import jax, jax.numpy as jnp
        import numpy as np
        EPS_RMS = 1e-06
        EPS_LN = 1e-05
        ETA_MIN = 1e-06
        B, T, D, F = (8, 64, 128, 64)

        def _rmsnorm(x, w):
            return x * jax.lax.rsqrt(jnp.mean(x * x, axis=-1, keepdims=True) + EPS_RMS) * w

        def _phi(x):
            return jax.nn.elu(x) + 1.0

        def _ln2(M):
            mu = jnp.mean(M, axis=(-2, -1), keepdims=True)
            var = jnp.mean((M - mu) ** 2, axis=(-2, -1), keepdims=True)
            return (M - mu) * jax.lax.rsqrt(var + EPS_LN)

        def _reference_tuple_inner(x, norm_weight, Wk, Wv, Wq, eta, Wout):
            b, t, d = x.shape
            f = Wk.shape[0]
            x_norm = _rmsnorm(x, norm_weight)
            k = _phi(jnp.einsum('btd,fd->btf', x_norm, Wk))
            v = jnp.einsum('btd,ed->bte', x_norm, Wv)
            eta_c = jnp.maximum(jnp.abs(eta), ETA_MIN)

            def step(M, kv):
                k_t, v_t = kv
                v_pred = jnp.einsum('bf,bfd->bd', k_t, M)
                surprise = jnp.linalg.norm(v_t - v_pred, axis=-1, keepdims=True)
                delta = k_t[:, :, None] * v_t[:, None, :]
                M = M + eta_c[None, :, None] * surprise[:, :, None] * delta
                return (_ln2(M), None)
            M0 = jnp.zeros((b, f, d), dtype=x.dtype)
            kT = jnp.transpose(k, (1, 0, 2))
            vT = jnp.transpose(v, (1, 0, 2))
            M, _ = jax.lax.scan(step, M0, (kT, vT))
            q = _phi(jnp.einsum('btd,fd->btf', x_norm, Wq))
            mem_out = jnp.einsum('btf,bfd->btd', q, M)
            out = jnp.einsum('btd,ed->bte', mem_out, Wout)
            output = x + out
            return (output, M)
        return _reference_tuple_inner(x, norm_weight, Wk, Wv, Wq, eta, Wout)[0]

    def _L0_ffn_ref(x, W1, b1, W2, b2):
        import jax, jax.numpy as jnp
        import numpy as np
        EPS = 1e-05

        def _quantize(W):
            gamma = jnp.mean(jnp.abs(W))
            return jnp.clip(jnp.round(W / (gamma + EPS)), -1.0, 1.0)
        Wq1 = _quantize(W1)
        Wq2 = _quantize(W2)
        h = jax.nn.relu(jnp.einsum('bsd,fd->bsf', x, Wq1) + b1)
        out = jnp.einsum('bsf,df->bsd', h, Wq2) + b2
        return out

    def _L1_attn_ref(x, norm_g, norm_b, qw, kw, vw, ow, ob, ffn_norm_g, ffn_norm_b, w1, b1, w2, b2):
        import jax, jax.numpy as jnp
        import numpy as np
        import math
        D_MODEL = 128
        N_HEADS = 16
        EPS_GN = 1e-05

        def channel_group_norm(x, gamma, beta, num_groups, eps=EPS_GN):
            B, T, D = x.shape
            g = num_groups
            xt = x.transpose(0, 2, 1).reshape(B, g, D // g, T)
            mu = xt.mean(axis=(2, 3), keepdims=True)
            var = xt.var(axis=(2, 3), keepdims=True)
            xn = ((xt - mu) / jnp.sqrt(var + eps)).reshape(B, D, T)
            xn = xn * gamma[None, :, None] + beta[None, :, None]
            return xn.transpose(0, 2, 1)

        def l2_normalize(x, eps=1e-12):
            n = jnp.linalg.norm(x, axis=-1, keepdims=True)
            return x / jnp.maximum(n, eps)

        def decay_gammas(num_heads, dtype=jnp.float32):
            return 1.0 - jnp.exp(jnp.linspace(math.log(1.0 / 32.0), math.log(1.0 / 512.0), num_heads)).astype(dtype)
        B, T, D = x.shape
        H = N_HEADS
        dh = D // H
        residual = x
        xn = channel_group_norm(x, norm_g, norm_b, H)
        q = l2_normalize(xn @ qw.T)
        k = l2_normalize(xn @ kw.T)
        v = xn @ vw.T

        def heads(t):
            return t.reshape(B, T, H, dh).transpose(0, 2, 1, 3)
        qh, kh, vh = (heads(q), heads(k), heads(v))
        gammas = decay_gammas(H)
        n = jnp.arange(T)[:, None]
        m = jnp.arange(T)[None, :]
        diff = n - m
        causal = diff >= 0
        exponent = jnp.where(causal, diff, 0).astype(jnp.float32)
        dmask = jnp.where(causal[None], gammas[:, None, None] ** exponent[None], 0.0)
        scale = 1.0 / math.sqrt(dh)
        sim = jnp.einsum('bhnd,bhmd->bhnm', qh, kh) * scale
        sim = sim * dmask[None]
        yh = jnp.einsum('bhnm,bhmd->bhnd', sim, vh)
        y = yh.transpose(0, 2, 1, 3).reshape(B, T, D)
        y = y @ ow.T + ob
        x = residual + y
        residual = x
        xn = channel_group_norm(x, ffn_norm_g, ffn_norm_b, H)
        h = jax.nn.silu(xn @ w1.T + b1)
        x = residual + (h @ w2.T + b2)
        return x

    def _L1_ffn_ref(x, gate_w, gate_b, dp_w1, dp_b1, dp_w2, dp_b2, ew1, eb1, ew2, eb2):
        import jax, jax.numpy as jnp
        import numpy as np
        D_MODEL = 128
        E = 4
        MIN_E = 1
        TH_LO = 0.5
        TH_HI = 2.0
        B, N, D = x.shape
        xf = x.reshape(B * N, D)
        T = B * N
        h = jax.nn.relu(xf @ dp_w1 + dp_b1)
        entropy = jax.nn.softplus(h @ dp_w2 + dp_b2)[:, 0]
        norm = jnp.clip((entropy - TH_LO) / (TH_HI - TH_LO), 0.0, 1.0)
        k_tok = jnp.clip(jnp.round(MIN_E + norm * (E - MIN_E)).astype(jnp.int32), MIN_E, E)
        logits = xf @ gate_w + gate_b
        top_logits, top_idx = jax.lax.top_k(logits, E)
        pos = jnp.arange(E)
        sel = pos[None, :] < k_tok[:, None]
        masked = jnp.where(sel, top_logits, -jnp.inf)
        w_top = jax.nn.softmax(masked, axis=-1)
        dense_w = jnp.zeros((T, E), dtype=xf.dtype).at[jnp.arange(T)[:, None], top_idx].set(w_top)
        hid = jax.nn.relu(jnp.einsum('td,edh->teh', xf, ew1) + eb1[None, :, :])
        y = jnp.einsum('teh,ehd->ted', hid, ew2) + eb2[None, :, :]
        out = jnp.einsum('te,ted->td', dense_w, y)
        return out.reshape(B, N, D)

    def _L2_attn_ref(x, mem_W, mem_b, P, Wi, bi, Wl1, bl1, Wl2, bl2, Wo, bo, fgate, lrate, Wg, bg, W1, b1, W2, b2, g1, be1, g2, be2, g3, be3):
        import jax, jax.numpy as jnp
        import numpy as np
        H = 128
        M = 128
        FF = 512
        WIN = 16
        SLOTS = 10
        B, S = (2, 512)
        EPS_LN = 1e-05
        EPS_NORM = 1e-12

        def _layernorm(x, g, b):
            m = jnp.mean(x, axis=-1, keepdims=True)
            v = jnp.var(x, axis=-1, keepdims=True)
            return (x - m) / jnp.sqrt(v + EPS_LN) * g + b
        b, s, h = x.shape
        k_full = jnp.concatenate([x, jnp.broadcast_to(P, (b,) + P.shape)], axis=1)
        idx = jnp.arange(s)[:, None] + jnp.arange(-WIN, 1)[None, :]
        valid = idx >= 0
        k_win = k_full[:, jnp.maximum(idx, 0)]
        scores = jnp.einsum('bsh,bswh->bsw', x, k_win) * h ** (-0.5)
        scores = jnp.where(valid[None], scores, -jnp.inf)
        attn_out = jnp.einsum('bsw,bswh->bsh', jax.nn.softmax(scores, axis=-1), k_win)
        x1 = _layernorm(x + attn_out, g1, be1)
        kv = k_full.reshape(-1, h)
        kn = kv / jnp.maximum(jnp.linalg.norm(kv, axis=-1, keepdims=True), EPS_NORM)
        kp = kn @ Wi.T + bi
        vp = kp
        hdd = jax.nn.silu(kp @ Wl1.T + bl1)
        hdd = jax.nn.silu(hdd @ Wl2.T + bl2)
        pred = hdd @ mem_W.T + mem_b
        diff = pred - vp
        n, m = diff.shape
        grad_W = 2.0 / (n * m) * diff.T @ hdd
        W_new = (1.0 - fgate) * mem_W + lrate * grad_W
        mem_out = hdd @ W_new.T + mem_b
        mo = (mem_out @ Wo.T + bo).reshape(b, -1, h)[:, :s]
        gate = jax.nn.sigmoid(jnp.concatenate([x1, mo], axis=-1) @ Wg.T + bg)
        combined = gate * x1 + (1.0 - gate) * mo
        x2 = _layernorm(x1 + combined, g2, be2)
        ff = jax.nn.silu(x2 @ W1.T + b1) @ W2.T + b2
        return _layernorm(x2 + ff, g3, be3)

    def _L2_ffn_ref(x, gate, W1, b1, W2, b2, Ws1, bs1, Ws2, bs2):
        import jax, jax.numpy as jnp
        import numpy as np
        NUM_EXPERTS = 8
        CAP_FACTOR = 1.0
        MIN_CAP = 8
        G, S, D = x.shape
        E = gate.shape[1]
        T = G * S
        capacity = max(MIN_CAP, int(CAP_FACTOR * T / E))
        logits = jnp.einsum('gsd,de->gse', x, gate)
        probs = jax.nn.softmax(logits, axis=-1)
        flat_probs = probs.transpose(2, 0, 1).reshape(E, T)
        scores, token_idx = jax.lax.top_k(flat_probs, k=capacity)
        scores = jnp.where(scores > -100000000.0, scores, 0.0)
        flat_x = x.reshape(T, D)
        tok = flat_x[token_idx]
        h = jax.nn.gelu(jnp.einsum('ecd,edh->ech', tok, W1) + b1[:, None, :])
        out_tok = jnp.einsum('ech,ehd->ecd', h, W2) + b2[:, None, :]
        scaled = out_tok * scores[..., None]
        routed = jnp.zeros_like(flat_x).at[token_idx.reshape(-1)].add(scaled.reshape(E * capacity, D)).reshape(G, S, D)
        shared = jax.nn.gelu(jnp.einsum('gsd,dh->gsh', x, Ws1) + bs1)
        shared = jnp.einsum('gsh,hd->gsd', shared, Ws2) + bs2
        return routed + shared

    def _L3_attn_ref(x, w_qkv, b_qkv, w_out, b_out):
        import jax, jax.numpy as jnp
        import numpy as np
        NUM_HEADS = 16
        SPARSITY_THRESHOLD = 0.1
        B, S, D = x.shape
        H = NUM_HEADS
        hd = D // H
        qkv = (x @ w_qkv.T + b_qkv).reshape(B, S, 3, H, hd)
        q, k, v = (qkv[:, :, 0], qkv[:, :, 1], qkv[:, :, 2])
        energy = jnp.linalg.norm(q, axis=-1)
        mask = (energy > energy.mean() * SPARSITY_THRESHOLD).astype(x.dtype)
        scores = jnp.einsum('bihd,bjhd->bijh', q, k) / jnp.sqrt(jnp.float32(hd))
        scores = scores * mask[:, :, None, :]
        probs = jax.nn.softmax(scores, axis=2)
        context = jnp.einsum('bijh,bjhd->bihd', probs, v).reshape(B, S, D)
        return context @ w_out.T + b_out

    def _L3_ffn_ref(x, w1, b1, w2, b2, gate_w, gate_b):
        import jax, jax.numpy as jnp
        import numpy as np
        E, D_MODEL, D_FF = (8, 128, 512)
        B, S = (4, 256)
        gate_logits = x @ gate_w + gate_b
        gate_probs = jax.nn.softmax(gate_logits, axis=-1)
        top1 = jnp.argmax(gate_probs, axis=-1)
        mask = jax.nn.one_hot(top1, E, dtype=x.dtype)
        h = jax.nn.relu(jnp.einsum('bsd,edf->ebsf', x, w1) + b1[:, None, None, :])
        y = jnp.einsum('ebsf,efd->ebsd', h, w2) + b2[:, None, None, :]
        out = jnp.einsum('ebsd,bse->bsd', y, mask)
        return out
    x = L0_attn_x
    xn = _layernorm(x, axis=-1)
    x = x + _L0_attn_ref(xn, L0_attn_norm_weight, L0_attn_Wk, L0_attn_Wv, L0_attn_Wq, L0_attn_eta, L0_attn_Wout) + _L0_ffn_ref(xn, L0_ffn_W1, L0_ffn_b1, L0_ffn_W2, L0_ffn_b2)
    xn = _layernorm(x, axis=-1)
    x = x + _L1_attn_ref(xn, L1_attn_norm_g, L1_attn_norm_b, L1_attn_qw, L1_attn_kw, L1_attn_vw, L1_attn_ow, L1_attn_ob, L1_attn_ffn_norm_g, L1_attn_ffn_norm_b, L1_attn_w1, L1_attn_b1, L1_attn_w2, L1_attn_b2) + _L1_ffn_ref(xn, L1_ffn_gate_w, L1_ffn_gate_b, L1_ffn_dp_w1, L1_ffn_dp_b1, L1_ffn_dp_w2, L1_ffn_dp_b2, L1_ffn_ew1, L1_ffn_eb1, L1_ffn_ew2, L1_ffn_eb2)
    xn = _layernorm(x, axis=-1)
    x = x + _L2_attn_ref(xn, L2_attn_mem_W, L2_attn_mem_b, L2_attn_P, L2_attn_Wi, L2_attn_bi, L2_attn_Wl1, L2_attn_bl1, L2_attn_Wl2, L2_attn_bl2, L2_attn_Wo, L2_attn_bo, L2_attn_fgate, L2_attn_lrate, L2_attn_Wg, L2_attn_bg, L2_attn_W1, L2_attn_b1, L2_attn_W2, L2_attn_b2, L2_attn_g1, L2_attn_be1, L2_attn_g2, L2_attn_be2, L2_attn_g3, L2_attn_be3) + _L2_ffn_ref(xn, L2_ffn_gate, L2_ffn_W1, L2_ffn_b1, L2_ffn_W2, L2_ffn_b2, L2_ffn_Ws1, L2_ffn_bs1, L2_ffn_Ws2, L2_ffn_bs2)
    xn = _layernorm(x, axis=-1)
    x = x + _L3_attn_ref(xn, L3_attn_w_qkv, L3_attn_b_qkv, L3_attn_w_out, L3_attn_b_out) + _L3_ffn_ref(xn, L3_ffn_w1, L3_ffn_b1, L3_ffn_w2, L3_ffn_b2, L3_ffn_gate_w, L3_ffn_gate_b)
    return x

_drawn_inputs = setup_inputs


def setup_inputs(seed=0):
    import zlib

    import numpy as np

    out = dict(_drawn_inputs(seed))
    spreads = {'L0_attn_norm_weight': (1.0, 0.6),
     'L0_attn_eta': (0.009999999776482582, 0.6),
     'L1_attn_norm_g': (1.0, 0.6),
     'L1_attn_norm_b': (0.0, 0.8),
     'L1_attn_ob': (0.0, 0.8),
     'L1_attn_ffn_norm_g': (1.0, 0.6),
     'L1_attn_ffn_norm_b': (0.0, 0.8),
     'L1_attn_b1': (0.0, 0.8),
     'L1_attn_b2': (0.0, 2.0),
     'L1_ffn_gate_b': (0.0, 0.8),
     'L1_ffn_dp_b1': (0.0, 0.1),
     'L1_ffn_eb1': (0.0, 0.8),
     'L1_ffn_eb2': (0.0, 2.0),
     'L2_attn_mem_b': (0.0, 2.0),
     'L2_attn_bi': (0.0, 2.0),
     'L2_attn_bl1': (0.0, 2.0),
     'L2_attn_bl2': (0.0, 2.0),
     'L2_attn_bo': (0.0, 2.0),
     'L2_attn_bg': (0.0, 0.8),
     'L2_attn_b1': (0.0, 2.0),
     'L2_attn_b2': (0.0, 2.0),
     'L2_attn_g1': (1.0, 0.6),
     'L2_attn_be1': (0.0, 2.0),
     'L2_attn_g2': (1.0, 0.6),
     'L2_attn_be2': (0.0, 2.0),
     'L2_attn_g3': (1.0, 0.6),
     'L2_attn_be3': (0.0, 2.0),
     'L2_ffn_b1': (0.0, 2.0),
     'L2_ffn_b2': (0.0, 2.0),
     'L2_ffn_bs1': (0.0, 0.8),
     'L2_ffn_bs2': (0.0, 2.0),
     'L3_attn_b_qkv': (0.0, 0.8),
     'L3_attn_b_out': (0.0, 2.0)}
    factors = {'L0_attn_Wk': 8.0,
     'L0_attn_Wq': 8.0,
     'L0_ffn_b1': 8.0,
     'L0_ffn_b2': 45.135,
     'L1_attn_qw': 8.0,
     'L1_attn_kw': 8.0,
     'L1_attn_vw': 8.0,
     'L1_attn_ow': 8.0,
     'L1_attn_w1': 8.0,
     'L1_attn_w2': 8.0,
     'L1_ffn_gate_w': 8.0,
     'L1_ffn_ew1': 8.0,
     'L1_ffn_ew2': 8.0,
     'L2_attn_mem_W': 8.0,
     'L2_attn_P': 200.0,
     'L2_attn_Wi': 139.144,
     'L2_attn_Wl1': 22.828,
     'L2_attn_Wl2': 22.926,
     'L2_attn_Wo': 8.0,
     'L2_attn_Wg': 8.0,
     'L2_attn_W1': 8.0,
     'L2_attn_W2': 8.0,
     'L2_ffn_gate': 8.0,
     'L2_ffn_W1': 8.0,
     'L2_ffn_W2': 8.0,
     'L2_ffn_Ws1': 8.0,
     'L2_ffn_Ws2': 8.0,
     'L3_attn_w_qkv': 8.0,
     'L3_attn_w_out': 8.0,
     'L3_ffn_w1': 8.0,
     'L3_ffn_b1': 181.763,
     'L3_ffn_w2': 8.0,
     'L3_ffn_b2': 200.0,
     'L3_ffn_gate_w': 8.0,
     'L3_ffn_gate_b': 8.0}
    for name, (base, spread) in spreads.items():
        noise = np.random.default_rng([zlib.crc32(name.encode()), seed]).standard_normal(out[name].shape)
        drawn = base * np.exp(spread * noise) if base else spread * noise
        out[name] = jnp.asarray(drawn.astype(out[name].dtype))
    for name, factor in factors.items():
        out[name] = (out[name] * factor).astype(out[name].dtype)
    return out
```

```python
from contextlib import ExitStack

import numpy as np
import concourse.bass as bass
from concourse import mybir

ALU = mybir.AluOpType
ACT = mybir.ActivationFunctionType
F32 = mybir.dt.float32
I32 = mybir.dt.int32
AX = mybir.AxisListType.X

T = 4096
NB, S = 16, 256
TW = 512
NT = T // TW
C = 8
NC = S // C

EARLY = [
    ("wk", 128), ("wq", 128), ("wv", 128), ("wout", 128), ("f1", 512), ("f2", 512),
    ("q1", 128), ("k1", 128), ("v1", 128), ("o1", 128), ("w11", 256), ("w12", 256),
    ("gw1", 4), ("dw1", 64), ("dw2", 1),
]
WEIGHTS = [
    ("wi", 128), ("wl1", 128), ("wl2", 128), ("memT", 128), ("wo2", 128), ("wg", 256),
    ("w21", 512), ("w22", 512), ("gw2", 8), ("ws1", 512), ("ws2", 512), ("pT", 10),
    ("qkv", 384), ("w3o", 128), ("gw3", 8),
]
BIASES = [
    ("nw", 1), ("eta", 1), ("f1b", 4), ("f2b", 1),
    ("g1", 1), ("b1n", 1), ("ob1", 1), ("fg1", 1), ("fb1", 1), ("b11", 2), ("b12", 1),
    ("gb1", 4), ("db1", 1), ("db2", 1), ("eb1", 8), ("eb2", 4),
    ("memb", 1), ("bi", 1), ("bl1", 1), ("bl2", 1), ("bo2", 1), ("fgate", 1), ("lrate", 1), ("bg", 1),
    ("b21", 4), ("b22", 1), ("g21", 1), ("be21", 1), ("g22", 1), ("be22", 1), ("g23", 1), ("be23", 1),
    ("m2b1", 32), ("m2b2", 8), ("bs1", 4), ("bs2", 1),
    ("bqkv", 3), ("bo3", 1), ("m3b1", 32), ("m3b2", 8), ("gb3", 8), ("bv3", 128),
]
CONSTS = [
    ("ident", 128), ("one", 128), ("mean", 128), ("blk", 128), ("hid", 16),
    ("oneh", 8), ("g8", 128), ("s8", 128), ("tri", 128), ("bd8", 128),
    ("rm", 4), ("lt", 128), ("band", 160), ("band0", 128), ("eps5", 1), ("eps6", 1), ("zero", 1),
    ("rselA", 128), ("pairm", 8), ("pairm2", 8), ("desc", 8), ("pm", 1), ("colr", 512),
]
ECONSTS = [("sel", 1024), ("dq", 256), ("dk", 256)]


def offsets(table):
    at, n = {}, 0
    for name, w in table:
        at[name] = (n, w)
        n += w
    return at, n


WAT, NW = offsets(WEIGHTS)
EAT, NE = offsets(EARLY + ECONSTS)
BAT, NBI = offsets(BIASES)
CAT, NCO = offsets(CONSTS)


def constants():
    p = np.arange(128)
    c = {}
    c["ident"] = np.eye(128)
    c["one"] = np.ones((128, 128))
    c["mean"] = np.full((128, 128), 1.0 / 128)
    c["blk"] = (p[:, None] // C == p[None, :] // C)
    c["sel"] = np.concatenate([(p[:, None] == (p[None, :] // C) * C + s) for s in range(C)], 1)
    c["hid"] = (p[:, None] // C == np.arange(16)[None, :])
    c["oneh"] = (p[:, None] % C == np.arange(C)[None, :])
    c["g8"] = (p[:, None] // 8 == p[None, :] // 8) / 8.0
    c["s8"] = (p[:, None] // 8 == p[None, :] // 8)
    gam = 1.0 - np.exp(np.linspace(np.log(1 / 32.0), np.log(1 / 512.0), 16)).astype(np.float32).astype(np.float64)
    g = gam[p // 8][:, None]
    t = np.arange(256)[None, :]
    c["dq"] = g ** (t - 128.0)
    c["dk"] = g ** (128.0 - t) / np.sqrt(8.0)
    c["tri"] = (p[None, :] >= p[:, None])
    c["bd8"] = (p[:, None] // 8 == p[None, :] // 8)
    c["rm"] = ((p[:, None] % 32) // 8 == np.arange(4)[None, :])
    c["lt"] = (p[:, None] < p[None, :])
    q, k = p[:, None], np.arange(160)[None, :] - 32
    c["band"] = np.where((k <= q) & (k >= q - 16), 0.0, -1e30)
    k = np.arange(128)[None, :]
    c["band0"] = np.where((k <= q) & (k >= q - 16), 0.0, -1e30)
    c["eps5"] = np.full((128, 1), 1e-5)
    c["eps6"] = np.full((128, 1), 1e-6)
    c["zero"] = np.zeros((128, 1))
    c["rselA"] = ((p[:, None] // C) % 2 == p[None, :] // 64) & (p[:, None] % C == 0)
    c["pairm"] = (p[:, None] // 16 == np.arange(8)[None, :])
    c["pairm2"] = np.zeros((128, 8))
    c["desc"] = np.tile(8.0 - np.arange(8), (128, 1))
    c["pm"] = np.zeros((128, 1))
    c["colr"] = np.tile(np.concatenate([(p // 8) % 4 == r for r in range(4)])[None, :], (128, 1))
    c["colr"] = np.tile(c["colr"], 1)
    return {n: np.asarray(a, np.float32) for n, a in c.items()}


class Eng:

    def __init__(self, sem):
        self.sem, self.n, self.items = sem, 0, []

    def __call__(self, fn, *waits):
        self.items.append((fn, flat(waits), True))
        self.n += 1
        return (self.sem, self.n)

    def chain(self, fn, *waits):
        return self(fn, (self.sem, self.n), *waits)

    def last(self):
        return (self.sem, self.n)

    def dma(self, fn, tok, *waits):
        self.items.append((lambda e: fn(e).then_inc(tok[0], 16), flat(waits), False))

    def play(self, eng):
        seen = {}
        for fn, waits, counted in self.items:
            for sem, v in waits:
                if v > seen.get(id(sem), 0):
                    eng.wait_ge(sem, v)
                    seen[id(sem)] = v
            r = fn(eng)
            if counted:
                r.then_inc(self.sem, 1)


def flat(waits):
    out = []
    for w in waits:
        if isinstance(w, list):
            out += flat(w)
        elif w is not None:
            out.append(w)
    return out


class Ring:

    def __init__(self, ids):
        self.idle = [(k, []) for k in ids]
        self.n = len(self.idle)

    def get(self):
        return self.idle.pop(0)

    def free(self, k, *toks):
        self.idle.append((k, list(toks)))

    def reset(self):
        assert len(self.idle) == self.n
        self.idle = [(k, []) for k, _ in sorted(self.idle)]


def pipe(gens, depth):
    gens = iter(gens)
    live = []
    while True:
        if len(live) < depth:
            g = next(gens, None)
            if g is not None:
                live.append(g)
        if not live:
            return
        for g in list(live):
            if next(g, 1) is not None:
                live.remove(g)


def program(nc, xT, early, wts, bia, con, m1, m2, m3, outT):
    with ExitStack() as ctx:
        def sb(name, shape, dt=F32):
            return ctx.enter_context(nc.sbuf_tensor(name, shape, dt))

        def sem(name):
            return ctx.enter_context(nc.semaphore(name))

        A, V, G, P, SP = (Eng(sem("s_" + n)) for n in ("act", "dve", "pool", "pe", "sp"))
        BIG = [sb(f"big{i}", [128, T]) for i in range(8)]
        WT = sb("wt", [128, NW])
        BI = sb("bi", [128, NBI])
        CO = sb("co", [128, NCO])
        MW = sb("mw", [128, 8192])
        TMP = sb("tmp", [128, 9, TW])
        SM = sb("sm", [128, 1100])
        PS = ctx.enter_context(nc.psum_tensor("ps", [128, 8, 512], F32))

        def W(n, a=0, b=None):
            if n in EAT:
                o, w = EAT[n]
                return MW[:, 2048 + o + a:2048 + o + (w if b is None else b)]
            o, w = WAT[n]
            return WT[:, o + a:o + (w if b is None else b)]

        def B(n, a=0, b=None):
            o, w = BAT[n]
            return BI[:, o + a:o + (w if b is None else b)]

        def K(n, a=0, b=None):
            if n in EAT:
                return W(n, a, b)
            o, w = CAT[n]
            return CO[:, o + a:o + (w if b is None else b)]

        smat = [0]

        def small(n):
            a = smat[0]
            smat[0] += n
            assert smat[0] <= 1100
            return SM[:, a:a + n]

        PB = Ring(range(8))
        TB = Ring(range(9))

        def mm(out, lhsT, rhs, start=True, stop=True):
            return lambda e: e.matmul(out, lhsT, rhs, start=start, stop=stop)

        def mms(*fs):
            def go(e):
                for f in fs:
                    r = f(e)
                return r
            return go

        def act(out, in_, f, scale=1.0, bias=None, **kw):
            if f == ACT.Copy:
                return lambda e: e.activation(out, in_, f, scale=scale, **kw)
            return lambda e: e.activation(out, in_, f, bias=K("zero")[0:out.shape[0], :] if bias is None else bias,
                                          scale=scale, **kw)

        def tt(out, a, b, op):
            return lambda e: e.tensor_tensor(out, a, b, op)

        def ts(out, a, s1, s2, op0, op1=None):
            if op1 is None:
                return lambda e: e.tensor_scalar(out, a, s1, None, op0)
            return lambda e: e.tensor_scalar(out, a, s1, s2, op0, op1)

        def stt(out, a, s, b, op0, op1):
            return lambda e: e.scalar_tensor_tensor(out=out, in0=a, scalar=s, in1=b, op0=op0, op1=op1)

        def ttr(out, a, b, acc):
            return lambda e: e.tensor_tensor_reduce(out, a, b, 1.0, 0.0, ALU.mult, ALU.add, acc)

        def red(out, a, op=ALU.add):
            return lambda e: e.tensor_reduce(out, a, AX, op)

        def rcp(out, a):
            return lambda e: e.reciprocal(out, a)

        def tr(out, a):
            n = a.shape[0]
            return lambda e: e.transpose(out, a, K("ident")[0:n, 0:n])

        def cp(out, a):
            return lambda e: e.tensor_copy(out, a)

        MU, AD, SU, MX, MN = ALU.mult, ALU.add, ALU.subtract, ALU.max, ALU.min

        def bar():
            toks = [e.last() for e in (A, V, G, P)]
            for e in (A, V, G, P):
                e.items.append((lambda eng: None, toks, False))
            for r in (PB, TB):
                r.reset()
            return toks

        def sl(t):
            return slice(t * TW, (t + 1) * TW)

        s_x, s_w, s_c, s_m1, s_m2, s_m3 = (sem(n) for n in ("d_x", "d_w", "d_c", "d_m1", "d_m2", "d_m3"))
        X = BIG[1]
        SP.dma(lambda e: e.dma_start(BIG[1][:, :], xT), (s_x, 16))
        SP.dma(lambda e: e.dma_start(CO[:, :], con), (s_c, 16))
        SP.dma(lambda e: e.dma_start(BI[:, :], bia), (s_c, 32))
        SP.dma(lambda e: e.dma_start(MW[:, 2048:2048 + NE], early), (s_c, 48))
        SP.dma(lambda e: e.dma_start(WT[:, :], wts), (s_w, 16))
        SP.dma(lambda e: e.dma_start(MW[:, 0:2048], m1), (s_m1, 16))
        for e in (A, V, G, P):
            e.items.append((lambda eng: None, [(s_x, 16), (s_c, 48), (s_w, 16)], False))

        def ln_gen(src, dst, t, eps=None, gb=None, rms=False, wait=()):
            s = sl(t)
            if not rms:
                b, w = PB.get()
                p = P(mm(PS[:, b, :], K("mean"), src[:, s]), w, *wait)
                yield
                v = V(tt(dst[:, s], src[:, s], PS[:, b, :], SU), p)
                PB.free(b, v)
                x = dst
            else:
                v = None
                x = src
            k, w = TB.get()
            yield
            a = A(act(TMP[:, k, :], x[:, s], ACT.Square), v, w, *wait)
            yield
            b, w = PB.get()
            p = P(mm(PS[:, b, :], K("mean"), TMP[:, k, :]), a, w)
            yield
            a = A(act(TMP[:, k, :], PS[:, b, :], ACT.Sqrt, bias=K("eps5") if eps is None else eps), p)
            PB.free(b, a)
            yield
            v = V(rcp(TMP[:, k, :], TMP[:, k, :]), a)
            yield
            if gb is None:
                v = V.chain(tt(dst[:, s], x[:, s], TMP[:, k, :], MU))
            elif len(gb) == 1:
                v = V.chain(stt(dst[:, s], x[:, s], gb[0], TMP[:, k, :], MU, MU))
            else:
                v = V.chain(tt(dst[:, s], x[:, s], TMP[:, k, :], MU))
                v = V.chain(ts(dst[:, s], dst[:, s], gb[0], gb[1], MU, AD))
            TB.free(k, v)

        def lin_gen(t, dst, w, src, f, bias=None, scale=1.0):
            b, wt = PB.get()
            p = P(mm(PS[:, b, :], w, src[:, sl(t)]), wt)
            yield
            a = A(act(dst[:, sl(t)], PS[:, b, :], f, bias=bias, scale=scale), p)
            PB.free(b, a)

        def ffn_gen(t, src, w1, b1, nh, func, w2, fin):
            bo, wo = PB.get()
            hs = []
            for j in range(nh):
                b, w = PB.get()
                p = P(mm(PS[:, b, :], w1(j), src[:, sl(t)]), w)
                yield
                k, w = TB.get()
                a = A(act(TMP[:, k, :], PS[:, b, :], func, bias=b1(j)), p, w)
                PB.free(b, a)
                hs.append((j, k, a))
                if len(hs) == 2:
                    jj, kk, aa = hs.pop(0)
                    p = P(mm(PS[:, bo, :], w2(jj), TMP[:, kk, :], start=(jj == 0), stop=False), aa, wo)
                    TB.free(kk, p)
            jj, kk, aa = hs.pop(0)
            p = P(mm(PS[:, bo, :], w2(jj), TMP[:, kk, :], start=(jj == 0), stop=True), aa, wo)
            TB.free(kk, p)
            yield
            tok = fin(bo, p)
            PB.free(bo, tok)

        VT, X, XN, XR, KB, EK, Q, U8 = BIG
        pipe((ln_gen(X, XN, t) for t in range(NT)), 4)
        bar()
        pipe((ln_gen(XN, XR, t, eps=K("eps6"), gb=[B("nw")], rms=True) for t in range(NT)), 4)
        etac = small(1)
        V(ts(etac, B("eta"), -1.0, None, MU))
        V.chain(tt(etac, etac, B("eta"), MX))
        V.chain(ts(etac, etac, 1e-6, None, MX))
        bar()

        def phi_gen(t, dst, w, edst=None):
            b, wt = PB.get()
            p = P(mm(PS[:, b, :], w, XR[:, sl(t)]), wt)
            yield
            k, w_ = TB.get()
            v = V(ts(TMP[:, k, :], PS[:, b, :], 0.0, None, MN), p, w_)
            yield
            a = A(act(TMP[:, k, :], TMP[:, k, :], ACT.Exp), v)
            yield
            v = V(stt(dst[:, sl(t)], PS[:, b, :], 0.0, TMP[:, k, :], MX, AD), a)
            PB.free(b, v)
            TB.free(k, v)
            if edst is not None:
                V.chain(ts(edst[:, sl(t)], dst[:, sl(t)], etac, None, MU))

        pipe([g for t in range(NT) for g in (phi_gen(t, KB, W("wk"), EK), phi_gen(t, Q, W("wq")),
                                              lin_gen(t, VT, W("wv"), XR, ACT.Copy))], 4)

        qs = small(8)
        q2 = TMP[:, 8, :]
        for n, j in (("f1", 0), ("f2", 1)):
            V.chain(ts(q2, W(n), -1.0, None, MU))
            V.chain(tt(q2, q2, W(n), MX))
            V.chain(red(qs[:, j:j + 1], q2))
        bar()
        b, w = PB.get()
        p = P(mm(PS[:, b, 0:2], K("one"), qs[:, 0:2]))
        PB.free(b)
        V(ts(qs[:, 2:4], PS[:, b, 0:2], 1.0 / 65536, 1e-5, MU, AD), p)
        V.chain(rcp(qs[:, 4:6], qs[:, 2:4]))
        RND = 12582912.0
        for n, j in (("f1", 0), ("f2", 1)):
            V.chain(ts(W(n), W(n), qs[:, 4 + j:5 + j], None, MU))
            V.chain(ts(W(n), W(n), 1.5, -1.5, MN, MX))
            V.chain(ts(W(n), W(n), RND, None, AD))
            V.chain(ts(W(n), W(n), -RND, None, AD))
            V.chain(ts(W(n), W(n), 1.0, -1.0, MN, MX))
        bar()

        def fin0(t):
            def f(b, p):
                V(stt(X[:, sl(t)], PS[:, b, :], B("f2b"), X[:, sl(t)], AD, AD), p)
                return V.chain(tt(X[:, sl(t)], X[:, sl(t)], XN[:, sl(t)], AD))
            return f

        pipe((ffn_gen(t, XN, lambda j: W("f1", 128 * j, 128 * j + 128), lambda j: B("f1b", j, j + 1), 4, ACT.Relu,
                      lambda j: W("f2", 128 * j, 128 * j + 128), fin0(t)) for t in range(NT)), 2)
        bar()

        def cv(buf, c, r=slice(0, 128)):
            return buf[r, 128 * c:128 * c + 128]

        Mst = BIG[7][:, 0:1024].rearrange("p (a d) -> p a d", a=8)
        Yb = BIG[7][:, 1024:2048].rearrange("p (s d) -> p s d", s=C)
        EKBL = BIG[7][:, 2048:3072].rearrange("p (a h f) -> p a h f", a=8, h=2)
        Yb2 = BIG[7][:, 3072:4096].rearrange("p (s d) -> p s d", s=C)
        YS = [Yb, Yb2]
        gr = [TMP[:, 0, 0:384], TMP[:, 1, 0:384]]
        vch = [TMP[:, 2, 0:128], TMP[:, 2, 128:256]]
        pj = TMP[:, 3, 0:128]
        scr = TMP[:, 3, 128:256]
        scr2 = TMP[:, 3, 256:384]
        vw = TMP[:, 3, 384:512]
        pT = TMP[:, 4, 0:256].rearrange("p (k n) -> p k n", k=2)
        ekt = [TMP[:, 5, 0:64], TMP[:, 5, 64:128]]
        SC = [TMP[:, 6 + i, :] for i in range(2)]

        def sv(i):
            o = SC[i]
            return dict(G=o[:, 0:24], kap=o[:, 24:25], eb=o[:, 25:26], vb=o[:, 26:27], c=o[:, 27:28],
                        cd=o[:, 28:36], dd=o[:, 36:52], crep=o[:, 52:60], nd=o[:, 60:76], nkc=o[:, 76:84],
                        BC=o[:, 84:100], cc=o[:, 100:108], kapn=o[:, 108:109], t1=o[:, 109:117], vs=o[:, 117:118])

        st = small(24)
        Sst = st[:, 0:3]
        Pst, qst, rP, mst, bia_, rR, Rm = (st[:, 3:4], st[:, 4:5], st[:, 5:6], st[:, 6:7], st[:, 7:8], st[:, 8:9], st[:, 9:10])
        w2r, g0, wc = st[:, 10:11], st[:, 11:12], st[:, 12:13]
        tq = st[:, 13:14]
        rp8 = small(8)
        Rc = small(8)
        Wst = small(8)
        V(lambda e: e.memset(Mst, 0.0))
        V(lambda e: e.memset(st, 0.0))
        V.chain(lambda e: e.memset(Pst, 1.0))
        V.chain(lambda e: e.memset(rP, 1.0))
        bar()

        def prep(c):
            i = c % 2
            s = sv(i)
            lo = slice(0, 64)
            p1 = P(mms(mm(PS[:, 0, 0:128], cv(KB, c, lo), cv(EK, c, lo)),
                       mm(PS[:, 0, 128:256], cv(EK, c, lo), cv(EK, c, lo)),
                       mm(PS[:, 0, 256:384], cv(VT, c), cv(VT, c))), prep.tok.get("b0", []))
            p2 = P(mms(mm(PS[:, 1, 0:128], cv(XR, c), W("wv")),
                       mm(PS[:, 1, 128:192], cv(EK, c, lo), K("ident")[0:64, 0:64]),
                       mm(PS[:, 1, 192:193], cv(KB, c, lo), K("one")[0:64, 0:1]),
                       mm(PS[:, 1, 193:194], cv(EK, c, lo), K("one")[0:64, 0:1]),
                       mm(PS[:, 1, 194:195], cv(VT, c), K("one")[:, 0:1])), prep.tok.get("b1", []))
            yield
            vv = V(tt(gr[i].rearrange("p (k b s) -> p k b s", k=3, b=NB),
                      PS[:, 0, 0:384].rearrange("p (k b s) -> p k b s", k=3, b=NB),
                      K("hid").rearrange("p (k b s) -> p k b s", k=1, s=1).broadcast_to((128, 3, NB, C)), MU), p1)
            a1 = A(act(vch[i], PS[:, 1, 0:128], ACT.Copy), p2, prep.tok.get(("v", i), []))
            a2 = A(act(ekt[i], PS[:, 1, 128:192], ACT.Copy), p2)
            a3 = A(act(s["kap"], PS[:, 1, 192:193], ACT.Copy), p2, prep.tok.get(("v", i), []))
            a4 = A(act(s["eb"], PS[:, 1, 193:194], ACT.Copy, scale=1.0 / 64), p2)
            a5 = A(act(s["vb"], PS[:, 1, 194:195], ACT.Copy, scale=1.0 / 128), p2)
            prep.tok["b1"] = [a5]
            prep.tok["b0"] = [vv]
            yield
            v = V(red(s["G"].rearrange("p (k s) -> p k s", k=3),
                      gr[i].rearrange("p (k b s) -> p k s b", k=3, b=NB)), vv)
            p3 = P(mms(*[mm(PS[:, 2 + s_ // 4, (s_ % 4) * 128:(s_ % 4) * 128 + 128], K("sel", 128 * s_, 128 * s_ + 128),
                            vch[i]) for s_ in range(C)]), a1, prep.tok.get("b23", []))
            g = G(tt(s["c"], s["eb"], s["vb"], MU), a5)
            yield
            g = G.chain(tt(s["cd"], K("oneh"), s["c"].broadcast_to((128, C)), MU))
            p4 = P(mm(PS[:, 1, 256:264], K("blk"), s["cd"]), g, a5)
            yield
            v = V(cp(s["crep"], PS[:, 1, 256:264]), p4)
            v = V.chain(ts(s["kapn"], s["kap"], -1.0, None, MU), a3)
            v = V.chain(ts(s["nkc"], s["crep"], s["kapn"], None, MU))
            yield
            gk, gg, gv = s["G"][:, 0:8], s["G"][:, 8:16], s["G"][:, 16:24]
            g = G(ts(s["cc"], s["crep"], s["c"], None, MU), v)
            g = G.chain(tt(s["t1"], gg, gv, MU))
            g = G.chain(ts(s["t1"], s["t1"], 1.0 / 8192, None, MU))
            g = G.chain(tt(s["cc"], s["t1"], s["cc"], SU))
            yield
            g = G.chain(ts(s["BC"][:, 8:16], s["cc"], 2.0, None, MU))
            g = G.chain(tt(s["dd"][:, 0:8], gv, K("oneh"), MU))
            g = G.chain(tt(s["dd"][:, 8:16], s["cc"], K("oneh"), MU))
            gd = g
            yield
            g = G.chain(ts(s["vs"], s["vb"], 128.0, None, MU))
            g = G.chain(tt(s["t1"], gk, gv, MU))
            g = G.chain(ts(s["cc"], s["nkc"], s["vs"], None, MU))
            g = G.chain(tt(s["cc"], s["cc"], s["t1"], AD))
            g = G.chain(ts(s["BC"][:, 0:8], s["cc"], -2.0, None, MU))
            p5 = P(mm(PS[:, 1, 272:288], K("blk"), s["dd"]), gd, v)
            yield
            v = V(cp(s["nd"], PS[:, 1, 272:288]), p5)
            prep.tok["b1"] = [v]
            out = [v, g]
            for s_ in range(C):
                a = A(act(YS[i][:, s_, :], PS[:, 2 + s_ // 4, (s_ % 4) * 128:(s_ % 4) * 128 + 128], ACT.Identity,
                          scale=s["G"][:, s_:s_ + 1], bias=s["nkc"][:, s_:s_ + 1]), p3, v)
                if s_ % 2:
                    yield
            prep.tok["b23"] = [a]
            prep.ready[c] = out + [a]

        prep.tok = {}
        prep.ready = {}
        for _ in prep(0):
            pass
        mtok = None
        for c in range(NC):
            i = c % 2
            s = sv(i)
            ahead = prep(c + 1) if c + 1 < NC else iter(())
            rdy = prep.ready[c]
            ps4 = [PS[:, 4 + h, 0:128].rearrange("p (k b j) -> p k b j", k=2, b=8) for h in range(2)]
            fs = []
            for b_ in range(NB):
                h = slice(64 * (b_ % 2), 64 * (b_ % 2) + 64)
                for kk, buf in ((0, KB), (1, EK)):
                    fs.append(mm(ps4[b_ % 2][:, kk, b_ // 2, :], Mst[h, b_ // 2, :], cv(buf, c, h)[:, 8 * b_:8 * b_ + 8]))
            p = P(mms(*fs), mtok, rdy)
            for h in range(2):
                a = A(act(pT[:, :, :].rearrange("p k (b h j) -> p h k b j", b=8, h=2)[:, h], ps4[h], ACT.Copy), p)
            p = P(mms(*[tr(PS[:, 6, 128 * k:128 * k + 128], pT[:, k, :])
                        for k in range(2)]), a)
            v = V(tt(wc, mst, s["kapn"], MU), rdy)
            v = V.chain(ts(pj, PS[:, 6, 0:128], wc, None, AD), p)
            v = V.chain(ttr(scr, pj, pj, Sst[:, 0:1]))
            v = V(ttr(scr2, pj, vch[i], Sst[:, 1:2]), v)
            v = V.chain(ts(Sst[:, 1:2], Sst[:, 1:2], -2.0, None, MU))
            v = V.chain(ttr(scr, PS[:, 6, 128:256], vch[i], g0))
            v = V.chain(tt(wc, mst, s["c"], MU))
            v = V.chain(ts(g0, g0, 1.0 / 8192, None, MU))
            v = V.chain(tt(g0, g0, wc, SU))
            v = V.chain(ts(Sst[:, 2:3], g0, 2.0, None, MU))
            vS = v
            aR = None
            for t in range(C):
                bk = 6 + t % 2
                p = P(mm(PS[:, bk, 0:3], K("sel", 128 * t, 128 * t + 128), Sst), vS)
                v = V(stt(bia_, s["nd"][:, t:t + 1], Pst, PS[:, bk, 0:1], MU, AD), p, V.last())
                a = A(act(w2r, PS[:, bk, 1:2], ACT.Identity, scale=rP, bias=bia_), v, aR)
                a = A.chain(act(w2r, w2r, ACT.Relu))
                aw = A.chain(act(Wst[:, t:t + 1], w2r, ACT.Sqrt))
                w_ = Wst[:, t:t + 1]
                if t < C - 1:
                    v1 = V(stt(pj, YS[i][:, t, :], w_, pj, MU, AD), aw)
                    v2 = V(stt(Sst[:, 1:3], s["BC"].rearrange("p (k s) -> p s k", k=2)[:, t, :], w_, Sst[:, 1:3], MU, AD),
                           aw, p)
                    v3 = V(ttr(scr, pj, pj, Sst[:, 0:1]), v1, v2)
                    vS = v3
                v = V(stt(tq, s["nd"][:, 8 + t:9 + t], w_, PS[:, bk, 2:3], MU, AD), aw, V.last())
                v = V.chain(stt(qst, tq, w_, qst, MU, AD))
                v = V.chain(stt(Pst, Pst, 1e-5, qst, MU, AD))
                aR = A(act(rP, Pst, ACT.Sqrt), v)
                v = V(stt(mst, s["crep"][:, t:t + 1], w_, mst, MU, AD), v)
                next(ahead, 0)
                next(ahead, 0)
            for _ in ahead:
                pass
            v = V(rcp(rR, rP), aR, v)
            v = V.chain(tt(qst, qst, rR, MU))
            v = V.chain(tt(qst, qst, rR, MU))
            v = V.chain(tt(mst, mst, rR, MU))
            v = V.chain(lambda e: e.memset(Pst, 1.0))
            v = V.chain(lambda e: e.memset(rP, 1.0))
            v = V.chain(ttr(rp8, Wst, K("oneh"), wc))
            v = V.chain(tt(wc, wc, rR, MU))
            v = V.chain(ts(vw, vch[i], wc, None, MU))
            vvw = v
            v = V.chain(ts(rp8, K("pairm"), rR, None, MU))
            g = G(tt(EKBL.rearrange("p a h f -> p (a h) f"),
                     ekt[i].rearrange("p (a f) -> p a f", a=1).broadcast_to((128, 16, 64)),
                     K("hid").rearrange("p (a f) -> p a f", f=1).broadcast_to((128, 16, 64)), MU), rdy, P.last())
            pr = P(mm(PS[:, 5, 256:264], K("rselA"), rp8), v)
            v = V(cp(Rc, PS[:, 5, 256:264]), pr)
            p = P(mms(*[mm(PS[:, 6 + a_ // 4, (a_ % 4) * 128:(a_ % 4) * 128 + 128],
                           EKBL[:, a_].rearrange("p h f -> p (h f)"), vw) for a_ in range(8)]), g, vvw, V.last())
            v = V(tt(Mst, Mst, Rc.rearrange("p (a d) -> p a d", d=1).broadcast_to((128, 8, 128)), MU), v)
            for h in range(2):
                v = V(tt(Mst[:, 4 * h:4 * h + 4, :], Mst[:, 4 * h:4 * h + 4, :],
                         PS[:, 6 + h, :].rearrange("p (a d) -> p a d", a=4), AD), v, p)
            mtok = v
            prep.tok[("v", i)] = [p, V.last()]
        b2 = V(ts(rp8, K("pairm"), mst, None, MU), mtok)
        pr = P(mm(PS[:, 5, 256:264], K("rselA"), rp8), b2)
        v = V(cp(Rc, PS[:, 5, 256:264]), pr)
        v = V.chain(tt(Mst, Mst, Rc.rearrange("p (a d) -> p a d", d=1).broadcast_to((128, 8, 128)), SU))
        bar()

        def mo_gen(b_):
            h = slice(64 * (b_ % 2), 64 * (b_ % 2) + 64)
            c0 = slice(b_ * S, (b_ + 1) * S)
            b, w = PB.get()
            p = P(mm(PS[:, b, 0:256], Mst[h, b_ // 2, :],
                     Q[h, :].rearrange("p (c b j) -> p b c j", b=NB, c=NC)[:, b_]), w)
            yield
            k, w = TB.get()
            a = A(act(TMP[:, k, 0:256], PS[:, b, 0:256], ACT.Copy), p, w)
            PB.free(b, a)
            yield
            b, w = PB.get()
            p = P(mm(PS[:, b, 0:256], W("wout"), TMP[:, k, 0:256]), a, w)
            TB.free(k, p)
            yield
            v = V(tt(BIG[0][:, c0].rearrange("p (c j) -> p c j", c=NC),
                     X[:, :].rearrange("p (c b j) -> p b c j", b=NB, c=NC)[:, b_],
                     PS[:, b, 0:256].rearrange("p (c j) -> p c j", c=NC), AD), p)
            PB.free(b, v)

        pipe((mo_gen(b_) for b_ in range(NB)), 4)
        bar()

        X = BIG[0]
        XG, XA, QF, KF, YF = BIG[2], BIG[3], BIG[4], BIG[5], BIG[6]
        XN = BIG[1]
        pipe((ln_gen(X, XN, t) for t in range(NT)), 4)
        bar()
        bst = small(6)
        agg = small(2)
        gs = small(32)
        gs2 = small(32)
        gsc = small(32)

        def group_norm(src, dst, g_, b_):
            for n in range(NB):
                V.chain(lambda e, n=n: e.bn_stats(bst, src[:, n * S:(n + 1) * S]))
                V.chain(lambda e, n=n: e.bn_aggr(agg, bst))
                V.chain(cp(gs[:, n:n + 1], agg[:, 0:1]))
                V.chain(stt(gs[:, 16 + n:17 + n], agg[:, 0:1], agg[:, 0:1], agg[:, 1:2], MU, AD))
            p = P(mm(PS[:, 0, 0:32], K("g8"), gs), V.last())
            V(cp(gs2, PS[:, 0, 0:32]), p)
            V.chain(tt(gsc[:, 0:16], gs2[:, 0:16], gs2[:, 0:16], MU))
            V.chain(tt(gsc[:, 0:16], gs2[:, 16:32], gsc[:, 0:16], SU))
            V.chain(ts(gsc[:, 0:16], gsc[:, 0:16], 0.0, None, MX))
            a = A(act(gsc[:, 0:16], gsc[:, 0:16], ACT.Sqrt, bias=K("eps5")), V.last())
            V.chain(rcp(gsc[:, 0:16], gsc[:, 0:16]), a)
            V.chain(ts(gsc[:, 0:16], gsc[:, 0:16], g_, None, MU))
            V.chain(tt(gsc[:, 16:32], gs2[:, 0:16], gsc[:, 0:16], MU))
            V.chain(ts(gsc[:, 16:32], gsc[:, 16:32], -1.0, b_, MU, AD))
            v = V.last()
            for n in range(NB):
                c0 = slice(n * S, (n + 1) * S)
                if n % 2:
                    A(act(dst[:, c0], src[:, c0], ACT.Identity, scale=gsc[:, n:n + 1], bias=gsc[:, 16 + n:17 + n]), v)
                else:
                    V(ts(dst[:, c0], src[:, c0], gsc[:, n:n + 1], gsc[:, 16 + n:17 + n], MU, AD), v)
            bar()

        group_norm(XN, XG, B("g1"), B("b1n"))

        def qk_gen(t, w, dst, dec):
            b, wt = PB.get()
            p = P(mm(PS[:, b, :], w, XG[:, sl(t)]), wt)
            yield
            k, w_ = TB.get()
            a = A(act(TMP[:, k, :], PS[:, b, :], ACT.Square), p, w_)
            yield
            b2, wt = PB.get()
            p = P(mm(PS[:, b2, :], K("one"), TMP[:, k, :]), a, wt)
            yield
            a = A(act(TMP[:, k, :], PS[:, b2, :], ACT.Sqrt), p)
            PB.free(b2, a)
            yield
            v = V(ts(TMP[:, k, :], TMP[:, k, :], 1e-12, None, MX), a)
            v = V.chain(rcp(TMP[:, k, :], TMP[:, k, :]))
            yield
            v = V.chain(tt(TMP[:, k, :], TMP[:, k, :], PS[:, b, :], MU))
            PB.free(b, v)
            yield
            v = V.chain(tt(dst[:, sl(t)].rearrange("p (a n) -> p a n", a=2),
                           TMP[:, k, :].rearrange("p (a n) -> p a n", a=2),
                           K(dec).rearrange("p (a n) -> p a n", a=1).broadcast_to((128, 2, 256)), MU))
            TB.free(k, v)

        pipe([g for t in range(NT) for g in (qk_gen(t, W("q1"), QF, "dq"), qk_gen(t, W("k1"), KF, "dk"))], 3)
        bar()
        AB = BIG[7]
        KM = [AB[:, 1024 * i:1024 * i + 1024].rearrange("p (r n) -> p r n", r=4) for i in range(2)]
        VM = [AB[:, 2048 + 1024 * i:3072 + 1024 * i].rearrange("p (a r n) -> p a r n", a=2, r=4) for i in range(2)]
        KT_ = [BIG[6][:, 256 * i:256 * i + 256].rearrange("p (a n) -> p a n", a=2) for i in range(2)]
        VTK = [BIG[6][:, 512 + 256 * i:768 + 256 * i].rearrange("p (a n) -> p a n", a=2) for i in range(2)]
        SBD = [BIG[6][:, 1024 + 128 * i:1152 + 128 * i] for i in range(2)]
        YT = [BIG[6][:, 1280 + 256 * i:1536 + 256 * i] for i in range(2)]
        S1 = [BIG[6][:, 1792 + 1024 * i:2816 + 1024 * i].rearrange("p (a r n) -> p a r n", a=2, r=4) for i in range(2)]
        setfree = [[], []]
        sring = Ring([0, 1])

        def ret_gen(n):
            i = n % 2
            c0 = n * S
            w0 = setfree[i]
            vs_ = []
            for r in range(4):
                vs_.append(V(ts(KM[i][:, r, :], KF[:, c0:c0 + S], K("rm", r, r + 1), None, MU), w0))
            b, wt = PB.get()
            p = P(mms(mm(PS[:, b, 0:128], XG[:, c0:c0 + 128], W("v1")),
                      mm(PS[:, b, 128:256], XG[:, c0 + 128:c0 + 256], W("v1")),
                      tr(PS[:, b, 256:384], KF[:, c0:c0 + 128])), wt)
            yield
            a = A(act(VTK[i], PS[:, b, 0:256].rearrange("p (a n) -> p a n", a=2), ACT.Copy), p, w0)
            a = A(act(KT_[i][:, 0, :], PS[:, b, 256:384], ACT.Copy), p)
            PB.free(b, a)
            yield
            gg = []
            for h in range(2):
                gg.append(G(tt(VM[i][:, h], VTK[i][:, h, :].rearrange("p (r n) -> p r n", r=1).broadcast_to((128, 4, 128)),
                               K("colr").rearrange("p (r n) -> p r n", r=4), MU), a, w0))
            b, wt = PB.get()
            p = P(mm(PS[:, b, 0:128], KT_[i][:, 0, :], VTK[i][:, 0, :]), a, wt)
            yield
            v = V(tt(SBD[i], PS[:, b, 0:128], K("bd8"), MU), p, w0)
            PB.free(b, v)
            vsb = v
            by, wy = PB.get()
            py = None
            for g_ in range(4):
                r32 = slice(32 * g_, 32 * g_ + 32)
                ks, ws = sring.get()
                done = []
                for h in range(2):
                    b, wt = PB.get()
                    cc = c0 + 128 * h
                    p = P(mms(*[mm(PS[:, b, 128 * r:128 * r + 128], KM[i][r32, r, 128 * h:128 * h + 128],
                                   QF[r32, cc:cc + 128]) for r in range(4)]), vs_, wt)
                    yield
                    v = V(tt(S1[ks][:, h], PS[:, b, :].rearrange("p (r n) -> p r n", r=4),
                             K("tri").rearrange("p (r n) -> p r n", r=1).broadcast_to((128, 4, 128)), MU), p, ws)
                    PB.free(b, v)
                    done.append(v)
                yield
                fs = []
                for h in range(2):
                    o = PS[r32, by, 128 * h:128 * h + 128]
                    if h:
                        fs.append(mm(o, SBD[i][:, r32], QF[:, c0 + 128:c0 + 256], start=True, stop=False))
                    for r in range(4):
                        fs.append(mm(o, VM[i][:, h, r, r32], S1[ks][:, h, r, :], start=(h == 0 and r == 0), stop=(r == 3)))
                py = P(mms(*fs), done, gg, vsb, wy)
                sring.free(ks, py)
            yield
            a = A(act(YT[i], PS[:, by, 0:256], ACT.Copy), py, w0)
            PB.free(by, a)
            yield
            b, wt = PB.get()
            p = P(mm(PS[:, b, 0:256], W("o1"), YT[i]), a, wt)
            yield
            v = V(stt(XA[:, c0:c0 + S], PS[:, b, 0:256], B("ob1"), XN[:, c0:c0 + S], AD, AD), p)
            PB.free(b, v)
            setfree[i] = [v, p, py]

        pipe((ret_gen(n) for n in range(NB)), 2)
        bar()
        group_norm(XA, XG, B("fg1"), B("fb1"))

        def fin1(t):
            def f(b, p):
                v = V(stt(X[:, sl(t)], PS[:, b, :], B("b12"), X[:, sl(t)], AD, AD), p)
                return V.chain(tt(X[:, sl(t)], X[:, sl(t)], XA[:, sl(t)], AD))
            return f

        pipe((ffn_gen(t, XG, lambda j: W("w11", 128 * j, 128 * j + 128), lambda j: B("b11", j, j + 1), 2, ACT.Silu,
                      lambda j: W("w12", 128 * j, 128 * j + 128), fin1(t)) for t in range(NT)), 2)
        bar()

        R = [BIG[7][:, 256 * i:256 * i + 256] for i in range(8)]

        def r3(ap, n):
            return ap[:, 0:32 * n].rearrange("p (b e) -> p b e", e=n)

        def bc(ap, n):
            return ap.rearrange("p (b e) -> p b e", e=1).broadcast_to((128, 32, n))

        def logits(wt, n, bias, dst):
            p = P(mms(*[mm(PS[:, 0, n * k:n * k + n], XN[:, 128 * k:128 * k + 128], wt) for k in range(32)]))
            if bias is None:
                V.chain(cp(dst[:, 0:32 * n], PS[:, 0, 0:32 * n]), p)
            else:
                V.chain(tt(r3(dst, n), r3(PS[:, 0, :], n),
                           bias.rearrange("p (b e) -> p b e", b=1).broadcast_to((128, 32, n)), AD), p)

        def softmax8(lg, n, tmp):
            m, z = small(32), small(32)
            V.chain(red(m, r3(lg, n), MX))
            V.chain(tt(r3(lg, n), r3(lg, n), bc(m, n), SU))
            a = A(act(lg[:, 0:32 * n], lg[:, 0:32 * n], ACT.Exp), V.last())
            V.chain(red(z, r3(lg, n)), a)
            V.chain(rcp(z, z))
            V.chain(tt(r3(lg, n), r3(lg, n), bc(z, n), MU))

        def moe(n, nh, w1, b1, func, w2, b2, wtok, waits):
            def gen(t, e_):
                b, w = PB.get()
                p = P(mms(*[mm(PS[:, b, 128 * k:128 * k + 128],
                               wtok[:, 4 * t + k, e_:e_ + 1].broadcast_to((128, 128)), K("ident")) for k in range(4)]),
                      w, waits)
                yield
                kb, w = TB.get()
                a0 = A(act(TMP[:, kb, :], PS[:, b, :], ACT.Copy), p, w)
                PB.free(b, a0)

                def fin(bo, p):
                    v = V(stt(TMP[:, kb, :], PS[:, bo, :], b2(e_), TMP[:, kb, :], AD, MU), p, a0)
                    v2 = V.chain(tt(X[:, sl(t)], X[:, sl(t)], TMP[:, kb, :], AD))
                    TB.free(kb, v2)
                    return v
                yield from ffn_gen(t, XN, lambda j: w1(e_, j), lambda j: b1(e_, j), nh, func, lambda j: w2(e_, j), fin)
            pipe((gen(t, e_) for e_ in range(n) for t in range(NT)), 2)
            bar()

        lg, wt1 = R[0], R[1]
        logits(W("gw1"), 4, B("gb1"), lg)
        ent = small(32)
        ab = small(32)
        held = PB.idle.pop([k for k, _ in PB.idle].index(7))
        for t in range(NT):
            b, w = PB.get()
            p = P(mm(PS[0:64, b, :], W("dw1"), XN[:, sl(t)]), w, V.last())
            k, w = TB.get()
            a = A(act(TMP[0:64, k, :], PS[0:64, b, :], ACT.Relu, bias=B("db1")[0:64, :]), p, w)
            PB.free(b, a)
            p = P(mms(*[mm(PS[:, 7, 4 * t + j:4 * t + j + 1], TMP[0:64, k, 128 * j:128 * j + 128], W("dw2")[0:64, :])
                        for j in range(4)]), a)
            TB.free(k, p)
        V.chain(ts(ent, PS[:, 7, 0:32], B("db2"), None, AD), p)
        PB.free(7)
        V.chain(ts(ab, ent, -1.0, None, MU))
        V.chain(tt(ab, ent, ab, MX))
        a = A(act(ab, ab, ACT.Exp, scale=-1.0), V.last())
        a = A.chain(act(ab, ab, ACT.Ln, bias=K("one")[:, 0:1]))
        V.chain(ts(ent, ent, 0.0, None, MX), a)
        V.chain(tt(ent, ent, ab, AD))
        V.chain(ts(ent, ent, -0.5, None, AD))
        V.chain(ts(ent, ent, 1.0 / 1.5, None, MU))
        V.chain(ts(ent, ent, 0.0, 1.0, MX, MN))
        V.chain(ts(ent, ent, 3.0, 1.0, MU, AD))
        V.chain(ts(ent, ent, RND, None, AD))
        V.chain(ts(ent, ent, -RND, None, AD))
        V.chain(ts(ent, ent, 1.0, 4.0, MX, MN))
        rk = R[2]
        V.chain(lambda e: e.memset(rk[:, 0:128], 0.0))
        l3, k3 = r3(lg, 4), r3(rk, 4)
        for i in range(4):
            for j in range(i + 1, 4):
                V.chain(tt(ab, l3[:, :, j], l3[:, :, i], ALU.is_gt))
                V.chain(tt(k3[:, :, i], k3[:, :, i], ab, AD))
                V.chain(ts(ab, ab, -1.0, 1.0, MU, AD))
                V.chain(tt(k3[:, :, j], k3[:, :, j], ab, AD))
        V.chain(tt(k3, k3, bc(ent, 4), ALU.is_lt))
        V.chain(red(ab, l3, MX))
        V.chain(tt(l3, l3, bc(ab, 4), SU))
        a = A(act(lg[:, 0:128], lg[:, 0:128], ACT.Exp), V.last())
        V.chain(tt(l3, l3, k3, MU), a)
        V.chain(red(ab, l3))
        V.chain(rcp(ab, ab))
        V.chain(tt(l3, l3, bc(ab, 4), MU))
        bar()
        moe(4, 2, lambda e, j: MW[:, 256 * e + 128 * j:256 * e + 128 * j + 128], lambda e, j: B("eb1", 2 * e + j, 2 * e + j + 1),
            ACT.Relu, lambda e, j: MW[:, 1024 + 256 * e + 128 * j:1024 + 256 * e + 128 * j + 128],
            lambda e: B("eb2", e, e + 1), l3, [(s_m1, 16)])
        mw_free = bar()
        SP.dma(lambda e: e.dma_start(MW[:, :], m2), (s_m2, 16), mw_free, (s_m1, 16))

        pipe((ln_gen(X, XN, t) for t in range(NT)), 4)
        bar()
        XT, X1, H1, H2, KN, DG = BIG[2], BIG[3], BIG[4], BIG[5], BIG[6], BIG[7]
        XT3 = XT[:, :].rearrange("p (b d) -> p b d", b=32)
        def xt_gen(k):
            b, w = PB.get()
            p = P(mms(*[tr(PS[:, b, 128 * j:128 * j + 128], XN[:, 128 * (k + j):128 * (k + j) + 128])
                        for j in range(4)]), w)
            yield
            a = A(act(XT[:, 128 * k:128 * k + 512], PS[:, b, :], ACT.Copy), p)
            PB.free(b, a)

        pipe((xt_gen(4 * k) for k in range(8)), 2)
        XP = DG[0:32, 0:2048].rearrange("p (b d) -> p b d", b=16)
        for q_ in range(4):
            b, w = PB.get()
            p = P(mms(*[tr(PS[0:32, b, 128 * j:128 * j + 128],
                           XN[:, 256 * (4 * q_ + j) + 96:256 * (4 * q_ + j) + 128]) for j in range(4)]), w)
            a = A(act(XP[:, 4 * q_:4 * q_ + 4, :], PS[0:32, b, :].rearrange("p (b d) -> p b d", b=4), ACT.Copy), p)
            PB.free(b, a)
        bar()
        wm, wz = small(32), small(32)
        SCL = 128 ** -0.5

        def win_gen(k):
            half = k % 2
            nk = 160 if half else 128
            q0 = 128 * k
            b, w = PB.get()
            p = P(mm(PS[:, b, 0:nk], XN[:, q0:q0 + 128], XN[:, q0 + 128 - nk:q0 + 128]), w)
            yield
            kt, w = TB.get()
            sc_ = TMP[:, kt, 0:nk]
            v = V(stt(sc_, PS[:, b, 0:nk], SCL, K("band") if half else K("band0"), MU, AD), p, w)
            PB.free(b, v)
            v = V.chain(red(wm[:, k:k + 1], sc_, MX))
            v = V.chain(ts(wm[:, k:k + 1], wm[:, k:k + 1], -1.0, None, MU))
            yield
            a = A(act(sc_, sc_, ACT.Exp, bias=wm[:, k:k + 1], accum_out=wz[:, k:k + 1]), v)
            yield
            v = V(rcp(wz[:, k:k + 1], wz[:, k:k + 1]), a)
            v = V.chain(ts(sc_, sc_, wz[:, k:k + 1], None, MU))
            yield
            b, w = PB.get()
            fs = [tr(PS[:, b, 0:128], sc_[:, nk - 128:nk])]
            if half:
                fs.append(tr(PS[0:32, b, 128:256], sc_[:, 0:32]))
            p = P(mms(*fs), v, w)
            yield
            a = A(act(TMP[:, kt, 256:384], PS[:, b, 0:128], ACT.Copy), p)
            if half:
                a = A(act(TMP[0:32, kt, 384:512], PS[0:32, b, 128:256], ACT.Copy), p)
            yield
            fs = [mm(PS[:, b, 256:384], XT3[:, k, :], TMP[:, kt, 256:384], stop=not half)]
            if half:
                fs.append(mm(PS[:, b, 256:384], XP[:, k // 2, :], TMP[0:32, kt, 384:512], start=False))
            p = P(mms(*fs), a)
            TB.free(kt, p)
            yield
            v = V(tt(X1[:, q0:q0 + 128], PS[:, b, 256:384], XN[:, q0:q0 + 128], AD), p)
            PB.free(b, v)

        pipe((win_gen(k) for k in range(32)), 4)
        bar()
        pipe((ln_gen(X1, X1, t, gb=[B("g21"), B("be21")]) for t in range(NT)), 4)
        bar()

        def kn_gen(src, dst, n0, n):
            k, w = TB.get()
            a = A(act(TMP[:, k, 0:n], src[:, n0:n0 + n], ACT.Square), w)
            yield
            b, w = PB.get()
            p = P(mm(PS[:, b, 0:n], K("one"), TMP[:, k, 0:n]), a, w)
            yield
            a = A(act(TMP[:, k, 0:n], PS[:, b, 0:n], ACT.Sqrt), p)
            PB.free(b, a)
            yield
            v = V(ts(TMP[:, k, 0:n], TMP[:, k, 0:n], 1e-12, None, MX), a)
            v = V.chain(rcp(TMP[:, k, 0:n], TMP[:, k, 0:n]))
            v = V.chain(tt(dst[:, n0:n0 + n], src[:, n0:n0 + n], TMP[:, k, 0:n], MU))
            TB.free(k, v)

        pk = small(50)
        pkn, pkp, ph1, ph2, pdf = (pk[:, 10 * i:10 * i + 10] for i in range(5))
        pipe([kn_gen(XN, KN, TW * t, TW) for t in range(NT)] + [kn_gen(W("pT"), pkn, 0, 10)], 3)
        bar()
        bim = small(1)
        V(tt(bim, B("memb"), B("bi"), SU))
        bar()
        DF = DG

        def mem_gen(kn, kp, h1, h2, df, n0, n):
            s = slice(n0, n0 + n)
            b, w = PB.get()
            p = P(mm(PS[:, b, 0:n], W("wi"), kn[:, s]), w)
            yield
            k, w = TB.get()
            a = A(act(TMP[:, k, 0:n], PS[:, b, 0:n], ACT.Identity, bias=B("bi")), p, w)
            PB.free(b, a)
            yield
            b, w = PB.get()
            p = P(mm(PS[:, b, 0:n], W("wl1"), TMP[:, k, 0:n]), a, w)
            yield
            k2, w = TB.get()
            a = A(act(TMP[:, k2, 0:n], PS[:, b, 0:n], ACT.Silu, bias=B("bl1")), p, w)
            PB.free(b, a)
            yield
            b, w = PB.get()
            p = P(mm(PS[:, b, 0:n], W("wl2"), TMP[:, k2, 0:n]), a, w)
            TB.free(k2, p)
            yield
            a = A(act(h2[:, s], PS[:, b, 0:n], ACT.Silu, bias=B("bl2")), p)
            PB.free(b, a)
            yield
            b, w = PB.get()
            p = P(mm(PS[:, b, 0:n], W("memT"), h2[:, s]), a, w)
            yield
            v = V(stt(df[:, s], PS[:, b, 0:n], B("memb"), TMP[:, k, 0:n], AD, SU), p)
            PB.free(b, v)
            TB.free(k, v)

        pipe([mem_gen(KN, None, None, H2, DF, TW * t, TW) for t in range(NT)]
             + [mem_gen(pkn, None, None, ph2, pdf, 0, 10)], 3)
        bar()
        V(ts(pdf, pdf, 16.0, None, MU))
        bar()
        PB = Ring(range(7))

        def gr_gen(k, n, h2, df):
            s = slice(128 * k, 128 * k + n)
            b, w = PB.get()
            p = P(mms(tr(PS[0:n, b, 0:128], h2[:, s]),
                      tr(PS[0:n, b, 128:256], df[:, s])), w)
            yield
            kt, w = TB.get()
            a = A(act(TMP[0:n, kt, 0:256], PS[0:n, b, 0:256], ACT.Copy), p, w)
            PB.free(b, a)
            yield
            last = n != 128
            p = P(mm(PS[:, 7, 0:128], TMP[0:n, kt, 0:128], TMP[0:n, kt, 128:256], start=(k == 0 and not last), stop=last), a)
            TB.free(kt, p)

        pipe([gr_gen(k, 128, H2, DF) for k in range(32)] + [gr_gen(0, 10, ph2, pdf)], 3)
        wnew = TMP[:, 8, 0:128]
        gsx = small(2)
        bar()
        V(ts(gsx[:, 0:1], B("lrate"), 2.0 / (4256 * 128), None, MU))
        V.chain(ts(gsx[:, 1:2], B("fgate"), -1.0, 1.0, MU, AD))
        V.chain(ts(wnew, PS[:, 7, 0:128], gsx[:, 0:1], None, MU))
        V.chain(stt(wnew, W("memT"), gsx[:, 1:2], wnew, MU, AD))
        bar()
        PB = Ring(range(8))
        TB = Ring(range(8))
        MO = KN

        def mo2_gen(t):
            s = sl(t)
            b, w = PB.get()
            p = P(mm(PS[:, b, :], wnew, H2[:, s]), w)
            yield
            k, w = TB.get()
            a = A(act(TMP[:, k, :], PS[:, b, :], ACT.Identity, bias=B("memb")), p, w)
            PB.free(b, a)
            yield
            b, w = PB.get()
            p = P(mm(PS[:, b, :], W("wo2"), TMP[:, k, :]), a, w)
            yield
            a = A(act(MO[:, s], PS[:, b, :], ACT.Identity, bias=B("bo2")), p)
            PB.free(b, a)
            yield
            b, w = PB.get()
            p = P(mms(mm(PS[:, b, :], W("wg", 0, 128), X1[:, s], stop=False),
                      mm(PS[:, b, :], W("wg", 128, 256), MO[:, s], start=False)), a, w)
            yield
            a = A(act(TMP[:, k, :], PS[:, b, :], ACT.Sigmoid, bias=B("bg")), p)
            PB.free(b, a)
            yield
            v = V(tt(DG[:, s], X1[:, s], MO[:, s], SU), a)
            v = V.chain(tt(DG[:, s], DG[:, s], TMP[:, k, :], MU))
            TB.free(k, v)
            yield
            v = V.chain(tt(DG[:, s], DG[:, s], MO[:, s], AD))
            v = V.chain(tt(DG[:, s], DG[:, s], X1[:, s], AD))

        pipe((mo2_gen(t) for t in range(NT)), 3)
        bar()
        TB = Ring(range(9))
        X2 = DG
        pipe((ln_gen(DG, X2, t, gb=[B("g22"), B("be22")]) for t in range(NT)), 4)
        bar()

        def fin2(t):
            def f(b, p):
                return V(stt(H1[:, sl(t)], PS[:, b, :], B("b22"), X2[:, sl(t)], AD, AD), p)
            return f

        pipe((ffn_gen(t, X2, lambda j: W("w21", 128 * j, 128 * j + 128), lambda j: B("b21", j, j + 1), 4, ACT.Silu,
                      lambda j: W("w22", 128 * j, 128 * j + 128), fin2(t)) for t in range(NT)), 2)
        bar()
        pipe((ln_gen(H1, H1, t, gb=[B("g23"), B("be23")]) for t in range(NT)), 4)
        bar()

        def fin2s(t):
            def f(b, p):
                v = V(stt(X[:, sl(t)], PS[:, b, :], B("bs2"), X[:, sl(t)], AD, AD), p)
                return V.chain(tt(X[:, sl(t)], X[:, sl(t)], H1[:, sl(t)], AD))
            return f

        pipe((ffn_gen(t, XN, lambda j: W("ws1", 128 * j, 128 * j + 128), lambda j: B("bs1", j, j + 1), 4,
                      ACT.Gelu_apprx_tanh, lambda j: W("ws2", 128 * j, 128 * j + 128), fin2s(t)) for t in range(NT)), 2)
        bar()
        lg, eq, sel, tmp_, pre, tot = R[0], R[1], R[2], R[3], R[4], R[5]
        logits(W("gw2"), 8, None, lg)
        softmax8(lg, 8, None)
        thr, cand, cnt, one8, need = (small(8) for _ in range(5))
        p3 = r3(lg, 8)
        V.chain(lambda e: e.memset(thr, 0.0))

        def b32(ap):
            return ap.rearrange("p (b e) -> p b e", b=1).broadcast_to((128, 32, 8))

        for bit in range(29, -1, -1):
            V.chain(ts(cand.bitcast(I32), thr.bitcast(I32), 1 << bit, None, ALU.bitwise_or))
            V.chain(tt(r3(eq, 8), p3, b32(cand), ALU.is_ge))
            V.chain(red(cnt, eq[:, 0:256].rearrange("p (b e) -> p e b", e=8)))
            p = P(mm(PS[:, 0, 0:8], K("one"), cnt), V.last())
            V.chain(ts(one8.bitcast(I32), PS[:, 0, 0:8], 512.0, None, ALU.is_ge), p)
            V.chain(lambda e: e.copy_predicated(thr, one8.bitcast(I32), cand))
        V.chain(tt(r3(sel, 8), p3, b32(thr), ALU.is_gt))
        V.chain(tt(r3(eq, 8), p3, b32(thr), ALU.is_equal))
        p = P(mms(mm(PS[:, 0, 0:256], K("lt"), eq), mm(PS[:, 0, 256:512], K("one"), eq),
                  mm(PS[:, 1, 0:256], K("one"), sel)), V.last())
        V.chain(cp(tot, PS[:, 0, 256:512]), p)
        V.chain(lambda e: e.memset(pre, 0.0))
        for k in range(1, 32):
            V.chain(tt(r3(pre, 8)[:, k, :], r3(pre, 8)[:, k - 1, :], r3(tot, 8)[:, k - 1, :], AD))
        V.chain(tt(pre, pre, PS[:, 0, 0:256], AD))
        V.chain(red(need, PS[:, 1, 0:256].rearrange("p (b e) -> p e b", e=8)))
        V.chain(ts(need, need, -1.0, 512.0, MU, AD))
        V.chain(tt(r3(pre, 8), r3(pre, 8), b32(need), ALU.is_lt))
        V.chain(tt(pre, pre, eq, MU))
        V.chain(tt(sel, sel, pre, AD))
        V.chain(tt(lg, lg, sel, MU))
        bar()
        moe(8, 4, lambda e, j: MW[:, 512 * e + 128 * j:512 * e + 128 * j + 128],
            lambda e, j: B("m2b1", 4 * e + j, 4 * e + j + 1), ACT.Gelu_apprx_tanh,
            lambda e, j: MW[:, 4096 + 512 * e + 128 * j:4096 + 512 * e + 128 * j + 128],
            lambda e: B("m2b2", e, e + 1), p3, [(s_m2, 16)])
        mw_free = bar()
        SP.dma(lambda e: e.dma_start(MW[:, :], m3), (s_m3, 16), mw_free, (s_m2, 16))

        pipe((ln_gen(X, XN, t) for t in range(NT)), 4)
        bar()
        QF, KF, VF, CF = BIG[2], BIG[3], BIG[4], BIG[5]
        pipe([g for t in range(NT) for g in (lin_gen(t, QF, W("qkv", 0, 128), XN, ACT.Identity, bias=B("bqkv", 0, 1)),
                                              lin_gen(t, KF, W("qkv", 128, 256), XN, ACT.Identity, bias=B("bqkv", 1, 2)))], 4)
        VF3 = VF[:, :].rearrange("p (b d) -> p b d", b=32)

        def v3_gen(k):
            b, w = PB.get()
            p = P(mms(*[mm(PS[:, b, 128 * j:128 * j + 128], XN[:, 128 * (k + j):128 * (k + j) + 128], W("qkv", 256, 384))
                        for j in range(4)]), w)
            yield
            v = V(tt(VF3[:, k:k + 4, :], PS[:, b, :].rearrange("p (b d) -> p b d", b=4),
                     B("bv3").rearrange("p (b d) -> p b d", b=1).broadcast_to((128, 4, 128)), AD), p)
            PB.free(b, v)

        pipe((v3_gen(4 * k) for k in range(8)), 2)
        bar()
        EN = CF
        esum = small(8)

        def en_gen(t):
            k, w = TB.get()
            a = A(act(TMP[:, k, :], QF[:, sl(t)], ACT.Square), w)
            yield
            b, w = PB.get()
            p = P(mm(PS[:, b, :], K("s8"), TMP[:, k, :]), a, w)
            TB.free(k, p)
            yield
            a = A(act(EN[:, sl(t)], PS[:, b, :], ACT.Sqrt, accum_out=esum[:, t:t + 1]), p)
            PB.free(b, a)

        pipe((en_gen(t) for t in range(NT)), 3)
        bar()
        et = small(2)
        V(red(et[:, 0:1], esum))
        p = P(mm(PS[:, 0, 0:1], K("one"), et[:, 0:1]), V.last())
        V(ts(et[:, 1:2], PS[:, 0, 0:1], 0.1 / (128.0 * T), None, MU), p)
        V.chain(ts(EN[:, :], EN[:, :], et[:, 1:2], None, ALU.is_gt))
        V.chain(tt(KF[:, :], KF[:, :], EN[:, :], MU))
        bar()
        ISQ = float(np.float32(1.0) / np.sqrt(np.float32(8.0)))
        QM = [BIG[6][:, 1024 * i:1024 * i + 1024].rearrange("p (r n) -> p r n", r=4) for i in range(2)]
        VM = [BIG[6][:, 2048 + 1024 * i:3072 + 1024 * i].rearrange("p (a r n) -> p a r n", a=2, r=4) for i in range(2)]
        PP = [BIG[7][:, 512 * i:512 * i + 512].rearrange("p (a n) -> p a n", a=2) for i in range(4)]
        PTT = [BIG[7][:, 2048 + 512 * i:2560 + 512 * i].rearrange("p (a n) -> p a n", a=2) for i in range(4)]
        setfree = [[], []]
        prg = Ring(range(4))
        ptr = Ring(range(4))
        mxr = Ring(range(8))
        mx = small(32)
        zz = small(32)

        def at_gen(n):
            i = n % 2
            c0 = n * S
            w0 = setfree[i]
            vq, gv = [], []
            for r in range(4):
                vq.append(V(ts(QM[i][:, r, :], QF[:, c0:c0 + S], K("rm", r, r + 1), None, MU), w0))
            for h in range(2):
                gv.append(G(tt(VM[i][:, h], VF3[:, 2 * n + h, :].rearrange("p (r n) -> p r n", r=1).broadcast_to((128, 4, 128)),
                               K("colr").rearrange("p (r n) -> p r n", r=4), MU), w0))
            bo, wo = PB.get()
            py = None
            for g_ in range(4):
                r32 = slice(32 * g_, 32 * g_ + 32)
                for r in range(4):
                    b, w = PB.get()
                    p = P(mms(*[mm(PS[:, b, 256 * h:256 * h + 256], QM[i][r32, r, 128 * h:128 * h + 128],
                                   KF[r32, c0:c0 + S]) for h in range(2)]), vq, w)
                    yield
                    m_, wm_ = mxr.get()
                    mm_ = mx[:, 4 * m_:4 * m_ + 2]
                    v = V(red(mm_, PS[:, b, :].rearrange("p (h n) -> p h n", h=2), MX), p, wm_)
                    v = V.chain(ts(mm_, mm_, -ISQ, None, MU))
                    yield
                    kp, wp = prg.get()
                    zt = zz[:, 4 * m_:4 * m_ + 2]
                    for h in range(2):
                        a = A(act(PP[kp][:, h, :], PS[:, b, 256 * h:256 * h + 256], ACT.Exp, scale=ISQ,
                                  bias=mm_[:, h:h + 1], accum_out=zt[:, h:h + 1]), v, wp)
                    PB.free(b, a)
                    yield
                    v = V(rcp(zt, zt), a)
                    g = G(tt(PP[kp], PP[kp], zt.rearrange("p (h n) -> p h n", n=1).broadcast_to((128, 2, 256)), MU), v)
                    mxr.free(m_, g)
                    yield
                    b, w = PB.get()
                    p = P(mms(*[tr(PS[:, b, 256 * jh + 128 * ih:256 * jh + 128 * ih + 128],
                                     PP[kp][:, ih, 128 * jh:128 * jh + 128]) for jh in range(2) for ih in range(2)]), g, w)
                    prg.free(kp, p)
                    yield
                    kt, wt = ptr.get()
                    f = PTT[kt]
                    if r % 2:
                        a = A(act(f, PS[:, b, :].rearrange("p (a n) -> p a n", a=2), ACT.Copy), p, wt)
                    else:
                        a = V(cp(f, PS[:, b, :].rearrange("p (a n) -> p a n", a=2)), p, wt)
                    PB.free(b, a)
                    yield
                    py = P(mms(*[mm(PS[r32, bo, 0:256], VM[i][:, jh, r, r32], PTT[kt][:, jh, :],
                                    start=(r == 0 and jh == 0), stop=(r == 3 and jh == 1)) for jh in range(2)]), a, gv, wo)
                    ptr.free(kt, py)
            yield
            k, w = TB.get()
            a = A(act(TMP[:, k, 0:256], PS[:, bo, 0:256], ACT.Copy), py, w)
            PB.free(bo, a)
            yield
            b, w = PB.get()
            p = P(mm(PS[:, b, 0:256], W("w3o"), TMP[:, k, 0:256]), a, w)
            TB.free(k, p)
            yield
            v = V(stt(X[:, c0:c0 + S], PS[:, b, 0:256], B("bo3"), X[:, c0:c0 + S], AD, AD), p)
            PB.free(b, v)
            setfree[i] = [v, py, p]

        pipe((at_gen(n) for n in range(NB)), 2)
        bar()
        logits(W("gw3"), 8, B("gb3"), R[0])
        softmax8(R[0], 8, None)
        m = small(32)
        p3 = r3(R[0], 8)
        V.chain(red(m, p3, MX))
        V.chain(tt(p3, p3, bc(m, 8), ALU.is_equal))
        V.chain(tt(p3, p3, K("desc").rearrange("p (b e) -> p b e", b=1).broadcast_to((128, 32, 8)), MU))
        V.chain(red(m, p3, MX))
        V.chain(tt(p3, p3, bc(m, 8), ALU.is_equal))
        bar()
        moe(8, 4, lambda e, j: MW[:, 512 * e + 128 * j:512 * e + 128 * j + 128],
            lambda e, j: B("m3b1", 4 * e + j, 4 * e + j + 1), ACT.Relu,
            lambda e, j: MW[:, 4096 + 512 * e + 128 * j:4096 + 512 * e + 128 * j + 128],
            lambda e: B("m3b2", e, e + 1), p3, [(s_m3, 16)])
        done = bar()
        s_o = sem("d_o")
        SP.dma(lambda e: e.dma_start(outT, X[:, :]), (s_o, 16), done)
        SP.items.append((lambda eng: None, [(s_o, 16)], False))

        block = ctx.enter_context(nc.Block())

        @block.sync
        def _(e):
            SP.play(e)

        @block.scalar
        def _(e):
            A.play(e)

        @block.vector
        def _(e):
            V.play(e)

        @block.gpsimd
        def _(e):
            G.play(e)

        @block.tensor
        def _(e):
            P.play(e)


def kernel(**inp):
    import concourse.bacc as bacc
    from concourse.bass_utils import run_bass_kernel_spmd as run

    f = {k: np.asarray(v) for k, v in inp.items()}

    def pad(a):
        out = np.zeros((128, a.shape[1]), np.float32)
        out[:a.shape[0]] = a
        return out

    def blocks(a):
        n = a.shape[0] // 128
        return a.reshape(n, 128, a.shape[1]).transpose(1, 0, 2).reshape(128, -1)

    def col(a):
        return a.reshape(-1, 128).T

    def row(a):
        return np.broadcast_to(a.reshape(1, -1), (128, a.size))

    L0, L1, L2, L3 = "L0_attn_", "L1_attn_", "L2_attn_", "L3_attn_"
    w = dict(
        wk=np.concatenate([f[L0 + "Wk"].T] * 2, 1), wq=np.concatenate([f[L0 + "Wq"].T] * 2, 1), wv=f[L0 + "Wv"].T,
        wout=f[L0 + "Wout"].T, f1=f["L0_ffn_W1"].T, f2=blocks(f["L0_ffn_W2"].T),
        q1=f[L1 + "qw"].T, k1=f[L1 + "kw"].T, v1=f[L1 + "vw"].T, o1=f[L1 + "ow"].T, w11=f[L1 + "w1"].T,
        w12=blocks(f[L1 + "w2"].T), gw1=f["L1_ffn_gate_w"], dw1=f["L1_ffn_dp_w1"], dw2=pad(f["L1_ffn_dp_w2"]),
        wi=f[L2 + "Wi"].T, wl1=f[L2 + "Wl1"].T, wl2=f[L2 + "Wl2"].T, memT=f[L2 + "mem_W"].T, wo2=f[L2 + "Wo"].T,
        wg=blocks(f[L2 + "Wg"].T), w21=f[L2 + "W1"].T, w22=blocks(f[L2 + "W2"].T), gw2=f["L2_ffn_gate"],
        ws1=f["L2_ffn_Ws1"], ws2=blocks(f["L2_ffn_Ws2"]), pT=f[L2 + "P"].T,
        qkv=f[L3 + "w_qkv"].T, w3o=f[L3 + "w_out"].T, gw3=f["L3_ffn_gate_w"])
    b = dict(
        nw=col(f[L0 + "norm_weight"]), eta=np.concatenate([f[L0 + "eta"]] * 2).reshape(128, 1),
        f1b=col(f["L0_ffn_b1"]), f2b=col(f["L0_ffn_b2"]),
        g1=col(f[L1 + "norm_g"]), b1n=col(f[L1 + "norm_b"]), ob1=col(f[L1 + "ob"]), fg1=col(f[L1 + "ffn_norm_g"]),
        fb1=col(f[L1 + "ffn_norm_b"]), b11=col(f[L1 + "b1"]), b12=col(f[L1 + "b2"]),
        gb1=row(f["L1_ffn_gate_b"]), db1=pad(f["L1_ffn_dp_b1"].reshape(-1, 1)), db2=row(f["L1_ffn_dp_b2"]),
        eb1=col(f["L1_ffn_eb1"].reshape(-1)), eb2=col(f["L1_ffn_eb2"].reshape(-1)),
        memb=col(f[L2 + "mem_b"]), bi=col(f[L2 + "bi"]), bl1=col(f[L2 + "bl1"]), bl2=col(f[L2 + "bl2"]),
        bo2=col(f[L2 + "bo"]), fgate=row(f[L2 + "fgate"]), lrate=row(f[L2 + "lrate"]), bg=col(f[L2 + "bg"]),
        b21=col(f[L2 + "b1"]), b22=col(f[L2 + "b2"]), g21=col(f[L2 + "g1"]), be21=col(f[L2 + "be1"]),
        g22=col(f[L2 + "g2"]), be22=col(f[L2 + "be2"]), g23=col(f[L2 + "g3"]), be23=col(f[L2 + "be3"]),
        m2b1=col(f["L2_ffn_b1"].reshape(-1)), m2b2=col(f["L2_ffn_b2"].reshape(-1)), bs1=col(f["L2_ffn_bs1"]),
        bs2=col(f["L2_ffn_bs2"]),
        bqkv=col(f[L3 + "b_qkv"]), bo3=col(f[L3 + "b_out"]), m3b1=col(f["L3_ffn_b1"].reshape(-1)),
        m3b2=col(f["L3_ffn_b2"].reshape(-1)), gb3=row(f["L3_ffn_gate_b"]), bv3=row(f[L3 + "b_qkv"][256:384]))

    def moe(w1, w2):
        e = w1.shape[0]
        return np.concatenate([w1.transpose(1, 0, 2).reshape(128, -1),
                               w2.reshape(e, -1, 128, 128).transpose(2, 0, 1, 3).reshape(128, -1)], 1)

    c = constants()
    arrays = {
        "xT": f["L0_attn_x"].reshape(NB, NC, C, 128).transpose(3, 1, 0, 2).reshape(128, T),
        "early": np.concatenate([w[n] for n, _ in EARLY] + [c[n] for n, _ in ECONSTS], 1),
        "wts": np.concatenate([w[n] for n, _ in WEIGHTS], 1),
        "bia": np.concatenate([b[n] for n, _ in BIASES], 1),
        "con": np.concatenate([c[n] for n, _ in CONSTS], 1),
        "m1": moe(f["L1_ffn_ew1"], f["L1_ffn_ew2"]),
        "m2": moe(f["L2_ffn_W1"], f["L2_ffn_W2"]),
        "m3": moe(f["L3_ffn_w1"], f["L3_ffn_w2"]),
    }
    arrays = {k: np.ascontiguousarray(v, dtype=np.float32) for k, v in arrays.items()}
    nc = bacc.Bacc("TRN2", target_bir_lowering=False, num_devices=1)
    args = [nc.dram_tensor(k, v.shape, F32, kind="ExternalInput").ap() for k, v in arrays.items()]
    args.append(nc.dram_tensor("outT", (128, T), F32, kind="ExternalOutput").ap())
    program(nc, *args)
    r = run(nc, [arrays], core_ids=[0])
    return np.ascontiguousarray(r.results[0]["outT"].T).reshape(NB, S, 128)
```

```python
from contextlib import ExitStack

import numpy as np
import concourse.bass as bass
from concourse import mybir

ALU = mybir.AluOpType
ACT = mybir.ActivationFunctionType
F32 = mybir.dt.float32
I32 = mybir.dt.int32
BF16 = mybir.dt.bfloat16
AX = mybir.AxisListType.X

T = 4096
NB, S = 16, 256
TW = 512
NT = T // TW
C = 8
NC = S // C

EARLY = [
    ("wk", 128), ("wq", 128), ("wv", 128), ("wout", 128), ("f1", 512), ("f2", 512),
    ("q1", 128), ("k1", 128), ("v1", 128), ("o1", 128), ("w11", 256), ("w12", 256),
    ("gw1", 4), ("dw1", 64), ("dw2", 1),
]
WEIGHTS = [
    ("wi", 128), ("wl1", 128), ("wl2", 128), ("memT", 128), ("wo2", 128), ("wg", 256),
    ("w21", 512), ("w22", 512), ("gw2", 8), ("ws1", 512), ("ws2", 512), ("pT", 10),
    ("qkv", 384), ("w3o", 128), ("gw3", 8),
]
BIASES = [
    ("nw", 1), ("eta", 1), ("f1b", 4), ("f2b", 1),
    ("g1", 1), ("b1n", 1), ("ob1", 1), ("fg1", 1), ("fb1", 1), ("b11", 2), ("b12", 1),
    ("gb1", 4), ("db1", 1), ("db2", 1), ("eb1", 8), ("eb2", 4),
    ("memb", 1), ("bi", 1), ("bl1", 1), ("bl2", 1), ("bo2", 1), ("fgate", 1), ("lrate", 1), ("bg", 1),
    ("b21", 4), ("b22", 1), ("g21", 1), ("be21", 1), ("g22", 1), ("be22", 1), ("g23", 1), ("be23", 1),
    ("m2b1", 32), ("m2b2", 8), ("bs1", 4), ("bs2", 1),
    ("bqkv", 3), ("bo3", 1), ("m3b1", 32), ("m3b2", 8), ("gb3", 8), ("bv3", 128),
]
CONSTS = [
    ("ident", 128), ("one", 128), ("mean", 128), ("blk", 128), ("hid", 16),
    ("oneh", 8), ("g8", 128), ("s8", 128), ("tri", 128), ("bd8", 128),
    ("rm", 4), ("lt", 128), ("band", 160), ("band0", 128), ("eps5", 1), ("eps6", 1), ("zero", 1),
    ("rselA", 128), ("pairm", 8), ("pairm2", 8), ("desc", 8), ("pm", 1), ("colr", 512), ("par", 128), ("i32", 32), ("pcol", 1), ("blkid", 32),
]
ECONSTS = [("sel", 1024), ("dq", 256), ("dk", 256)]


def offsets(table):
    at, n = {}, 0
    for name, w in table:
        at[name] = (n, w)
        n += w
    return at, n


WAT, NW = offsets(WEIGHTS)
EAT, NE = offsets(EARLY + ECONSTS)
BAT, NBI = offsets(BIASES)
CAT, NCO = offsets(CONSTS)


def constants():
    p = np.arange(128)
    c = {}
    c["ident"] = np.eye(128)
    c["one"] = np.ones((128, 128))
    c["mean"] = np.full((128, 128), 1.0 / 128)
    c["blk"] = (p[:, None] // C == p[None, :] // C)
    c["sel"] = np.concatenate([(p[:, None] == (p[None, :] // C) * C + s) for s in range(C)], 1)
    c["hid"] = (p[:, None] // C == np.arange(16)[None, :])
    c["oneh"] = (p[:, None] % C == np.arange(C)[None, :])
    c["g8"] = (p[:, None] // 8 == p[None, :] // 8) / 8.0
    c["s8"] = (p[:, None] // 8 == p[None, :] // 8)
    gam = 1.0 - np.exp(np.linspace(np.log(1 / 32.0), np.log(1 / 512.0), 16)).astype(np.float32).astype(np.float64)
    g = gam[p // 8][:, None]
    t = np.arange(256)[None, :]
    c["dq"] = g ** (t - 128.0)
    c["dk"] = g ** (128.0 - t) / np.sqrt(8.0)
    c["tri"] = (p[None, :] >= p[:, None])
    c["bd8"] = (p[:, None] // 8 == p[None, :] // 8)
    c["rm"] = ((p[:, None] % 32) // 8 == np.arange(4)[None, :])
    c["lt"] = (p[:, None] < p[None, :])
    q, k = p[:, None], np.arange(160)[None, :] - 32
    c["band"] = np.where((k <= q) & (k >= q - 16), 0.0, -1e30)
    k = np.arange(128)[None, :]
    c["band0"] = np.where((k <= q) & (k >= q - 16), 0.0, -1e30)
    c["eps5"] = np.full((128, 1), 1e-5)
    c["eps6"] = np.full((128, 1), 1e-6)
    c["zero"] = np.zeros((128, 1))
    c["rselA"] = ((p[:, None] // C) % 2 == p[None, :] // 64) & (p[:, None] % C == 0)
    c["pairm"] = (p[:, None] // 16 == np.arange(8)[None, :])
    c["pairm2"] = np.zeros((128, 8))
    c["desc"] = np.tile(8.0 - np.arange(8), (128, 1))
    c["par"] = (p[:, None] // 64 == (p[None, :] // C) % 2)
    c["i32"] = np.tile(np.arange(32)[None, :], (128, 1))
    c["blkid"] = c["i32"]
    c["pcol"] = p[:, None]
    c["pm"] = np.zeros((128, 1))
    c["colr"] = np.tile(np.concatenate([(p // 8) % 4 == r for r in range(4)])[None, :], (128, 1))
    c["colr"] = np.tile(c["colr"], 1)
    return {n: np.asarray(a, np.float32) for n, a in c.items()}


class Eng:

    def __init__(self, sem):
        self.sem, self.n, self.items = sem, 0, []

    def __call__(self, fn, *waits):
        self.items.append((fn, flat(waits), True))
        self.n += 1
        return (self.sem, self.n)

    def chain(self, fn, *waits):
        return self(fn, (self.sem, self.n), *waits)

    def last(self):
        return (self.sem, self.n)

    def dma(self, fn, tok, *waits):
        self.items.append((lambda e: fn(e).then_inc(tok[0], 16), flat(waits), False))

    def play(self, eng):
        seen = {}
        for fn, waits, counted in self.items:
            for sem, v in waits:
                if v > seen.get(id(sem), 0):
                    eng.wait_ge(sem, v)
                    seen[id(sem)] = v
            r = fn(eng)
            if counted:
                r.then_inc(self.sem, 1)


def flat(waits):
    out = []
    for w in waits:
        if isinstance(w, list):
            out += flat(w)
        elif w is not None:
            out.append(w)
    return out


class Ring:

    def __init__(self, ids):
        self.idle = [(k, []) for k in ids]
        self.n = len(self.idle)

    def get(self):
        return self.idle.pop(0)

    def free(self, k, *toks):
        self.idle.append((k, list(toks)))

    def reset(self):
        assert len(self.idle) == self.n
        self.idle = [(k, []) for k, _ in sorted(self.idle)]


def pipe(gens, depth):
    gens = iter(gens)
    live = []
    while True:
        if len(live) < depth:
            g = next(gens, None)
            if g is not None:
                live.append(g)
        if not live:
            return
        for g in list(live):
            if next(g, 1) is not None:
                live.remove(g)


def program(nc, xT, early, wts, bia, con, m1, m2, m3, outT):
    with ExitStack() as ctx:
        def sb(name, shape, dt=F32):
            return ctx.enter_context(nc.sbuf_tensor(name, shape, dt))

        def sem(name):
            return ctx.enter_context(nc.semaphore(name))

        A, V, G, P, SP = (Eng(sem("s_" + n)) for n in ("act", "dve", "pool", "pe", "sp"))
        BIG = [sb(f"big{i}", [128, T]) for i in range(8)]
        WT = sb("wt", [128, NW])
        BI = sb("bi", [128, NBI])
        CO = sb("co", [128, NCO])
        MW = sb("mw", [128, 8192])
        TMP = sb("tmp", [128, 9, TW])
        SM = sb("sm", [128, 1100])
        PS = ctx.enter_context(nc.psum_tensor("ps", [128, 8, 512], F32))

        def W(n, a=0, b=None):
            if n in EAT:
                o, w = EAT[n]
                return MW[:, 2048 + o + a:2048 + o + (w if b is None else b)]
            o, w = WAT[n]
            return WT[:, o + a:o + (w if b is None else b)]

        def B(n, a=0, b=None):
            o, w = BAT[n]
            return BI[:, o + a:o + (w if b is None else b)]

        def K(n, a=0, b=None):
            if n in EAT:
                return W(n, a, b)
            o, w = CAT[n]
            return CO[:, o + a:o + (w if b is None else b)]

        smat = [0]

        def small(n):
            a = smat[0]
            smat[0] += n
            assert smat[0] <= 1100
            return SM[:, a:a + n]

        PB = Ring(range(8))
        TB = Ring(range(9))
        RST = small(32)
        RR = Ring(range(8))

        def mm(out, lhsT, rhs, start=True, stop=True):
            return lambda e: e.matmul(out, lhsT, rhs, start=start, stop=stop)

        def mms(*fs):
            def go(e):
                for f in fs:
                    r = f(e)
                return r
            return go

        def act(out, in_, f, scale=1.0, bias=None, **kw):
            if f == ACT.Copy:
                return lambda e: e.activation(out, in_, f, scale=scale, **kw)
            return lambda e: e.activation(out, in_, f, bias=K("zero")[0:out.shape[0], :] if bias is None else bias,
                                          scale=scale, **kw)

        def tt(out, a, b, op):
            return lambda e: e.tensor_tensor(out, a, b, op)

        def ts(out, a, s1, s2, op0, op1=None):
            if op1 is None:
                return lambda e: e.tensor_scalar(out, a, s1, None, op0)
            return lambda e: e.tensor_scalar(out, a, s1, s2, op0, op1)

        def stt(out, a, s, b, op0, op1):
            return lambda e: e.scalar_tensor_tensor(out=out, in0=a, scalar=s, in1=b, op0=op0, op1=op1)

        def ttr(out, a, b, acc):
            return lambda e: e.tensor_tensor_reduce(out, a, b, 1.0, 0.0, ALU.mult, ALU.add, acc)

        def red(out, a, op=ALU.add):
            return lambda e: e.tensor_reduce(out, a, AX, op)

        def rcp(out, a):
            return lambda e: e.reciprocal(out, a)

        def tr(out, a):
            n = a.shape[0]
            return lambda e: e.transpose(out, a, K("ident")[0:n, 0:n])

        def cp(out, a):
            return lambda e: e.tensor_copy(out, a)

        MU, AD, SU, MX, MN = ALU.mult, ALU.add, ALU.subtract, ALU.max, ALU.min

        def bar():
            toks = [e.last() for e in (A, V, G, P)]
            for e in (A, V, G, P):
                e.items.append((lambda eng: None, toks, False))
            for r in (PB, TB, RR):
                r.reset()
            return toks

        def sl(t):
            return slice(t * TW, (t + 1) * TW)

        s_x, s_w, s_c, s_m1, s_m2, s_m3 = (sem(n) for n in ("d_x", "d_w", "d_c", "d_m1", "d_m2", "d_m3"))
        X = BIG[1]
        SP.dma(lambda e: e.dma_start(BIG[1][:, :], xT), (s_x, 16))
        SP.dma(lambda e: e.dma_start(CO[:, :], con), (s_c, 16))
        SP.dma(lambda e: e.dma_start(BI[:, :], bia), (s_c, 32))
        SP.dma(lambda e: e.dma_start(MW[:, 2048:2048 + NE], early), (s_c, 48))
        SP.dma(lambda e: e.dma_start(WT[:, :], wts), (s_w, 16))
        SP.dma(lambda e: e.dma_start(MW[:, 0:2048], m1), (s_m1, 16))
        for e in (A, V, G, P):
            e.items.append((lambda eng: None, [(s_x, 16), (s_c, 48), (s_w, 16)], False))

        def rstd_gen(sq, k, eps, mean, res, floor=None, n=TW):
            nb = (n + 127) // 128
            m = min(n, 128)
            b, w = PB.get()
            p = P(mms(*[mm(PS[0:m, b, j:j + 1], TMP[:, k, 128 * j:128 * j + m], K("mean" if mean else "one", 0, 1))
                        for j in range(nb)]), sq, w)
            yield
            kr, w = RR.get()
            r = RST[0:m, 4 * kr:4 * kr + nb]
            a = A(act(r, PS[0:m, b, 0:nb], ACT.Sqrt, bias=None if eps is None else eps[0:m]), p, w)
            yield
            v = V(ts(r, r, floor or 0.0, None, MX), a)
            v = V.chain(rcp(r, r))
            yield
            p = P(mms(*[mm(PS[:, b, 128 * j:128 * j + m], r[:, j:j + 1].broadcast_to((m, 128)), K("ident")[0:m, 0:m])
                        for j in range(nb)]), v)
            RR.free(kr, p)
            TB.free(k, p)
            yield
            res.append((b, p))

        def ln_gen(src, dst, t, eps=None, gb=None, rms=False, wait=()):
            s = sl(t)
            if not rms:
                b, w = PB.get()
                p = P(mm(PS[:, b, :], K("mean"), src[:, s]), w, *wait)
                yield
                v = V(tt(dst[:, s], src[:, s], PS[:, b, :], SU), p)
                PB.free(b, v)
                x = dst
            else:
                v = None
                x = src
            yield
            k, w = TB.get()
            a = A(act(TMP[:, k, :], x[:, s], ACT.Square), v, w, *wait)
            yield
            res = []
            yield from rstd_gen(a, k, K("eps5") if eps is None else eps, True, res)
            b, p = res[0]
            if gb is None:
                v = V(tt(dst[:, s], x[:, s], PS[:, b, :], MU), p, v)
            else:
                v = V(stt(dst[:, s], x[:, s], gb[0], PS[:, b, :], MU, MU), p, v)
            PB.free(b, v)
            if gb is not None and len(gb) == 2:
                yield
                A(act(dst[:, s], dst[:, s], ACT.Identity, bias=gb[1]), v)

        def lin_gen(t, dst, w, src, f, bias=None, scale=1.0):
            b, wt = PB.get()
            p = P(mm(PS[:, b, :], w, src[:, sl(t)]), wt)
            yield
            a = A(act(dst[:, sl(t)], PS[:, b, :], f, bias=bias, scale=scale), p)
            PB.free(b, a)

        def ffn_gen(t, src, w1, b1, nh, func, w2, fin):
            bo, wo = PB.get()
            hs = []
            for j in range(nh):
                b, w = PB.get()
                p = P(mm(PS[:, b, :], w1(j), src[:, sl(t)]), w)
                yield
                k, w = TB.get()
                a = A(act(TMP[:, k, :], PS[:, b, :], func, bias=b1(j)), p, w)
                PB.free(b, a)
                hs.append((j, k, a))
                if len(hs) == 2:
                    jj, kk, aa = hs.pop(0)
                    p = P(mm(PS[:, bo, :], w2(jj), TMP[:, kk, :], start=(jj == 0), stop=False), aa, wo)
                    TB.free(kk, p)
            jj, kk, aa = hs.pop(0)
            p = P(mm(PS[:, bo, :], w2(jj), TMP[:, kk, :], start=(jj == 0), stop=True), aa, wo)
            TB.free(kk, p)
            yield
            tok = fin(bo, p)
            PB.free(bo, tok)

        VT, X, XN, XR, KB, EK, Q, U8 = BIG
        pipe((ln_gen(X, XN, t) for t in range(NT)), 4)
        bar()
        pipe((ln_gen(XN, XR, t, eps=K("eps6"), gb=[B("nw")], rms=True) for t in range(NT)), 4)
        etac = small(1)
        V(ts(etac, B("eta"), -1.0, None, MU))
        V.chain(tt(etac, etac, B("eta"), MX))
        V.chain(ts(etac, etac, 1e-6, None, MX))
        bar()

        def phi_gen(t, dst, w, edst=None):
            b, wt = PB.get()
            p = P(mm(PS[:, b, :], w, XR[:, sl(t)]), wt)
            yield
            k, w_ = TB.get()
            v = V(ts(TMP[:, k, :], PS[:, b, :], 0.0, None, MN), p, w_)
            yield
            a = A(act(TMP[:, k, :], TMP[:, k, :], ACT.Exp), v)
            yield
            v = V(stt(dst[:, sl(t)], PS[:, b, :], 0.0, TMP[:, k, :], MX, AD), a)
            PB.free(b, v)
            TB.free(k, v)
            if edst is not None:
                V.chain(ts(edst[:, sl(t)], dst[:, sl(t)], etac, None, MU))

        pipe([g for t in range(NT) for g in (phi_gen(t, KB, W("wk"), EK), phi_gen(t, Q, W("wq")),
                                              lin_gen(t, VT, W("wv"), XR, ACT.Copy))], 4)

        qs = small(8)
        q2 = TMP[:, 8, :]
        for n, j in (("f1", 0), ("f2", 1)):
            V.chain(ts(q2, W(n), -1.0, None, MU))
            V.chain(tt(q2, q2, W(n), MX))
            V.chain(red(qs[:, j:j + 1], q2))
        bar()
        b, w = PB.get()
        p = P(mm(PS[:, b, 0:2], K("one"), qs[:, 0:2]))
        PB.free(b)
        V(ts(qs[:, 2:4], PS[:, b, 0:2], 1.0 / 65536, 1e-5, MU, AD), p)
        V.chain(rcp(qs[:, 4:6], qs[:, 2:4]))
        RND = 12582912.0
        for n, j in (("f1", 0), ("f2", 1)):
            V.chain(ts(W(n), W(n), qs[:, 4 + j:5 + j], None, MU))
            V.chain(ts(W(n), W(n), 1.5, -1.5, MN, MX))
            V.chain(ts(W(n), W(n), RND, None, AD))
            V.chain(ts(W(n), W(n), -RND, None, AD))
            V.chain(ts(W(n), W(n), 1.0, -1.0, MN, MX))
        bar()

        def fin0(t):
            def f(b, p):
                V(stt(X[:, sl(t)], PS[:, b, :], B("f2b"), X[:, sl(t)], AD, AD), p)
                return V.chain(tt(X[:, sl(t)], X[:, sl(t)], XN[:, sl(t)], AD))
            return f

        pipe((ffn_gen(t, XN, lambda j: W("f1", 128 * j, 128 * j + 128), lambda j: B("f1b", j, j + 1), 4, ACT.Relu,
                      lambda j: W("f2", 128 * j, 128 * j + 128), fin0(t)) for t in range(NT)), 2)
        bar()

        def cv(buf, c, r=slice(0, 128)):
            return buf[r, 128 * c:128 * c + 128]

        U = BIG[7]
        Mst = U[:, 0:1024].rearrange("p (a d) -> p a d", a=8)
        Mun = U[:, 1024:2048].rearrange("p (a d) -> p a d", a=8)
        EKBL = U[:, 2048:3072].rearrange("p (a h f) -> p a h f", a=8, h=2)
        RT = [U[:, 3072:3776].rearrange("p (j x) -> p j x", j=8), TMP[:, 0:2, :].rearrange("p a n -> p (a n)")[:, 0:704]
              .rearrange("p (j x) -> p j x", j=8)]
        EXP = TMP[:, 2:4, :].rearrange("p a n -> p (a n)")[:, 0:704].rearrange("p (j x) -> p j x", j=8)
        vch = [TMP[:, 4, 0:128], TMP[:, 4, 128:256]]
        vw = TMP[:, 4, 256:384]
        sqp = TMP[:, 4, 384:512]
        pT = TMP[:, 5, 0:256].rearrange("p (k n) -> p k n", k=2)
        mk = TMP[:, 5, 256:384]
        mk2 = TMP[:, 5, 384:512]
        SC = [TMP[:, 6 + i, :] for i in range(2)]
        grm = TMP[:, 8, 0:384]
        q64 = TMP[:, 8, 384:448]
        q64b = TMP[:, 8, 448:512]

        KEM = [XN[:, 256 * i:256 * i + 256].rearrange("p (k n) -> p k n", k=2) for i in range(2)]

        def sv(i):
            o = SC[i]
            return dict(ek=o[:, 0:64], kap=o[:, 64:65], eb=o[:, 65:66], vs=o[:, 66:67], c=o[:, 67:68],
                        G=o[:, 68:92], e1=o[:, 92:172], rep=o[:, 172:252], B=o[:, 252:260], F=o[:, 260:268],
                        x=o[:, 268:356], t8=o[:, 356:364], kapn=o[:, 364:365], nB=o[:, 365:373],
                        K3=o[:, 373:400], C2=o[:, 400:424], d8=o[:, 424:432], u8=o[:, 432:440])

        st = small(64)
        Pst, qst, rP, mst, rR, wc = (st[:, i:i + 1] for i in range(6))
        Xv, Yv, zz1 = st[:, 6:9], st[:, 9:12], st[:, 12:13]
        C1v, C0v, Av = st[:, 13:16], st[:, 16:19], st[:, 19:20]
        tmp8, al = st[:, 20:28], st[:, 28:36]
        km, sg, al0, g0, b0 = (st[:, i:i + 1] for i in range(36, 41))
        pv, L8 = st[:, 41:49], st[:, 49:57]
        x11 = small(11)
        ex11 = small(88)
        dt = small(88)
        dt3 = dt.rearrange("p (j x) -> p j x", x=11)
        rp8 = small(8)
        Rc = small(8)
        Wst = small(8)
        sg3 = small(3)
        one8_ = K("oneh")
        V(lambda e: e.memset(Mst, 0.0))
        V(lambda e: e.memset(st, 0.0))
        V.chain(lambda e: e.memset(Pst, 1.0))
        V.chain(lambda e: e.memset(rR, 1.0))
        V(lambda e: e.memset(sg3[:, 0:1], 0.0))
        V(lambda e: e.memset(sg3[:, 1:2], 1.0))
        V(lambda e: e.memset(sg3[:, 2:3], -1.0))
        bar()

        def outer(a, n, b, m):
            return (a.rearrange("p (x y) -> p x y", y=1).broadcast_to((128, n, m)),
                    b.rearrange("p (x y) -> p x y", x=1).broadcast_to((128, n, m)))

        def prep(c):
            i = c % 2
            s = sv(i)
            lo = slice(0, 64)
            old = prep.old.get(i, [])
            p1 = P(mm(PS[:, 0, 0:128], cv(KB, c, lo), cv(EK, c, lo)), prep.b[0])
            yield
            P(mm(PS[:, 0, 128:256], cv(EK, c, lo), cv(EK, c, lo)))
            p1 = P(mm(PS[:, 0, 256:384], cv(VT, c), cv(VT, c)))
            yield
            p2 = P(mms(mm(PS[:, 1, 0:128], cv(XR, c), W("wv")),
                       mm(PS[:, 1, 128:192], cv(EK, c, lo), K("ident")[0:64, 0:64]),
                       mm(PS[:, 1, 192:193], cv(KB, c, lo), K("one")[0:64, 0:1]),
                       mm(PS[:, 1, 193:194], cv(EK, c, lo), K("mean")[0:64, 0:1]),
                       mm(PS[:, 1, 194:195], cv(VT, c), K("one")[:, 0:1])), prep.b[1])
            yield
            vv = V(tt(grm.rearrange("p (k b s) -> p k b s", k=3, b=NB),
                      PS[:, 0, 0:384].rearrange("p (k b s) -> p k b s", k=3, b=NB),
                      K("hid").rearrange("p (k b s) -> p k b s", k=1, s=1).broadcast_to((128, 3, NB, C)), MU), p1)
            prep.b[0] = [vv]
            yield
            for k_, buf in ((0, KB), (1, EK)):
                G.chain(tt(KEM[i][:, k_, :], cv(buf, c), K("par"), MU), old)
            yield
            a1 = A(act(vch[i], PS[:, 1, 0:128], ACT.Copy), p2, old)
            yield
            a2 = A(act(SC[i][:, 0:67], PS[:, 1, 128:195], ACT.Copy), p2, old)
            prep.b[1] = [a2]
            yield
            v = V(red(s["G"].rearrange("p (k s) -> p k s", k=3),
                      grm.rearrange("p (k b s) -> p k s b", k=3, b=NB)), vv, old)
            gk, gg, gv = s["G"][:, 0:8], s["G"][:, 8:16], s["G"][:, 16:24]
            g = G(tt(s["c"], s["eb"], s["vs"], MU), a2)
            g = G.chain(ts(s["c"], s["c"], 2.0 / 128, None, MU))
            g = G.chain(ts(s["kapn"], s["kap"], -1.0, None, MU))
            g = G.chain(ts(s["e1"][:, 0:8], one8_, s["c"], None, MU))
            g = G.chain(ts(s["e1"][:, 8:16], one8_, s["vs"], None, MU))
            yield
            g = G.chain(tt(s["e1"][:, 16:80].rearrange("p (x y) -> p x y", x=8), *outer(one8_, 8, gv, 8), MU), v)
            p = P(mm(PS[:, 1, 256:336], K("blk"), s["e1"]), g, a2)
            yield
            a = A(act(s["rep"], PS[:, 1, 256:336], ACT.Copy), p)
            prep.b[1] = [a]
            yield
            crep, vrep, vvr = s["rep"][:, 0:8], s["rep"][:, 8:16], s["rep"][:, 16:80]
            g = G.chain(ts(s["B"], crep, s["kap"], None, MU), a)
            g = G.chain(ts(s["nB"], s["B"], -1.0, None, MU))
            g = G.chain(tt(s["F"], gk, vrep, MU))
            g = G.chain(ts(s["t8"], s["B"], -64.0, None, MU))
            g = G.chain(tt(s["F"], s["F"], s["t8"], AD))
            yield
            x2 = lambda ap: ap.rearrange("p (x y) -> p x y", x=8)
            xq, xn, xb, xc = s["x"][:, 0:64], s["x"][:, 64:72], s["x"][:, 72:80], s["x"][:, 80:88]
            g = G.chain(tt(x2(q64), *outer(gk, 8, gk, 8), MU))
            g = G.chain(tt(q64, q64, vvr, MU))
            g = G.chain(tt(x2(q64b), *outer(s["F"], 8, s["nB"], 8), MU))
            g = G.chain(tt(q64, q64, q64b, AD))
            yield
            g = G.chain(tt(x2(q64b), *outer(s["nB"], 8, s["F"], 8), MU))
            g = G.chain(tt(q64, q64, q64b, AD))
            g = G.chain(ts(xq, q64, 2.0, None, MU))
            g = G.chain(lambda e: e.tensor_copy(xn, q64[:, 0:64:9]))
            yield
            g = G.chain(tt(s["t8"], gk, gv, MU))
            g = G.chain(ts(xb, s["nB"], s["vs"], None, MU))
            g = G.chain(tt(xb, xb, s["t8"], AD))
            g = G.chain(ts(xb, xb, -2.0, None, MU))
            g = G.chain(tt(s["t8"], gg, gv, MU))
            g = G.chain(ts(s["t8"], s["t8"], 2.0 / 8192, None, MU))
            g = G.chain(ts(xc, crep, s["c"], None, MU))
            g = G.chain(ts(xc, xc, -2.0, None, MU))
            g = G.chain(tt(xc, xc, s["t8"], AD))
            yield
            g = G.chain(tt(EXP, *outer(one8_, 8, s["x"], 88), MU), prep.b[2])
            yield
            e_ = EXP.rearrange("p j x -> p (j x)")
            p = None
            for h in range(2):
                p = P(mm(PS[:, 2 + h, 0:352], K("blk"), e_[:, 352 * h:352 * h + 352]), g)
            yield
            for h in range(4):
                a = A(act(RT[i].rearrange("p j x -> p (j x)")[:, 176 * h:176 * h + 176],
                          PS[:, 2 + h // 2, 176 * (h % 2):176 * (h % 2) + 176], ACT.Copy), p, old)
                yield
            prep.b[2] = [p, a]
            K3 = s["K3"].rearrange("p (t x) -> p t x", x=3)
            C2 = s["C2"].rearrange("p (t x) -> p t x", x=3)
            g = G.chain(lambda e: e.tensor_copy(K3[:, 0:8, 0], K("one")[:, 0:8]))
            g = G.chain(lambda e: e.tensor_copy(K3[:, 0:7, 1], vvr[:, 9:64:9]))
            g = G.chain(ts(K3[:, 0:7, 2], vvr[:, 9:64:9], -1.0, None, MU))
            rf = RT[i].rearrange("p j x -> p (j x)")
            g = G.chain(ts(s["d8"], rf[:, 80:704:89], 0.5, None, MU), a)
            yield
            g = G.chain(lambda e: e.tensor_copy(s["u8"][:, 0:7], rf[:, 88 + 64:704:89]))
            g = G.chain(tt(C2[:, 0:7, :], K3[:, 0:7, :],
                           s["d8"][:, 0:7].rearrange("p (t x) -> p t x", x=1).broadcast_to((128, 7, 3)), MU))
            g = G.chain(tt(C2[:, 0:7, 1], C2[:, 0:7, 1], s["u8"][:, 0:7], AD))
            g = G.chain(tt(C2[:, 0:7, 2], C2[:, 0:7, 2], s["u8"][:, 0:7], SU))
            g = G.chain(lambda e: e.tensor_copy(C2[:, 7, 0:1], s["d8"][:, 7:8]))
            prep.ready[c] = [g, a, v]

        prep.old = {}
        prep.b = {0: [], 1: [], 2: []}
        prep.ready = {}
        for _ in prep(0):
            pass
        mtok = []
        gM = None
        P_, q_ = Pst, qst
        for c in range(NC):
            i = c % 2
            s = sv(i)
            ahead = prep(c + 1) if c + 1 < NC else iter(())
            rdy = prep.ready[c]
            crep, vrep, vvr = s["rep"][:, 0:8], s["rep"][:, 8:16], s["rep"][:, 16:80]
            K3 = s["K3"].rearrange("p (t x) -> p t x", x=3)
            C2 = s["C2"].rearrange("p (t x) -> p t x", x=3)
            ps4 = PS[:, 4, 0:256].rearrange("p (k n) -> p k n", k=2)
            msrc = Mst if c == 0 else Mun
            for half in range(2):
                p = P(mms(*[mm(ps4[:, :, 16 * a_:16 * a_ + 16], msrc[:, a_, :], KEM[i][:, :, 16 * a_:16 * a_ + 16])
                            for a_ in range(4 * half, 4 * half + 4)]), mtok[half:half + 1], rdy)
            a = A(act(pT, ps4, ACT.Copy), p)
            p1 = P(mms(mm(PS[:, 6, 0:128], pT[:, 0, :], cv(VT, c)), mm(PS[:, 6, 256:257], pT[:, 0, :], K("one")[:, 0:1])), a)
            a = A(act(sqp, pT[:, 0, :], ACT.Square), a)
            p2 = P(mm(PS[:, 6, 128:256], pT[:, 1, :], cv(VT, c)))
            p3 = P(mm(PS[:, 7, 0:1], sqp, K("one")[:, 0:1]), a)
            p1 = p2
            v = V(tt(km, mst, s["kap"], MU), rdy, V.last())
            v = V(tt(mk.rearrange("p (b s) -> p b s", b=NB), PS[:, 6, 0:128].rearrange("p (b s) -> p b s", b=NB),
                     K("hid").rearrange("p (b s) -> p b s", s=1).broadcast_to((128, NB, C)), MU), p1)
            vk = V.chain(red(pv, mk.rearrange("p (b s) -> p s b", b=NB)))
            vg = V(ttr(mk2, PS[:, 6, 128:256], K("ident"), g0), p2)
            v = V(ts(tmp8, vrep, km, None, MU), vk)
            va = V(ts(al0, PS[:, 6, 256:257], -2.0, None, MU), p1)
            v = V(tt(pv, pv, tmp8, SU), v)
            va = V(stt(al0, km, 128.0, al0, MU, AD), va)
            vs_ = V(stt(sg, km, -128.0, PS[:, 6, 256:257], MU, AD), p1)
            vL = V(tt(L8, s["G"][:, 0:8], pv, MU), v)
            va = V(stt(al0, al0, km, PS[:, 7, 0:1], MU, AD), va, p3)
            vb = V(ttr(tmp8, pv, one8_, b0), vL)
            vL = V(stt(L8, s["nB"], sg, L8, MU, AD), vs_, vL)
            vg = V(ts(g0, g0, 1.0 / 8192, None, MU), vg)
            vx = V(ts(x11[:, 0:8], L8, 2.0, None, MU), vL)
            v = V(tt(wc, s["c"], mst, MU), rdy)
            va = V(ts(x11[:, 8:9], al0, rR, None, MU), va)
            vb = V(ts(x11[:, 9:10], b0, -2.0, None, MU), vb)
            vg = V(tt(g0, g0, wc, SU), v, vg)
            v = V(ts(mst, mst, rR, None, MU), vg)
            vg = V(ts(x11[:, 10:11], g0, 2.0, None, MU), vg)
            v = V(ts(x11, x11, rR, None, MU), vx, va, vb, vg)
            v = V.chain(tt(ex11.rearrange("p (x y) -> p x y", x=8), *outer(one8_, 8, x11, 11), MU))
            p = P(mm(PS[:, 7, 16:104], K("blk"), ex11), v)
            v = V(cp(dt, PS[:, 7, 16:104]), p)
            vF = V(tt(Yv[:, 1:2], dt[:, 8:9], vvr[:, 0:1], AD), v)
            vA = V(ts(Av, qst, 1e-5, None, AD))
            vC = V(ts(C1v, K3[:, 0, :], dt3[:, 0, 10:11], None, MU), v)
            vN = V(ts(Yv[:, 2:3], Yv[:, 1:2], -1.0, None, MU), vF)
            vD = V(ts(C0v, K3[:, 0, :], Av, None, MU), vA)
            vC = V(stt(C1v, sg3, dt3[:, 1, 0:1], C1v, MU, AD), vC)
            vz = V(tt(zz1, dt3[:, 0, 9:10], Yv[:, 2:3], MX), vN)
            vD = V(stt(C0v, sg3, dt3[:, 1, 8:9], C0v, MU, AD), vD)
            aw = A(act(Wst[:, 0:1], zz1, ACT.Sqrt, bias=Yv[:, 1:2]), vz)
            if c:
                v = V(ts(rp8, K("pairm"), rR, None, MU), gM)
                pr = P(mm(PS[:, 5, 256:264], K("rselA"), rp8), v)
                v = V(cp(Rc, PS[:, 5, 256:264]), pr)
                gM = G(tt(Mst, Mun, Rc.rearrange("p (a d) -> p a d", d=1).broadcast_to((128, 8, 128)), MU), v, p)
            gE = G(tt(EKBL.rearrange("p a h f -> p (a h) f"),
                      s["ek"].rearrange("p (a f) -> p a f", a=1).broadcast_to((128, 16, 64)),
                      K("hid").rearrange("p (a f) -> p a f", f=1).broadcast_to((128, 16, 64)), MU), rdy, mtok)
            for t in range(C):
                w_ = Wst[:, t:t + 1]
                last = t == C - 1
                m = 1 if last else 3
                vX = V(stt(Xv[:, 0:m], C2[:, t, 0:m], w_, C1v[:, 0:m], MU, AD), aw, vC)
                if not last:
                    vd = V(stt(dt3[:, t + 1:8, 9:11], RT[i][:, t + 1:8, 72 + t:88:8], w_, dt3[:, t + 1:8, 9:11], MU, AD), aw)
                vY = V(stt(Yv[:, 0:m], Xv[:, 0:m], w_, C0v[:, 0:m], MU, AD), vX, vD)
                ar = A(act(rP, Yv[:, 0:1], ACT.Sqrt), vY)
                if not last:
                    va = V(stt(tmp8[:, 0:7 - t], RT[i][:, t + 1:8, 64 + t], w_, dt3[:, t + 1:8, t], MU, AD), aw)
                vq = V(stt(qst, Xv[:, 0:1], w_, qst, MU, AD), vX)
                if last:
                    break
                va = V(stt(dt3[:, t + 1:8, 8], tmp8[:, 0:7 - t], w_, dt3[:, t + 1:8, 8], MU, AD), va)
                vz = V(stt(zz1, dt3[:, t + 1, 9:10], rP, Yv[:, 2:3], MU, MX), vd, vY, ar)
                aw = A(act(Wst[:, t + 1:t + 2], zz1, ACT.Sqrt, bias=Yv[:, 1:2]), vz)
                vA = V(stt(Av, Yv[:, 0:1], 1e-5, qst, MU, AD), vY, vq)
                m = 1 if t + 1 == C - 1 else 3
                vC = V(ts(C1v[:, 0:m], K3[:, t + 1, 0:m], dt3[:, t + 1, 10:11], None, MU), vd, vX)
                if m == 3:
                    vT = V(stt(dt3[:, t + 2:8, t + 1:8], RT[i][:, t + 2:8, 8 * t + t + 1:8 * t + 8], w_,
                               dt3[:, t + 2:8, t + 1:8], MU, AD), va)
                vD = V(ts(C0v[:, 0:m], K3[:, t + 1, 0:m], Av, None, MU), vA)
                if m == 3:
                    vC = V(stt(C1v, sg3, dt3[:, t + 2, t + 1:t + 2], C1v, MU, AD), vC, vT)
                    vD = V(stt(C0v, sg3, dt3[:, t + 2, 8:9], C0v, MU, AD), vD, va)
                for _ in range(4):
                    next(ahead, 0)
            for _ in ahead:
                pass
            v = V(ttr(rp8, Wst, one8_, wc), aw)
            v = V.chain(ts(vw, vch[i], wc, None, MU))
            for h in range(2):
                p = P(mms(*[mm(PS[:, 6 + h, (a_ % 4) * 128:(a_ % 4) * 128 + 128],
                               EKBL[:, a_].rearrange("p h f -> p (h f)"), vw) for a_ in range(4 * h, 4 * h + 4)]), gE, v)
                mtok[h:h + 1] = [p]
            v = V(ttr(tmp8, Wst, crep, wc), v)
            v = V.chain(tt(mst, mst, wc, AD))
            v = V(rcp(rR, rP), ar)
            v = V.chain(tt(qst, qst, rR, MU))
            v = V.chain(tt(qst, qst, rR, MU))
            pd = list(mtok)
            for h in range(2):
                mtok[h] = V(tt(Mun[:, 4 * h:4 * h + 4, :], Mst[:, 4 * h:4 * h + 4, :],
                               PS[:, 6 + h, :].rearrange("p (a d) -> p a d", a=4), AD), pd[h], gM)
            prep.old[i] = [pd, V.last(), G.last()]
        v = V(ts(rp8, K("pairm"), rR, None, MU), gM)
        pr = P(mm(PS[:, 5, 256:264], K("rselA"), rp8), v)
        v = V(cp(Rc, PS[:, 5, 256:264]), pr)
        v = V(tt(Mst, Mun, Rc.rearrange("p (a d) -> p a d", d=1).broadcast_to((128, 8, 128)), MU), v, mtok)
        v = V.chain(ts(mst, mst, rR, None, MU))
        mtok = v
        b2 = V(ts(rp8, K("pairm"), mst, None, MU), mtok, pr)
        pr = P(mm(PS[:, 5, 256:264], K("rselA"), rp8), b2)
        v = V(cp(Rc, PS[:, 5, 256:264]), pr)
        v = V.chain(tt(Mst, Mst, Rc.rearrange("p (a d) -> p a d", d=1).broadcast_to((128, 8, 128)), SU))
        bar()

        def mo_gen(b_):
            h = slice(64 * (b_ % 2), 64 * (b_ % 2) + 64)
            c0 = slice(b_ * S, (b_ + 1) * S)
            b, w = PB.get()
            p = P(mm(PS[:, b, 0:256], Mst[h, b_ // 2, :],
                     Q[h, :].rearrange("p (c b j) -> p b c j", b=NB, c=NC)[:, b_]), w)
            yield
            k, w = TB.get()
            a = A(act(TMP[:, k, 0:256], PS[:, b, 0:256], ACT.Copy), p, w)
            PB.free(b, a)
            yield
            b, w = PB.get()
            p = P(mm(PS[:, b, 0:256], W("wout"), TMP[:, k, 0:256]), a, w)
            TB.free(k, p)
            yield
            v = V(tt(BIG[0][:, c0].rearrange("p (c j) -> p c j", c=NC),
                     X[:, :].rearrange("p (c b j) -> p b c j", b=NB, c=NC)[:, b_],
                     PS[:, b, 0:256].rearrange("p (c j) -> p c j", c=NC), AD), p)
            PB.free(b, v)

        pipe((mo_gen(b_) for b_ in range(NB)), 4)
        bar()

        X = BIG[0]
        XG, XA, QF, KF, YF = BIG[2], BIG[3], BIG[4], BIG[5], BIG[6]
        XN = BIG[1]
        pipe((ln_gen(X, XN, t) for t in range(NT)), 4)
        bar()
        bst = small(6)
        agg = small(2)
        gs = small(32)
        gs2 = small(32)
        gsc = small(32)

        def group_norm(src, dst, g_, b_):
            for n in range(NB):
                V.chain(lambda e, n=n: e.bn_stats(bst, src[:, n * S:(n + 1) * S]))
                V.chain(lambda e, n=n: e.bn_aggr(agg, bst))
                V.chain(cp(gs[:, n:n + 1], agg[:, 0:1]))
                V.chain(stt(gs[:, 16 + n:17 + n], agg[:, 0:1], agg[:, 0:1], agg[:, 1:2], MU, AD))
            p = P(mm(PS[:, 0, 0:32], K("g8"), gs), V.last())
            V(cp(gs2, PS[:, 0, 0:32]), p)
            V.chain(tt(gsc[:, 0:16], gs2[:, 0:16], gs2[:, 0:16], MU))
            V.chain(tt(gsc[:, 0:16], gs2[:, 16:32], gsc[:, 0:16], SU))
            V.chain(ts(gsc[:, 0:16], gsc[:, 0:16], 0.0, None, MX))
            a = A(act(gsc[:, 0:16], gsc[:, 0:16], ACT.Sqrt, bias=K("eps5")), V.last())
            V.chain(rcp(gsc[:, 0:16], gsc[:, 0:16]), a)
            V.chain(ts(gsc[:, 0:16], gsc[:, 0:16], g_, None, MU))
            V.chain(tt(gsc[:, 16:32], gs2[:, 0:16], gsc[:, 0:16], MU))
            V.chain(ts(gsc[:, 16:32], gsc[:, 16:32], -1.0, b_, MU, AD))
            v = V.last()
            for n in range(NB):
                c0 = slice(n * S, (n + 1) * S)
                if n % 2:
                    A(act(dst[:, c0], src[:, c0], ACT.Identity, scale=gsc[:, n:n + 1], bias=gsc[:, 16 + n:17 + n]), v)
                else:
                    V(ts(dst[:, c0], src[:, c0], gsc[:, n:n + 1], gsc[:, 16 + n:17 + n], MU, AD), v)
            bar()

        group_norm(XN, XG, B("g1"), B("b1n"))

        def qk_gen(t, w, dst, dec):
            b, wt = PB.get()
            p = P(mm(PS[:, b, :], w, XG[:, sl(t)]), wt)
            yield
            k, w_ = TB.get()
            a = A(act(TMP[:, k, :], PS[:, b, :], ACT.Square), p, w_)
            yield
            res = []
            yield from rstd_gen(a, k, None, False, res, 1e-12)
            b2, p = res[0]
            v = V(tt(dst[:, sl(t)].rearrange("p (a n) -> p a n", a=2), PS[:, b, :].rearrange("p (a n) -> p a n", a=2),
                     K(dec).rearrange("p (a n) -> p a n", a=1).broadcast_to((128, 2, 256)), MU), p)
            PB.free(b, v)
            yield
            v = V.chain(tt(dst[:, sl(t)], dst[:, sl(t)], PS[:, b2, :], MU))
            PB.free(b2, v)

        pipe([g for t in range(NT) for g in (qk_gen(t, W("q1"), QF, "dq"), qk_gen(t, W("k1"), KF, "dk"))], 3)
        bar()
        AB = BIG[7]
        KM = [AB[:, 1024 * i:1024 * i + 1024].rearrange("p (r n) -> p r n", r=4) for i in range(2)]
        VM = [AB[:, 2048 + 1024 * i:3072 + 1024 * i].rearrange("p (a r n) -> p a r n", a=2, r=4) for i in range(2)]
        KT_ = [BIG[6][:, 256 * i:256 * i + 256].rearrange("p (a n) -> p a n", a=2) for i in range(2)]
        VTK = [BIG[6][:, 512 + 256 * i:768 + 256 * i].rearrange("p (a n) -> p a n", a=2) for i in range(2)]
        SBD = [BIG[6][:, 1024 + 128 * i:1152 + 128 * i] for i in range(2)]
        YT = [BIG[6][:, 1280 + 256 * i:1536 + 256 * i] for i in range(2)]
        S1 = [BIG[6][:, 1792 + 1024 * i:2816 + 1024 * i].rearrange("p (a r n) -> p a r n", a=2, r=4) for i in range(2)]
        setfree = [[], []]
        sring = Ring([0, 1])

        def ret_gen(n):
            i = n % 2
            c0 = n * S
            w0 = setfree[i]
            vs_ = []
            for r in range(4):
                vs_.append(V(ts(KM[i][:, r, :], KF[:, c0:c0 + S], K("rm", r, r + 1), None, MU), w0))
            b, wt = PB.get()
            p = P(mms(mm(PS[:, b, 0:128], XG[:, c0:c0 + 128], W("v1")),
                      mm(PS[:, b, 128:256], XG[:, c0 + 128:c0 + 256], W("v1")),
                      tr(PS[:, b, 256:384], KF[:, c0:c0 + 128])), wt)
            yield
            a = A(act(VTK[i], PS[:, b, 0:256].rearrange("p (a n) -> p a n", a=2), ACT.Copy), p, w0)
            a = A(act(KT_[i][:, 0, :], PS[:, b, 256:384], ACT.Copy), p)
            PB.free(b, a)
            yield
            gg = []
            for h in range(2):
                gg.append(G(tt(VM[i][:, h], VTK[i][:, h, :].rearrange("p (r n) -> p r n", r=1).broadcast_to((128, 4, 128)),
                               K("colr").rearrange("p (r n) -> p r n", r=4), MU), a, w0))
            b, wt = PB.get()
            p = P(mm(PS[:, b, 0:128], KT_[i][:, 0, :], VTK[i][:, 0, :]), a, wt)
            yield
            v = V(tt(SBD[i], PS[:, b, 0:128], K("bd8"), MU), p, w0)
            PB.free(b, v)
            vsb = v
            by, wy = PB.get()
            py = None
            for g_ in range(4):
                r32 = slice(32 * g_, 32 * g_ + 32)
                ks, ws = sring.get()
                done = []
                for h in range(2):
                    b, wt = PB.get()
                    cc = c0 + 128 * h
                    p = P(mms(*[mm(PS[:, b, 128 * r:128 * r + 128], KM[i][r32, r, 128 * h:128 * h + 128],
                                   QF[r32, cc:cc + 128]) for r in range(4)]), vs_, wt)
                    yield
                    v = V(tt(S1[ks][:, h], PS[:, b, :].rearrange("p (r n) -> p r n", r=4),
                             K("tri").rearrange("p (r n) -> p r n", r=1).broadcast_to((128, 4, 128)), MU), p, ws)
                    PB.free(b, v)
                    done.append(v)
                yield
                fs = []
                for h in range(2):
                    o = PS[r32, by, 128 * h:128 * h + 128]
                    if h:
                        fs.append(mm(o, SBD[i][:, r32], QF[:, c0 + 128:c0 + 256], start=True, stop=False))
                    for r in range(4):
                        fs.append(mm(o, VM[i][:, h, r, r32], S1[ks][:, h, r, :], start=(h == 0 and r == 0), stop=(r == 3)))
                py = P(mms(*fs), done, gg, vsb, wy)
                sring.free(ks, py)
            yield
            a = A(act(YT[i], PS[:, by, 0:256], ACT.Copy), py, w0)
            PB.free(by, a)
            yield
            b, wt = PB.get()
            p = P(mm(PS[:, b, 0:256], W("o1"), YT[i]), a, wt)
            yield
            v = V(stt(XA[:, c0:c0 + S], PS[:, b, 0:256], B("ob1"), XN[:, c0:c0 + S], AD, AD), p)
            PB.free(b, v)
            setfree[i] = [v, p, py]

        pipe((ret_gen(n) for n in range(NB)), 2)
        bar()
        group_norm(XA, XG, B("fg1"), B("fb1"))

        def fin1(t):
            def f(b, p):
                v = V(stt(X[:, sl(t)], PS[:, b, :], B("b12"), X[:, sl(t)], AD, AD), p)
                return V.chain(tt(X[:, sl(t)], X[:, sl(t)], XA[:, sl(t)], AD))
            return f

        pipe((ffn_gen(t, XG, lambda j: W("w11", 128 * j, 128 * j + 128), lambda j: B("b11", j, j + 1), 2, ACT.Silu,
                      lambda j: W("w12", 128 * j, 128 * j + 128), fin1(t)) for t in range(NT)), 2)
        bar()

        R = [BIG[7][:, 256 * i:256 * i + 256] for i in range(8)]

        def r3(ap, n):
            return ap[:, 0:32 * n].rearrange("p (b e) -> p b e", e=n)

        def bc(ap, n):
            return ap.rearrange("p (b e) -> p b e", e=1).broadcast_to((128, 32, n))

        def logits(wt, n, bias, dst):
            p = P(mms(*[mm(PS[:, 0, n * k:n * k + n], XN[:, 128 * k:128 * k + 128], wt) for k in range(32)]))
            if bias is None:
                V.chain(cp(dst[:, 0:32 * n], PS[:, 0, 0:32 * n]), p)
            else:
                V.chain(tt(r3(dst, n), r3(PS[:, 0, :], n),
                           bias.rearrange("p (b e) -> p b e", b=1).broadcast_to((128, 32, n)), AD), p)

        def softmax8(lg, n, tmp):
            m, z = small(32), small(32)
            V.chain(red(m, r3(lg, n), MX))
            V.chain(tt(r3(lg, n), r3(lg, n), bc(m, n), SU))
            a = A(act(lg[:, 0:32 * n], lg[:, 0:32 * n], ACT.Exp), V.last())
            V.chain(red(z, r3(lg, n)), a)
            V.chain(rcp(z, z))
            V.chain(tt(r3(lg, n), r3(lg, n), bc(z, n), MU))

        def moe(n, nh, w1, b1, func, w2, b2, wtok, waits):
            def gen(t, e_):
                b, w = PB.get()
                p = P(mms(*[mm(PS[:, b, 128 * k:128 * k + 128],
                               wtok[:, 4 * t + k, e_:e_ + 1].broadcast_to((128, 128)), K("ident")) for k in range(4)]),
                      w, waits)
                yield
                kb, w = TB.get()
                a0 = A(act(TMP[:, kb, :], PS[:, b, :], ACT.Copy), p, w)
                PB.free(b, a0)

                def fin(bo, p):
                    v = V(stt(TMP[:, kb, :], PS[:, bo, :], b2(e_), TMP[:, kb, :], AD, MU), p, a0)
                    v2 = V.chain(tt(X[:, sl(t)], X[:, sl(t)], TMP[:, kb, :], AD))
                    TB.free(kb, v2)
                    return v
                yield from ffn_gen(t, XN, lambda j: w1(e_, j), lambda j: b1(e_, j), nh, func, lambda j: w2(e_, j), fin)
            pipe((gen(t, e_) for e_ in range(n) for t in range(NT)), 2)
            bar()

        lg, wt1 = R[0], R[1]
        logits(W("gw1"), 4, B("gb1"), lg)
        ent = small(32)
        ab = small(32)
        held = PB.idle.pop([k for k, _ in PB.idle].index(7))
        for t in range(NT):
            b, w = PB.get()
            p = P(mm(PS[0:64, b, :], W("dw1"), XN[:, sl(t)]), w, V.last())
            k, w = TB.get()
            a = A(act(TMP[0:64, k, :], PS[0:64, b, :], ACT.Relu, bias=B("db1")[0:64, :]), p, w)
            PB.free(b, a)
            p = P(mms(*[mm(PS[:, 7, 4 * t + j:4 * t + j + 1], TMP[0:64, k, 128 * j:128 * j + 128], W("dw2")[0:64, :])
                        for j in range(4)]), a)
            TB.free(k, p)
        V.chain(ts(ent, PS[:, 7, 0:32], B("db2"), None, AD), p)
        PB.free(7)
        V.chain(ts(ab, ent, -1.0, None, MU))
        V.chain(tt(ab, ent, ab, MX))
        a = A(act(ab, ab, ACT.Exp, scale=-1.0), V.last())
        a = A.chain(act(ab, ab, ACT.Ln, bias=K("one")[:, 0:1]))
        V.chain(ts(ent, ent, 0.0, None, MX), a)
        V.chain(tt(ent, ent, ab, AD))
        V.chain(ts(ent, ent, -0.5, None, AD))
        V.chain(ts(ent, ent, 1.0 / 1.5, None, MU))
        V.chain(ts(ent, ent, 0.0, 1.0, MX, MN))
        V.chain(ts(ent, ent, 3.0, 1.0, MU, AD))
        V.chain(ts(ent, ent, RND, None, AD))
        V.chain(ts(ent, ent, -RND, None, AD))
        V.chain(ts(ent, ent, 1.0, 4.0, MX, MN))
        rk = R[2]
        V.chain(lambda e: e.memset(rk[:, 0:128], 0.0))
        l3, k3 = r3(lg, 4), r3(rk, 4)
        for i in range(4):
            for j in range(i + 1, 4):
                V.chain(tt(ab, l3[:, :, j], l3[:, :, i], ALU.is_gt))
                V.chain(tt(k3[:, :, i], k3[:, :, i], ab, AD))
                V.chain(ts(ab, ab, -1.0, 1.0, MU, AD))
                V.chain(tt(k3[:, :, j], k3[:, :, j], ab, AD))
        V.chain(tt(k3, k3, bc(ent, 4), ALU.is_lt))
        V.chain(red(ab, l3, MX))
        V.chain(tt(l3, l3, bc(ab, 4), SU))
        a = A(act(lg[:, 0:128], lg[:, 0:128], ACT.Exp), V.last())
        V.chain(tt(l3, l3, k3, MU), a)
        V.chain(red(ab, l3))
        V.chain(rcp(ab, ab))
        V.chain(tt(l3, l3, bc(ab, 4), MU))
        bar()
        moe(4, 2, lambda e, j: MW[:, 256 * e + 128 * j:256 * e + 128 * j + 128], lambda e, j: B("eb1", 2 * e + j, 2 * e + j + 1),
            ACT.Relu, lambda e, j: MW[:, 1024 + 256 * e + 128 * j:1024 + 256 * e + 128 * j + 128],
            lambda e: B("eb2", e, e + 1), l3, [(s_m1, 16)])
        mw_free = bar()
        SP.dma(lambda e: e.dma_start(MW[:, :], m2), (s_m2, 16), mw_free, (s_m1, 16))

        pipe((ln_gen(X, XN, t) for t in range(NT)), 4)
        bar()
        XT, X1, H1, H2, KN, DG = BIG[2], BIG[3], BIG[4], BIG[5], BIG[6], BIG[7]
        XT3 = XT[:, :].rearrange("p (b d) -> p b d", b=32)
        def xt_gen(k):
            b, w = PB.get()
            p = P(mms(*[tr(PS[:, b, 128 * j:128 * j + 128], XN[:, 128 * (k + j):128 * (k + j) + 128])
                        for j in range(4)]), w)
            yield
            a = A(act(XT[:, 128 * k:128 * k + 512], PS[:, b, :], ACT.Copy), p)
            PB.free(b, a)

        pipe((xt_gen(4 * k) for k in range(8)), 2)
        bar()
        d_idx = nc.dram_tensor("d_idx", (4096,), mybir.dt.uint32).ap()
        d_xt = nc.dram_tensor("d_xt", (4096, 136), F32).ap()
        d_acc = nc.dram_tensor("d_acc", (4096, 128), F32).ap()
        s_i, s_i2, s_xt, s_z = sem("d_i"), sem("d_i2"), sem("d_xt"), sem("d_z")
        s_g = [sem(f"d_g{i}") for i in range(8)]
        s_s = [sem(f"d_s{i}") for i in range(8)]
        IX = small(32).bitcast(mybir.dt.uint32)

        def views(a, n, b, m):
            return (a[:, 0:n].rearrange("p (x y) -> p x y", y=1).broadcast_to((128, n, m)),
                    b.rearrange("p (x y) -> p x y", x=1).broadcast_to((128, n, m)))

        lg, eq, sel, pre, tot = R[0], R[1], R[2], R[4], R[5]
        logits(W("gw2"), 8, None, lg)
        softmax8(lg, 8, None)
        thr, cand, cnt, one8, need = (small(8) for _ in range(5))
        p3 = r3(lg, 8)
        V.chain(lambda e: e.memset(thr, 0.0))

        def b32(ap):
            return ap.rearrange("p (b e) -> p b e", b=1).broadcast_to((128, 32, 8))

        for bit in range(29, -1, -1):
            V.chain(ts(cand.bitcast(I32), thr.bitcast(I32), 1 << bit, None, ALU.bitwise_or))
            V.chain(tt(r3(eq, 8), p3, b32(cand), ALU.is_ge))
            V.chain(red(cnt, eq[:, 0:256].rearrange("p (b e) -> p e b", e=8)))
            p = P(mm(PS[:, 0, 0:8], K("one"), cnt), V.last())
            V.chain(ts(one8.bitcast(I32), PS[:, 0, 0:8], 512.0, None, ALU.is_ge), p)
            V.chain(lambda e: e.copy_predicated(thr, one8.bitcast(I32), cand))
        V.chain(tt(r3(sel, 8), p3, b32(thr), ALU.is_gt))
        V.chain(tt(r3(eq, 8), p3, b32(thr), ALU.is_equal))

        def prefix(m, out, tmp):
            p = P(mms(mm(PS[:, 0, 0:256], K("lt"), m), mm(PS[:, 0, 256:512], K("one"), m)), V.last())
            V.chain(cp(tmp, PS[:, 0, 256:512]), p)
            x, y = tmp, out
            for sh in (1, 2, 4, 8, 16):
                V.chain(cp(y[:, 0:8 * sh], x[:, 0:8 * sh]))
                V.chain(tt(y[:, 8 * sh:256], x[:, 8 * sh:256], x[:, 0:256 - 8 * sh], AD))
                x, y = y, x
            V.chain(tt(x, x, PS[:, 0, 256:512], SU))
            V.chain(tt(out, x, PS[:, 0, 0:256], AD))

        prefix(eq, pre, tot)
        V.chain(red(cnt, sel[:, 0:256].rearrange("p (b e) -> p e b", e=8)))
        p = P(mm(PS[:, 0, 0:8], K("one"), cnt), V.last())
        V.chain(ts(need, PS[:, 0, 0:8], -1.0, 512.0, MU, AD), p)
        V.chain(tt(r3(pre, 8), r3(pre, 8), b32(need), ALU.is_lt))
        V.chain(tt(pre, pre, eq, MU))
        V.chain(tt(sel, sel, pre, AD))
        prefix(sel, pre, tot)
        V.chain(ts(pre, pre, 1.0, None, AD))
        V.chain(tt(pre, pre, sel, MU))
        V.chain(ts(pre, pre, -1.0, None, AD))
        pi, ph = tot.bitcast(I32), R[6]
        V.chain(cp(pi, pre))
        V.chain(ts(eq.bitcast(I32), pi, 4, None, ALU.arith_shift_right))
        V.chain(cp(ph, eq.bitcast(I32)))
        V.chain(ts(eq.bitcast(I32), pi, 15, None, ALU.bitwise_and))
        V.chain(cp(pre, eq.bitcast(I32)))
        OH = BIG[4][:, :].bitcast(BF16).rearrange("p (x n) -> p x n", n=32)
        OL = BIG[5][:, :].bitcast(BF16).rearrange("p (x v n) -> p x v n", v=2, n=16)
        V.chain(tt(OH, *views(ph, 256, K("i32"), 32), ALU.is_equal))
        LO = BIG[6][:, 0:2048].bitcast(BF16).rearrange("p (x n) -> p x n", n=16)
        V.chain(tt(LO, *views(pre, 256, K("i32", 0, 16), 16), ALU.is_equal))
        V.chain(ts(OL[:, :, 0, :], LO, K("pcol"), None, MU))
        for k in range(32):
            V(ts(OL[:, 8 * k:8 * k + 8, 1, :], LO[:, 8 * k:8 * k + 8, :], K("blkid", k, k + 1), None, MU))
        OHf = OH.rearrange("p x n -> p (x n)")
        OLf = OL.rearrange("p x v n -> p (x v n)")
        for hh in range(2):
            p = P(mms(*[mm(PS[:, 1 + hh, 0:256], OHf[:, 256 * k + 128 * hh:256 * k + 128 * hh + 128],
                           OLf[:, 256 * k:256 * k + 256], start=(k == 0), stop=(k == 31)) for k in range(32)]), V.last())
        idf = R[7]
        IDX = BIG[6][:, 2048:2048 + 32].bitcast(mybir.dt.uint32).rearrange("p (h l) -> p h l", h=2)
        for hh in range(2):
            a = A(act(R[6 + hh], PS[:, 1 + hh, 0:256], ACT.Copy), p)
        for hh in range(2):
            for e4 in range(4):
                q = slice(32 * e4, 32 * e4 + 32)
                c = 32 * (4 * hh + e4)
                v = V(stt(IDX[q, hh, :], R[6 + hh][q, c + 16:c + 32], 128.0, R[6 + hh][q, c:c + 16], MU, AD), a)
        SP.dma(lambda e: e.dma_start(d_idx.rearrange("(h p l) -> p h l", h=2, l=16), IDX), (s_i, 16), v)
        SP.dma(lambda e: e.dma_start(IX, d_idx.rearrange("(c p) -> p c", p=128), allow_slow_non_contiguous=True), (s_i2, 16), (s_i, 16))
        SP.dma(lambda e: e.dma_start(d_xt.rearrange("(b p) d -> p b d", p=128)[:, :, 0:128], XT3), (s_xt, 16), v)
        SP.dma(lambda e: e.dma_start(d_xt.rearrange("(b p) d -> p b d", p=128)[:, :, 128:136], r3(lg, 8)), (s_xt, 32), v)
        for e_ in (A, V, G, P):
            e_.items.append((lambda eng: None, [(s_xt, 32), (s_i2, 16)], False))
        bar()

        def fetch2():
            z = BIG[7][:, 1024:2048]
            v = V(lambda e: e.memset(z, 0.0))
            for q in range(4):
                SP.dma(lambda e, q=q: e.dma_start(
                    d_acc.rearrange("(p b) d -> p (b d)", p=128)[:, 1024 * q:1024 * q + 1024], z), (s_z, 16 * q + 16), v)
            for e_ in range(8):
                for q in range(4):
                    dst = gx(e_)[:, 136 * q:136 * q + 136]
                    c = 4 * e_ + q
                    G.dma(lambda e, dst=dst, c=c: e.indirect_dma_start(
                        dst, None, d_xt, bass.IndirectOffsetOnAxis(ap=IX[:, c:c + 1], axis=0)), (s_g[e_], 0),
                        (s_xt, 32), (s_i2, 16), v)

        def gx(e_):
            return BIG[3][:, 544 * e_:544 * e_ + 544] if e_ < 7 else BIG[7][:, 0:544]

        def experts2():
            YO = [BIG[5][:, 512 * i:512 * i + 512] for i in range(8)]

            def gen(e_):
                b, w = PB.get()
                p = P(mms(*[tr(PS[:, b, 128 * q:128 * q + 128], gx(e_)[:, 136 * q:136 * q + 128]) for q in range(4)]),
                      w, (s_g[e_], 64), (s_m2, 16))
                yield
                kx, w = TB.get()
                ax = A(act(TMP[:, kx, :], PS[:, b, :], ACT.Copy), p, w)
                PB.free(b, ax)
                yield
                bo, wo = PB.get()
                hs = []
                for j in range(4):
                    b, w = PB.get()
                    p = P(mm(PS[:, b, :], MW[:, 512 * e_ + 128 * j:512 * e_ + 128 * j + 128], TMP[:, kx, :]), w, ax)
                    yield
                    k, w = TB.get()
                    a = A(act(TMP[:, k, :], PS[:, b, :], ACT.Gelu_apprx_tanh, bias=B("m2b1", 4 * e_ + j, 4 * e_ + j + 1)), p, w)
                    PB.free(b, a)
                    hs.append((k, a))
                    if j:
                        kk, aa = hs[j - 1]
                        p = P(mm(PS[:, bo, :], MW[:, 4096 + 512 * e_ + 128 * (j - 1):4096 + 512 * e_ + 128 * j],
                                 TMP[:, kk, :], start=(j == 1), stop=False), aa, wo)
                        TB.free(kk, p)
                TB.free(kx, p)
                kk, aa = hs[3]
                p = P(mm(PS[:, bo, :], MW[:, 4096 + 512 * e_ + 384:4096 + 512 * e_ + 512], TMP[:, kk, :],
                         start=False, stop=True), aa)
                TB.free(kk, p)
                yield
                k, w = TB.get()
                a = A(act(TMP[:, k, :], PS[:, bo, :], ACT.Identity, bias=B("m2b2", e_, e_ + 1)), p, w)
                yield
                p = P(mms(*[tr(PS[:, bo, 128 * q:128 * q + 128], TMP[:, k, 128 * q:128 * q + 128]) for q in range(4)]), a)
                TB.free(k, p)
                yield
                for q in range(4):
                    v = V(ts(YO[e_][:, 128 * q:128 * q + 128], PS[:, bo, 128 * q:128 * q + 128],
                             gx(e_)[:, 136 * q + 128 + e_:136 * q + 129 + e_], None, MU), p)
                PB.free(bo, v)
                before = (s_s[e_ - 1], 64) if e_ else (s_z, 64)
                for q in range(4):
                    c = 4 * e_ + q
                    src = YO[e_][:, 128 * q:128 * q + 128]
                    G.dma(lambda e, src=src, c=c: e.indirect_dma_start(
                        d_acc, bass.IndirectOffsetOnAxis(ap=IX[:, c:c + 1], axis=0), src, None, compute_op=AD),
                        (s_s[e_], 0), v, before)

            pipe((gen(e_) for e_ in range(8)), 2)
            s_a = sem("d_a")
            SP.dma(lambda e: e.dma_start(BIG[6][:, :].rearrange("p (b d) -> p b d", b=32),
                                         d_acc.rearrange("(b p) d -> p b d", p=128)), (s_a, 16), (s_s[7], 64), bar())
            for k in range(8):
                b, w = PB.get()
                p = P(mms(*[tr(PS[:, b, 128 * q:128 * q + 128], BIG[6][:, 512 * k + 128 * q:512 * k + 128 * q + 128])
                            for q in range(4)]), w, (s_a, 16))
                v = V(tt(X[:, 512 * k:512 * k + 512], X[:, 512 * k:512 * k + 512], PS[:, b, :], AD), p)
                PB.free(b, v)

        XP = DG[0:32, 0:2048].rearrange("p (b d) -> p b d", b=16)
        for q_ in range(4):
            b, w = PB.get()
            p = P(mms(*[tr(PS[0:32, b, 128 * j:128 * j + 128],
                           XN[:, 256 * (4 * q_ + j) + 96:256 * (4 * q_ + j) + 128]) for j in range(4)]), w)
            a = A(act(XP[:, 4 * q_:4 * q_ + 4, :], PS[0:32, b, :].rearrange("p (b d) -> p b d", b=4), ACT.Copy), p)
            PB.free(b, a)
        bar()
        wm, wz = small(32), small(32)
        SCL = 128 ** -0.5

        def win_gen(k):
            half = k % 2
            nk = 160 if half else 128
            q0 = 128 * k
            b, w = PB.get()
            p = P(mm(PS[:, b, 0:nk], XN[:, q0:q0 + 128], XN[:, q0 + 128 - nk:q0 + 128]), w)
            yield
            kt, w = TB.get()
            sc_ = TMP[:, kt, 0:nk]
            v = V(stt(sc_, PS[:, b, 0:nk], SCL, K("band") if half else K("band0"), MU, AD), p, w)
            PB.free(b, v)
            v = V.chain(red(wm[:, k:k + 1], sc_, MX))
            v = V.chain(ts(wm[:, k:k + 1], wm[:, k:k + 1], -1.0, None, MU))
            yield
            a = A(act(sc_, sc_, ACT.Exp, bias=wm[:, k:k + 1], accum_out=wz[:, k:k + 1]), v)
            yield
            v = V(rcp(wz[:, k:k + 1], wz[:, k:k + 1]), a)
            v = V.chain(ts(sc_, sc_, wz[:, k:k + 1], None, MU))
            yield
            b, w = PB.get()
            fs = [tr(PS[:, b, 0:128], sc_[:, nk - 128:nk])]
            if half:
                fs.append(tr(PS[0:32, b, 128:256], sc_[:, 0:32]))
            p = P(mms(*fs), v, w)
            yield
            a = A(act(TMP[:, kt, 256:384], PS[:, b, 0:128], ACT.Copy), p)
            if half:
                a = A(act(TMP[0:32, kt, 384:512], PS[0:32, b, 128:256], ACT.Copy), p)
            yield
            fs = [mm(PS[:, b, 256:384], XT3[:, k, :], TMP[:, kt, 256:384], stop=not half)]
            if half:
                fs.append(mm(PS[:, b, 256:384], XP[:, k // 2, :], TMP[0:32, kt, 384:512], start=False))
            p = P(mms(*fs), a)
            TB.free(kt, p)
            yield
            v = V(tt(X1[:, q0:q0 + 128], PS[:, b, 256:384], XN[:, q0:q0 + 128], AD), p)
            PB.free(b, v)

        pipe((win_gen(k) for k in range(32)), 4)
        bar()
        pipe((ln_gen(X1, X1, t, gb=[B("g21"), B("be21")]) for t in range(NT)), 4)
        bar()

        def kn_gen(src, dst, n0, n):
            k, w = TB.get()
            a = A(act(TMP[:, k, 0:n], src[:, n0:n0 + n], ACT.Square), w)
            yield
            res = []
            yield from rstd_gen(a, k, None, False, res, 1e-12, n)
            b, p = res[0]
            v = V(tt(dst[:, n0:n0 + n], src[:, n0:n0 + n], PS[:, b, 0:n], MU), p)
            PB.free(b, v)

        pk = small(50)
        pkn, pkp, ph1, ph2, pdf = (pk[:, 10 * i:10 * i + 10] for i in range(5))
        pipe([kn_gen(XN, KN, TW * t, TW) for t in range(NT)] + [kn_gen(W("pT"), pkn, 0, 10)], 3)
        bar()
        bim = small(1)
        V(tt(bim, B("memb"), B("bi"), SU))
        bar()
        DF = DG

        def mem_gen(kn, kp, h1, h2, df, n0, n):
            s = slice(n0, n0 + n)
            b, w = PB.get()
            p = P(mm(PS[:, b, 0:n], W("wi"), kn[:, s]), w)
            yield
            k, w = TB.get()
            a = A(act(TMP[:, k, 0:n], PS[:, b, 0:n], ACT.Identity, bias=B("bi")), p, w)
            PB.free(b, a)
            yield
            b, w = PB.get()
            p = P(mm(PS[:, b, 0:n], W("wl1"), TMP[:, k, 0:n]), a, w)
            yield
            k2, w = TB.get()
            a = A(act(TMP[:, k2, 0:n], PS[:, b, 0:n], ACT.Silu, bias=B("bl1")), p, w)
            PB.free(b, a)
            yield
            b, w = PB.get()
            p = P(mm(PS[:, b, 0:n], W("wl2"), TMP[:, k2, 0:n]), a, w)
            TB.free(k2, p)
            yield
            a = A(act(h2[:, s], PS[:, b, 0:n], ACT.Silu, bias=B("bl2")), p)
            PB.free(b, a)
            yield
            b, w = PB.get()
            p = P(mm(PS[:, b, 0:n], W("memT"), h2[:, s]), a, w)
            yield
            v = V(stt(df[:, s], PS[:, b, 0:n], B("memb"), TMP[:, k, 0:n], AD, SU), p)
            PB.free(b, v)
            TB.free(k, v)

        pipe([mem_gen(KN, None, None, H2, DF, TW * t, TW) for t in range(NT)]
             + [mem_gen(pkn, None, None, ph2, pdf, 0, 10)], 3)
        bar()
        V(ts(pdf, pdf, 16.0, None, MU))
        bar()
        PB = Ring(range(7))

        def gr_gen(k, n, h2, df):
            s = slice(128 * k, 128 * k + n)
            b, w = PB.get()
            p = P(mms(tr(PS[0:n, b, 0:128], h2[:, s]),
                      tr(PS[0:n, b, 128:256], df[:, s])), w)
            yield
            kt, w = TB.get()
            a = A(act(TMP[0:n, kt, 0:256], PS[0:n, b, 0:256], ACT.Copy), p, w)
            PB.free(b, a)
            yield
            last = n != 128
            p = P(mm(PS[:, 7, 0:128], TMP[0:n, kt, 0:128], TMP[0:n, kt, 128:256], start=(k == 0 and not last), stop=last), a)
            TB.free(kt, p)

        pipe([gr_gen(k, 128, H2, DF) for k in range(32)] + [gr_gen(0, 10, ph2, pdf)], 3)
        wnew = TMP[:, 8, 0:128]
        gsx = small(2)
        bar()
        V(ts(gsx[:, 0:1], B("lrate"), 2.0 / (4256 * 128), None, MU))
        V.chain(ts(gsx[:, 1:2], B("fgate"), -1.0, 1.0, MU, AD))
        V.chain(ts(wnew, PS[:, 7, 0:128], gsx[:, 0:1], None, MU))
        V.chain(stt(wnew, W("memT"), gsx[:, 1:2], wnew, MU, AD))
        bar()
        PB = Ring(range(8))
        TB = Ring(range(8))
        MO = KN

        def mo2_gen(t):
            s = sl(t)
            b, w = PB.get()
            p = P(mm(PS[:, b, :], wnew, H2[:, s]), w)
            yield
            k, w = TB.get()
            a = A(act(TMP[:, k, :], PS[:, b, :], ACT.Identity, bias=B("memb")), p, w)
            PB.free(b, a)
            yield
            b, w = PB.get()
            p = P(mm(PS[:, b, :], W("wo2"), TMP[:, k, :]), a, w)
            yield
            a = A(act(MO[:, s], PS[:, b, :], ACT.Identity, bias=B("bo2")), p)
            PB.free(b, a)
            yield
            b, w = PB.get()
            p = P(mms(mm(PS[:, b, :], W("wg", 0, 128), X1[:, s], stop=False),
                      mm(PS[:, b, :], W("wg", 128, 256), MO[:, s], start=False)), a, w)
            yield
            a = A(act(TMP[:, k, :], PS[:, b, :], ACT.Sigmoid, bias=B("bg")), p)
            PB.free(b, a)
            yield
            v = V(tt(DG[:, s], X1[:, s], MO[:, s], SU), a)
            v = V.chain(tt(DG[:, s], DG[:, s], TMP[:, k, :], MU))
            TB.free(k, v)
            yield
            v = V.chain(tt(DG[:, s], DG[:, s], MO[:, s], AD))
            v = V.chain(tt(DG[:, s], DG[:, s], X1[:, s], AD))

        pipe((mo2_gen(t) for t in range(NT)), 3)
        bar()
        TB = Ring(range(9))
        X2 = DG
        pipe((ln_gen(DG, X2, t, gb=[B("g22"), B("be22")]) for t in range(NT)), 4)
        bar()

        def fin2(t):
            def f(b, p):
                return V(stt(H1[:, sl(t)], PS[:, b, :], B("b22"), X2[:, sl(t)], AD, AD), p)
            return f

        pipe((ffn_gen(t, X2, lambda j: W("w21", 128 * j, 128 * j + 128), lambda j: B("b21", j, j + 1), 4, ACT.Silu,
                      lambda j: W("w22", 128 * j, 128 * j + 128), fin2(t)) for t in range(NT)), 2)
        bar()
        pipe((ln_gen(H1, H1, t, gb=[B("g23"), B("be23")]) for t in range(NT)), 4)
        bar()

        fetch2()

        def fin2s(t):
            def f(b, p):
                v = V(stt(X[:, sl(t)], PS[:, b, :], B("bs2"), X[:, sl(t)], AD, AD), p)
                return V.chain(tt(X[:, sl(t)], X[:, sl(t)], H1[:, sl(t)], AD))
            return f

        pipe((ffn_gen(t, XN, lambda j: W("ws1", 128 * j, 128 * j + 128), lambda j: B("bs1", j, j + 1), 4,
                      ACT.Gelu_apprx_tanh, lambda j: W("ws2", 128 * j, 128 * j + 128), fin2s(t)) for t in range(NT)), 2)
        bar()
        experts2()
        mw_free = bar()
        SP.dma(lambda e: e.dma_start(MW[:, :], m3), (s_m3, 16), mw_free, (s_m2, 16))

        pipe((ln_gen(X, XN, t) for t in range(NT)), 4)
        bar()
        QF, KF, VF, CF = BIG[2], BIG[3], BIG[4], BIG[5]
        pipe([g for t in range(NT) for g in (lin_gen(t, QF, W("qkv", 0, 128), XN, ACT.Identity, bias=B("bqkv", 0, 1)),
                                              lin_gen(t, KF, W("qkv", 128, 256), XN, ACT.Identity, bias=B("bqkv", 1, 2)))], 4)
        VF3 = VF[:, :].rearrange("p (b d) -> p b d", b=32)

        def v3_gen(k):
            b, w = PB.get()
            p = P(mms(*[mm(PS[:, b, 128 * j:128 * j + 128], XN[:, 128 * (k + j):128 * (k + j) + 128], W("qkv", 256, 384))
                        for j in range(4)]), w)
            yield
            v = V(tt(VF3[:, k:k + 4, :], PS[:, b, :].rearrange("p (b d) -> p b d", b=4),
                     B("bv3").rearrange("p (b d) -> p b d", b=1).broadcast_to((128, 4, 128)), AD), p)
            PB.free(b, v)

        pipe((v3_gen(4 * k) for k in range(8)), 2)
        bar()
        EN = CF
        esum = small(8)

        def en_gen(t):
            k, w = TB.get()
            a = A(act(TMP[:, k, :], QF[:, sl(t)], ACT.Square), w)
            yield
            b, w = PB.get()
            p = P(mm(PS[:, b, :], K("s8"), TMP[:, k, :]), a, w)
            TB.free(k, p)
            yield
            a = A(act(EN[:, sl(t)], PS[:, b, :], ACT.Sqrt, accum_out=esum[:, t:t + 1]), p)
            PB.free(b, a)

        pipe((en_gen(t) for t in range(NT)), 3)
        bar()
        et = small(2)
        V(red(et[:, 0:1], esum))
        p = P(mm(PS[:, 0, 0:1], K("one"), et[:, 0:1]), V.last())
        V(ts(et[:, 1:2], PS[:, 0, 0:1], 0.1 / (128.0 * T), None, MU), p)
        V.chain(ts(EN[:, :], EN[:, :], et[:, 1:2], None, ALU.is_gt))
        V.chain(tt(KF[:, :], KF[:, :], EN[:, :], MU))
        bar()
        ISQ = float(np.float32(1.0) / np.sqrt(np.float32(8.0)))
        QM = [BIG[6][:, 1024 * i:1024 * i + 1024].rearrange("p (r n) -> p r n", r=4) for i in range(2)]
        VM = [BIG[6][:, 2048 + 1024 * i:3072 + 1024 * i].rearrange("p (a r n) -> p a r n", a=2, r=4) for i in range(2)]
        PP = [BIG[7][:, 512 * i:512 * i + 512].rearrange("p (a n) -> p a n", a=2) for i in range(8)]
        PTT = [BIG[5][:, 512 * i:512 * i + 512].rearrange("p (a n) -> p a n", a=2) for i in range(8)]
        prg = Ring(range(8))
        ptr = Ring(range(8))
        mxr = Ring(range(8))
        mx = small(16)
        ZZ = [small(32) for _ in range(2)]
        setfree = [[], []]
        con_ = {}

        def at_gen(n, h_):
            i = n % 2
            c0 = n * S
            g_, r = h_ // 4, h_ % 4
            r32 = slice(32 * g_, 32 * g_ + 32)
            if h_ == 0:
                w0 = setfree[i]
                vq = [V(ts(QM[i][:, q, :], QF[:, c0:c0 + S], K("rm", q, q + 1), None, MU), w0) for q in range(4)]
                gv = [G(tt(VM[i][:, h], VF3[:, 2 * n + h, :].rearrange("p (r n) -> p r n", r=1).broadcast_to((128, 4, 128)),
                           K("colr").rearrange("p (r n) -> p r n", r=4), MU), w0) for h in range(2)]
                con_[n] = (vq, gv, w0) + PB.get()
            vq, gv, w0, bo, wo = con_[n]
            b, w = PB.get()
            p = P(mms(*[mm(PS[:, b, 256 * h:256 * h + 256], QM[i][r32, r, 128 * h:128 * h + 128],
                           KF[r32, c0:c0 + S]) for h in range(2)]), vq, w)
            yield
            m_, wm_ = mxr.get()
            mm_ = mx[:, 2 * m_:2 * m_ + 2]
            v = V(red(mm_, PS[:, b, :].rearrange("p (h n) -> p h n", h=2), MX), p, wm_)
            v = V.chain(ts(mm_, mm_, -ISQ, None, MU))
            yield
            kp, wp = prg.get()
            for h in range(2):
                a = A(act(PP[kp][:, h, :], PS[:, b, 256 * h:256 * h + 256], ACT.Exp, scale=ISQ,
                          bias=mm_[:, h:h + 1], accum_out=ZZ[i][:, 16 * h + h_:16 * h + h_ + 1]), v, wp, w0)
            mxr.free(m_, a)
            PB.free(b, a)
            yield
            b, w = PB.get()
            p = P(mms(*[tr(PS[:, b, 256 * jh + 128 * ih:256 * jh + 128 * ih + 128],
                           PP[kp][:, ih, 128 * jh:128 * jh + 128]) for jh in range(2) for ih in range(2)]), a, w)
            prg.free(kp, p)
            yield
            kt, wt = ptr.get()
            f = PTT[kt]
            if r % 2:
                a2 = A(act(f, PS[:, b, :].rearrange("p (a n) -> p a n", a=2), ACT.Copy), p, wt)
            else:
                a2 = V(cp(f, PS[:, b, :].rearrange("p (a n) -> p a n", a=2)), p, wt)
            PB.free(b, a2)
            yield
            py = P(mms(*[mm(PS[r32, bo, 0:256], VM[i][:, jh, r, r32], PTT[kt][:, jh, :],
                            start=(r == 0 and jh == 0), stop=(r == 3 and jh == 1)) for jh in range(2)]), a2, gv, wo)
            ptr.free(kt, py)
            if h_ < 15:
                return
            yield
            k2, w2 = TB.get()
            v = V(rcp(ZZ[i], ZZ[i]), a)
            v = V.chain(cp(TMP[:, k2, 0:256].rearrange("p (a d) -> p a d", d=8),
                           ZZ[i].rearrange("p (a d) -> p a d", d=1).broadcast_to((128, 32, 8))), w2)
            k, w = TB.get()
            a = A(act(TMP[:, k, 0:256], PS[:, bo, 0:256], ACT.Copy), py, w)
            p = P(mms(*[mm(PS[:, bo, 128 * h:128 * h + 128], TMP[:, k2, 128 * h:128 * h + 128], K("ident"))
                        for h in range(2)]), v, a)
            TB.free(k2, p)
            yield
            v = V(tt(TMP[:, k, 0:256], TMP[:, k, 0:256], PS[:, bo, 0:256], MU), p)
            yield
            p = P(mm(PS[:, bo, 0:256], W("w3o"), TMP[:, k, 0:256]), v)
            TB.free(k, p)
            yield
            v = V(stt(X[:, c0:c0 + S], PS[:, bo, 0:256], B("bo3"), X[:, c0:c0 + S], AD, AD), p)
            PB.free(bo, v)
            setfree[i] = [v, py, p]

        pipe((at_gen(n, h_) for n in range(NB) for h_ in range(16)), 6)
        bar()
        logits(W("gw3"), 8, B("gb3"), R[0])
        softmax8(R[0], 8, None)
        m = small(32)
        p3 = r3(R[0], 8)
        V.chain(red(m, p3, MX))
        V.chain(tt(p3, p3, bc(m, 8), ALU.is_equal))
        V.chain(tt(p3, p3, K("desc").rearrange("p (b e) -> p b e", b=1).broadcast_to((128, 32, 8)), MU))
        V.chain(red(m, p3, MX))
        V.chain(tt(p3, p3, bc(m, 8), ALU.is_equal))
        bar()
        moe(8, 4, lambda e, j: MW[:, 512 * e + 128 * j:512 * e + 128 * j + 128],
            lambda e, j: B("m3b1", 4 * e + j, 4 * e + j + 1), ACT.Relu,
            lambda e, j: MW[:, 4096 + 512 * e + 128 * j:4096 + 512 * e + 128 * j + 128],
            lambda e: B("m3b2", e, e + 1), p3, [(s_m3, 16)])
        done = bar()
        s_o = sem("d_o")
        SP.dma(lambda e: e.dma_start(outT, X[:, :]), (s_o, 16), done)
        SP.items.append((lambda eng: None, [(s_o, 16)], False))

        block = ctx.enter_context(nc.Block())

        @block.sync
        def _(e):
            SP.play(e)

        @block.scalar
        def _(e):
            A.play(e)

        @block.vector
        def _(e):
            V.play(e)

        @block.gpsimd
        def _(e):
            G.play(e)

        @block.tensor
        def _(e):
            P.play(e)


def kernel(**inp):
    import concourse.bacc as bacc
    from concourse.bass_utils import run_bass_kernel_spmd as run

    f = {k: np.asarray(v) for k, v in inp.items()}

    def pad(a):
        out = np.zeros((128, a.shape[1]), np.float32)
        out[:a.shape[0]] = a
        return out

    def blocks(a):
        n = a.shape[0] // 128
        return a.reshape(n, 128, a.shape[1]).transpose(1, 0, 2).reshape(128, -1)

    def col(a):
        return a.reshape(-1, 128).T

    def row(a):
        return np.broadcast_to(a.reshape(1, -1), (128, a.size))

    L0, L1, L2, L3 = "L0_attn_", "L1_attn_", "L2_attn_", "L3_attn_"
    w = dict(
        wk=np.concatenate([f[L0 + "Wk"].T] * 2, 1), wq=np.concatenate([f[L0 + "Wq"].T] * 2, 1), wv=f[L0 + "Wv"].T,
        wout=f[L0 + "Wout"].T, f1=f["L0_ffn_W1"].T, f2=blocks(f["L0_ffn_W2"].T),
        q1=f[L1 + "qw"].T, k1=f[L1 + "kw"].T, v1=f[L1 + "vw"].T, o1=f[L1 + "ow"].T, w11=f[L1 + "w1"].T,
        w12=blocks(f[L1 + "w2"].T), gw1=f["L1_ffn_gate_w"], dw1=f["L1_ffn_dp_w1"], dw2=pad(f["L1_ffn_dp_w2"]),
        wi=f[L2 + "Wi"].T, wl1=f[L2 + "Wl1"].T, wl2=f[L2 + "Wl2"].T, memT=f[L2 + "mem_W"].T, wo2=f[L2 + "Wo"].T,
        wg=blocks(f[L2 + "Wg"].T), w21=f[L2 + "W1"].T, w22=blocks(f[L2 + "W2"].T), gw2=f["L2_ffn_gate"],
        ws1=f["L2_ffn_Ws1"], ws2=blocks(f["L2_ffn_Ws2"]), pT=f[L2 + "P"].T,
        qkv=f[L3 + "w_qkv"].T, w3o=f[L3 + "w_out"].T, gw3=f["L3_ffn_gate_w"])
    b = dict(
        nw=col(f[L0 + "norm_weight"]), eta=np.concatenate([f[L0 + "eta"]] * 2).reshape(128, 1),
        f1b=col(f["L0_ffn_b1"]), f2b=col(f["L0_ffn_b2"]),
        g1=col(f[L1 + "norm_g"]), b1n=col(f[L1 + "norm_b"]), ob1=col(f[L1 + "ob"]), fg1=col(f[L1 + "ffn_norm_g"]),
        fb1=col(f[L1 + "ffn_norm_b"]), b11=col(f[L1 + "b1"]), b12=col(f[L1 + "b2"]),
        gb1=row(f["L1_ffn_gate_b"]), db1=pad(f["L1_ffn_dp_b1"].reshape(-1, 1)), db2=row(f["L1_ffn_dp_b2"]),
        eb1=col(f["L1_ffn_eb1"].reshape(-1)), eb2=col(f["L1_ffn_eb2"].reshape(-1)),
        memb=col(f[L2 + "mem_b"]), bi=col(f[L2 + "bi"]), bl1=col(f[L2 + "bl1"]), bl2=col(f[L2 + "bl2"]),
        bo2=col(f[L2 + "bo"]), fgate=row(f[L2 + "fgate"]), lrate=row(f[L2 + "lrate"]), bg=col(f[L2 + "bg"]),
        b21=col(f[L2 + "b1"]), b22=col(f[L2 + "b2"]), g21=col(f[L2 + "g1"]), be21=col(f[L2 + "be1"]),
        g22=col(f[L2 + "g2"]), be22=col(f[L2 + "be2"]), g23=col(f[L2 + "g3"]), be23=col(f[L2 + "be3"]),
        m2b1=col(f["L2_ffn_b1"].reshape(-1)), m2b2=col(f["L2_ffn_b2"].reshape(-1)), bs1=col(f["L2_ffn_bs1"]),
        bs2=col(f["L2_ffn_bs2"]),
        bqkv=col(f[L3 + "b_qkv"]), bo3=col(f[L3 + "b_out"]), m3b1=col(f["L3_ffn_b1"].reshape(-1)),
        m3b2=col(f["L3_ffn_b2"].reshape(-1)), gb3=row(f["L3_ffn_gate_b"]), bv3=row(f[L3 + "b_qkv"][256:384]))

    def moe(w1, w2):
        e = w1.shape[0]
        return np.concatenate([w1.transpose(1, 0, 2).reshape(128, -1),
                               w2.reshape(e, -1, 128, 128).transpose(2, 0, 1, 3).reshape(128, -1)], 1)

    c = constants()
    arrays = {
        "xT": f["L0_attn_x"].reshape(NB, NC, C, 128).transpose(3, 1, 0, 2).reshape(128, T),
        "early": np.concatenate([w[n] for n, _ in EARLY] + [c[n] for n, _ in ECONSTS], 1),
        "wts": np.concatenate([w[n] for n, _ in WEIGHTS], 1),
        "bia": np.concatenate([b[n] for n, _ in BIASES], 1),
        "con": np.concatenate([c[n] for n, _ in CONSTS], 1),
        "m1": moe(f["L1_ffn_ew1"], f["L1_ffn_ew2"]),
        "m2": moe(f["L2_ffn_W1"], f["L2_ffn_W2"]),
        "m3": moe(f["L3_ffn_w1"], f["L3_ffn_w2"]),
    }
    arrays = {k: np.ascontiguousarray(v, dtype=np.float32) for k, v in arrays.items()}
    nc = bacc.Bacc("TRN2", target_bir_lowering=False, num_devices=1)
    args = [nc.dram_tensor(k, v.shape, F32, kind="ExternalInput").ap() for k, v in arrays.items()]
    args.append(nc.dram_tensor("outT", (128, T), F32, kind="ExternalOutput").ap())
    program(nc, *args)
    r = run(nc, [arrays], core_ids=[0])
    return np.ascontiguousarray(r.results[0]["outT"].T).reshape(NB, S, 128)
```

```python
from contextlib import ExitStack

import numpy as np
import concourse.bass as bass
from concourse import mybir

ALU = mybir.AluOpType
ACT = mybir.ActivationFunctionType
F32 = mybir.dt.float32
I32 = mybir.dt.int32
BF16 = mybir.dt.bfloat16
AX = mybir.AxisListType.X

T = 4096
NB, S = 16, 256
TW = 512
NT = T // TW
C = 8
NC = S // C

EARLY = [
    ("wk", 128), ("wq", 128), ("wv", 128), ("wout", 128), ("f1", 512), ("f2", 512),
    ("q1", 128), ("k1", 128), ("v1", 128), ("o1", 128), ("w11", 256), ("w12", 256),
    ("gw1", 4), ("dw1", 64), ("dw2", 1),
]
WEIGHTS = [
    ("wi", 128), ("wl1", 128), ("wl2", 128), ("memT", 128), ("wo2", 128), ("wg", 256),
    ("w21", 512), ("w22", 512), ("gw2", 8), ("ws1", 512), ("ws2", 512), ("pT", 10),
    ("qkv", 384), ("w3o", 128), ("gw3", 8), ("b2r", 128),
]
BIASES = [
    ("nw", 1), ("eta", 1), ("f1b", 4), ("f2b", 1),
    ("g1", 1), ("b1n", 1), ("ob1", 1), ("fg1", 1), ("fb1", 1), ("b11", 2), ("b12", 1),
    ("gb1", 4), ("db1", 1), ("db2", 1), ("eb1", 8), ("eb2", 4),
    ("memb", 1), ("bi", 1), ("bl1", 1), ("bl2", 1), ("bo2", 1), ("fgate", 1), ("lrate", 1), ("bg", 1),
    ("b21", 4), ("b22", 1), ("g21", 1), ("be21", 1), ("g22", 1), ("be22", 1), ("g23", 1), ("be23", 1),
    ("m2b1", 32), ("m2b2", 8), ("bs1", 4), ("bs2", 1),
    ("bqkv", 3), ("bo3", 1), ("m3b1", 32), ("gb3", 8), ("bv3", 128),
]
CONSTS = [
    ("ident", 128), ("one", 128), ("mean", 128), ("blk", 128), ("hid", 16),
    ("oneh", 8), ("g8", 128), ("s8", 128), ("tri", 128), ("bd8", 128),
    ("rm", 4), ("lt", 128), ("band", 160), ("band0", 128), ("eps5", 1), ("eps6", 1), ("zero", 1),
    ("rselA", 128), ("pairm", 8), ("desc", 8), ("colr", 512), ("par", 128), ("i40", 40), ("pcol", 1),
]
ECONSTS = [("sel", 1024), ("dq", 256), ("dk", 256)]


def offsets(table):
    at, n = {}, 0
    for name, w in table:
        at[name] = (n, w)
        n += w
    return at, n


WAT, NW = offsets(WEIGHTS)
EAT, NE = offsets(EARLY + ECONSTS)
BAT, NBI = offsets(BIASES)
CAT, NCO = offsets(CONSTS)


def constants():
    p = np.arange(128)
    c = {}
    c["ident"] = np.eye(128)
    c["one"] = np.ones((128, 128))
    c["mean"] = np.full((128, 128), 1.0 / 128)
    c["blk"] = (p[:, None] // C == p[None, :] // C)
    c["sel"] = np.concatenate([(p[:, None] == (p[None, :] // C) * C + s) for s in range(C)], 1)
    c["hid"] = (p[:, None] // C == np.arange(16)[None, :])
    c["oneh"] = (p[:, None] % C == np.arange(C)[None, :])
    c["g8"] = (p[:, None] // 8 == p[None, :] // 8) / 8.0
    c["s8"] = (p[:, None] // 8 == p[None, :] // 8)
    gam = 1.0 - np.exp(np.linspace(np.log(1 / 32.0), np.log(1 / 512.0), 16)).astype(np.float32).astype(np.float64)
    g = gam[p // 8][:, None]
    t = np.arange(256)[None, :]
    c["dq"] = g ** (t - 128.0)
    c["dk"] = g ** (128.0 - t) / np.sqrt(8.0)
    c["tri"] = (p[None, :] >= p[:, None])
    c["bd8"] = (p[:, None] // 8 == p[None, :] // 8)
    c["rm"] = ((p[:, None] % 32) // 8 == np.arange(4)[None, :])
    c["lt"] = (p[:, None] < p[None, :])
    q, k = p[:, None], np.arange(160)[None, :] - 32
    c["band"] = np.where((k <= q) & (k >= q - 16), 0.0, -1e30)
    k = np.arange(128)[None, :]
    c["band0"] = np.where((k <= q) & (k >= q - 16), 0.0, -1e30)
    c["eps5"] = np.full((128, 1), 1e-5)
    c["eps6"] = np.full((128, 1), 1e-6)
    c["zero"] = np.zeros((128, 1))
    c["rselA"] = ((p[:, None] // C) % 2 == p[None, :] // 64) & (p[:, None] % C == 0)
    c["pairm"] = (p[:, None] // 16 == np.arange(8)[None, :])
    c["desc"] = np.tile(8.0 - np.arange(8), (128, 1))
    c["par"] = (p[:, None] // 64 == (p[None, :] // C) % 2)
    c["i40"] = np.tile(np.arange(40)[None, :], (128, 1))
    c["pcol"] = p[:, None]
    c["colr"] = np.tile(np.concatenate([(p // 8) % 4 == r for r in range(4)])[None, :], (128, 1))
    c["colr"] = np.tile(c["colr"], 1)
    return {n: np.asarray(a, np.float32) for n, a in c.items()}


class Eng:

    def __init__(self, sem):
        self.sem, self.n, self.items = sem, 0, []

    def __call__(self, fn, *waits):
        self.items.append((fn, flat(waits), True))
        self.n += 1
        return (self.sem, self.n)

    def chain(self, fn, *waits):
        return self(fn, (self.sem, self.n), *waits)

    def last(self):
        return (self.sem, self.n)

    def dma(self, fn, tok, *waits):
        self.items.append((lambda e: fn(e).then_inc(tok[0], 16), flat(waits), False))

    def play(self, eng):
        seen = {}
        for fn, waits, counted in self.items:
            for sem, v in waits:
                if v > seen.get(id(sem), 0):
                    eng.wait_ge(sem, v)
                    seen[id(sem)] = v
            r = fn(eng)
            if counted:
                r.then_inc(self.sem, 1)


def flat(waits):
    out = []
    for w in waits:
        if isinstance(w, list):
            out += flat(w)
        elif w is not None:
            out.append(w)
    return out


class Ring:

    def __init__(self, ids):
        self.idle = [(k, []) for k in ids]
        self.n = len(self.idle)

    def get(self):
        return self.idle.pop(0)

    def free(self, k, *toks):
        self.idle.append((k, list(toks)))

    def reset(self):
        assert len(self.idle) == self.n
        self.idle = [(k, []) for k, _ in sorted(self.idle)]


def pipe(gens, depth):
    gens = iter(gens)
    live = []
    while True:
        if len(live) < depth:
            g = next(gens, None)
            if g is not None:
                live.append(g)
        if not live:
            return
        for g in list(live):
            if next(g, 1) is not None:
                live.remove(g)


def program(nc, xT, early, wts, bia, con, m1, m2, m3, outT):
    with ExitStack() as ctx:
        def sb(name, shape, dt=F32):
            return ctx.enter_context(nc.sbuf_tensor(name, shape, dt))

        def sem(name):
            return ctx.enter_context(nc.semaphore(name))

        A, V, G, P, SP = (Eng(sem("s_" + n)) for n in ("act", "dve", "pool", "pe", "sp"))
        BIG = [sb(f"big{i}", [128, T]) for i in range(8)]
        WT = sb("wt", [128, NW])
        BI = sb("bi", [128, NBI])
        CO = sb("co", [128, NCO])
        MW = sb("mw", [128, 8192])
        TMP = sb("tmp", [128, 9, TW])
        SM = sb("sm", [128, 1100])
        PS = ctx.enter_context(nc.psum_tensor("ps", [128, 8, 512], F32))

        def W(n, a=0, b=None):
            if n in EAT:
                o, w = EAT[n]
                return MW[:, 2048 + o + a:2048 + o + (w if b is None else b)]
            o, w = WAT[n]
            return WT[:, o + a:o + (w if b is None else b)]

        def B(n, a=0, b=None):
            o, w = BAT[n]
            return BI[:, o + a:o + (w if b is None else b)]

        def K(n, a=0, b=None):
            if n in EAT:
                return W(n, a, b)
            o, w = CAT[n]
            return CO[:, o + a:o + (w if b is None else b)]

        smat = [0]

        def small(n):
            a = smat[0]
            smat[0] += n
            assert smat[0] <= 1100
            return SM[:, a:a + n]

        PB = Ring(range(8))
        TB = Ring(range(9))
        RST = small(32)
        RR = Ring(range(8))

        def mm(out, lhsT, rhs, start=True, stop=True):
            return lambda e: e.matmul(out, lhsT, rhs, start=start, stop=stop)

        def mms(*fs):
            def go(e):
                for f in fs:
                    r = f(e)
                return r
            return go

        def act(out, in_, f, scale=1.0, bias=None, **kw):
            if f == ACT.Copy:
                return lambda e: e.activation(out, in_, f, scale=scale, **kw)
            return lambda e: e.activation(out, in_, f, bias=K("zero")[0:out.shape[0], :] if bias is None else bias,
                                          scale=scale, **kw)

        def tt(out, a, b, op):
            return lambda e: e.tensor_tensor(out, a, b, op)

        def ts(out, a, s1, s2, op0, op1=None):
            if op1 is None:
                return lambda e: e.tensor_scalar(out, a, s1, None, op0)
            return lambda e: e.tensor_scalar(out, a, s1, s2, op0, op1)

        def stt(out, a, s, b, op0, op1):
            return lambda e: e.scalar_tensor_tensor(out=out, in0=a, scalar=s, in1=b, op0=op0, op1=op1)

        def ttr(out, a, b, acc):
            return lambda e: e.tensor_tensor_reduce(out, a, b, 1.0, 0.0, ALU.mult, ALU.add, acc)

        def red(out, a, op=ALU.add):
            return lambda e: e.tensor_reduce(out, a, AX, op)

        def rcp(out, a):
            return lambda e: e.reciprocal(out, a)

        def tr(out, a):
            n = a.shape[0]
            return lambda e: e.transpose(out, a, K("ident")[0:n, 0:n])

        def cp(out, a):
            return lambda e: e.tensor_copy(out, a)

        MU, AD, SU, MX, MN = ALU.mult, ALU.add, ALU.subtract, ALU.max, ALU.min

        def bar():
            toks = [e.last() for e in (A, V, G, P)]
            for e in (A, V, G, P):
                e.items.append((lambda eng: None, toks, False))
            for r in (PB, TB, RR):
                r.reset()
            return toks

        def sl(t):
            return slice(t * TW, (t + 1) * TW)

        s_x, s_w, s_c, s_m1, s_m2, s_m3 = (sem(n) for n in ("d_x", "d_w", "d_c", "d_m1", "d_m2", "d_m3"))
        X = BIG[1]
        SP.dma(lambda e: e.dma_start(BIG[1][:, :], xT), (s_x, 16))
        SP.dma(lambda e: e.dma_start(CO[:, :], con), (s_c, 16))
        SP.dma(lambda e: e.dma_start(BI[:, :], bia), (s_c, 32))
        SP.dma(lambda e: e.dma_start(MW[:, 2048:2048 + NE], early), (s_c, 48))
        SP.dma(lambda e: e.dma_start(WT[:, :], wts), (s_w, 16))
        SP.dma(lambda e: e.dma_start(MW[:, 0:2048], m1), (s_m1, 16))
        for e in (A, V, G, P):
            e.items.append((lambda eng: None, [(s_x, 16), (s_c, 48), (s_w, 16)], False))

        def rstd_gen(sq, k, eps, mean, res, floor=None, n=TW):
            nb = (n + 127) // 128
            m = min(n, 128)
            b, w = PB.get()
            p = P(mms(*[mm(PS[0:m, b, j:j + 1], TMP[:, k, 128 * j:128 * j + m], K("mean" if mean else "one", 0, 1))
                        for j in range(nb)]), sq, w)
            yield
            kr, w = RR.get()
            r = RST[0:m, 4 * kr:4 * kr + nb]
            a = A(act(r, PS[0:m, b, 0:nb], ACT.Sqrt, bias=None if eps is None else eps[0:m]), p, w)
            yield
            v = V(ts(r, r, floor or 0.0, None, MX), a)
            v = V.chain(rcp(r, r))
            yield
            p = P(mms(*[mm(PS[:, b, 128 * j:128 * j + m], r[:, j:j + 1].broadcast_to((m, 128)), K("ident")[0:m, 0:m])
                        for j in range(nb)]), v)
            RR.free(kr, p)
            TB.free(k, p)
            yield
            res.append((b, p))

        def ln_gen(src, dst, t, eps=None, gb=None, rms=False, wait=()):
            s = sl(t)
            if not rms:
                b, w = PB.get()
                p = P(mm(PS[:, b, :], K("mean"), src[:, s]), w, *wait)
                yield
                v = V(tt(dst[:, s], src[:, s], PS[:, b, :], SU), p)
                PB.free(b, v)
                x = dst
            else:
                v = None
                x = src
            yield
            k, w = TB.get()
            a = A(act(TMP[:, k, :], x[:, s], ACT.Square), v, w, *wait)
            yield
            res = []
            yield from rstd_gen(a, k, K("eps5") if eps is None else eps, True, res)
            b, p = res[0]
            if gb is None:
                v = V(tt(dst[:, s], x[:, s], PS[:, b, :], MU), p, v)
            else:
                v = V(stt(dst[:, s], x[:, s], gb[0], PS[:, b, :], MU, MU), p, v)
            PB.free(b, v)
            if gb is not None and len(gb) == 2:
                yield
                A(act(dst[:, s], dst[:, s], ACT.Identity, bias=gb[1]), v)

        def lin_gen(t, dst, w, src, f, bias=None, scale=1.0):
            b, wt = PB.get()
            p = P(mm(PS[:, b, :], w, src[:, sl(t)]), wt)
            yield
            a = A(act(dst[:, sl(t)], PS[:, b, :], f, bias=bias, scale=scale), p)
            PB.free(b, a)

        def ffn_gen(t, src, w1, b1, nh, func, w2, fin):
            bo, wo = PB.get()
            hs = []
            for j in range(nh):
                b, w = PB.get()
                p = P(mm(PS[:, b, :], w1(j), src[:, sl(t)]), w)
                yield
                k, w = TB.get()
                a = A(act(TMP[:, k, :], PS[:, b, :], func, bias=b1(j)), p, w)
                PB.free(b, a)
                hs.append((j, k, a))
                if len(hs) == 2:
                    jj, kk, aa = hs.pop(0)
                    p = P(mm(PS[:, bo, :], w2(jj), TMP[:, kk, :], start=(jj == 0), stop=False), aa, wo)
                    TB.free(kk, p)
            jj, kk, aa = hs.pop(0)
            p = P(mm(PS[:, bo, :], w2(jj), TMP[:, kk, :], start=(jj == 0), stop=True), aa, wo)
            TB.free(kk, p)
            yield
            tok = fin(bo, p)
            PB.free(bo, tok)

        VT, X, XN, XR, KB, EK, Q, U8 = BIG
        pipe((ln_gen(X, XN, t) for t in range(NT)), 4)
        bar()
        pipe((ln_gen(XN, XR, t, eps=K("eps6"), gb=[B("nw")], rms=True) for t in range(NT)), 4)
        etac = small(1)
        V(ts(etac, B("eta"), -1.0, None, MU))
        V.chain(tt(etac, etac, B("eta"), MX))
        V.chain(ts(etac, etac, 1e-6, None, MX))
        bar()

        def phi_gen(t, dst, w, edst=None):
            b, wt = PB.get()
            p = P(mm(PS[:, b, :], w, XR[:, sl(t)]), wt)
            yield
            k, w_ = TB.get()
            v = V(ts(TMP[:, k, :], PS[:, b, :], 0.0, None, MN), p, w_)
            yield
            a = A(act(TMP[:, k, :], TMP[:, k, :], ACT.Exp), v)
            yield
            v = V(stt(dst[:, sl(t)], PS[:, b, :], 0.0, TMP[:, k, :], MX, AD), a)
            PB.free(b, v)
            TB.free(k, v)
            if edst is not None:
                V.chain(ts(edst[:, sl(t)], dst[:, sl(t)], etac, None, MU))

        pipe([g for t in range(NT) for g in (phi_gen(t, KB, W("wk"), EK), phi_gen(t, Q, W("wq")),
                                              lin_gen(t, VT, W("wv"), XR, ACT.Copy))], 4)

        qs = small(8)
        q2 = TMP[:, 8, :]
        for n, j in (("f1", 0), ("f2", 1)):
            V.chain(ts(q2, W(n), -1.0, None, MU))
            V.chain(tt(q2, q2, W(n), MX))
            V.chain(red(qs[:, j:j + 1], q2))
        bar()
        b, w = PB.get()
        p = P(mm(PS[:, b, 0:2], K("one"), qs[:, 0:2]))
        PB.free(b)
        V(ts(qs[:, 2:4], PS[:, b, 0:2], 1.0 / 65536, 1e-5, MU, AD), p)
        V.chain(rcp(qs[:, 4:6], qs[:, 2:4]))
        RND = 12582912.0
        for n, j in (("f1", 0), ("f2", 1)):
            V.chain(ts(W(n), W(n), qs[:, 4 + j:5 + j], None, MU))
            V.chain(ts(W(n), W(n), 1.5, -1.5, MN, MX))
            V.chain(ts(W(n), W(n), RND, None, AD))
            V.chain(ts(W(n), W(n), -RND, None, AD))
            V.chain(ts(W(n), W(n), 1.0, -1.0, MN, MX))
        bar()

        def fin0(t):
            def f(b, p):
                V(stt(X[:, sl(t)], PS[:, b, :], B("f2b"), X[:, sl(t)], AD, AD), p)
                return V.chain(tt(X[:, sl(t)], X[:, sl(t)], XN[:, sl(t)], AD))
            return f

        pipe((ffn_gen(t, XN, lambda j: W("f1", 128 * j, 128 * j + 128), lambda j: B("f1b", j, j + 1), 4, ACT.Relu,
                      lambda j: W("f2", 128 * j, 128 * j + 128), fin0(t)) for t in range(NT)), 2)
        bar()

        def cv(buf, c, r=slice(0, 128)):
            return buf[r, 128 * c:128 * c + 128]

        U = BIG[7]
        Mst = U[:, 0:1024].rearrange("p (a d) -> p a d", a=8)
        Mun = U[:, 1024:2048].rearrange("p (a d) -> p a d", a=8)
        EKBL = U[:, 2048:3072].rearrange("p (a h f) -> p a h f", a=8, h=2)
        RT = [U[:, 3072:3776].rearrange("p (j x) -> p j x", j=8), TMP[:, 0:2, :].rearrange("p a n -> p (a n)")[:, 0:704]
              .rearrange("p (j x) -> p j x", j=8)]
        EXP = TMP[:, 2:4, :].rearrange("p a n -> p (a n)")[:, 0:704].rearrange("p (j x) -> p j x", j=8)
        vch = [TMP[:, 4, 0:128], TMP[:, 4, 128:256]]
        vw = TMP[:, 4, 256:384]
        sqp = TMP[:, 4, 384:512]
        pT = TMP[:, 5, 0:256].rearrange("p (k n) -> p k n", k=2)
        mk = TMP[:, 5, 256:384]
        mk2 = TMP[:, 5, 384:512]
        SC = [TMP[:, 6 + i, :] for i in range(2)]
        grm = TMP[:, 8, 0:384]
        q64 = TMP[:, 8, 384:448]
        q64b = TMP[:, 8, 448:512]

        KEM = [XN[:, 256 * i:256 * i + 256].rearrange("p (k n) -> p k n", k=2) for i in range(2)]

        def sv(i):
            o = SC[i]
            return dict(ek=o[:, 0:64], kap=o[:, 64:65], eb=o[:, 65:66], vs=o[:, 66:67], c=o[:, 67:68],
                        G=o[:, 68:92], e1=o[:, 92:172], rep=o[:, 172:252], B=o[:, 252:260], F=o[:, 260:268],
                        x=o[:, 268:356], t8=o[:, 356:364], kapn=o[:, 364:365], nB=o[:, 365:373],
                        K3=o[:, 373:400], C2=o[:, 400:424], d8=o[:, 424:432], u8=o[:, 432:440])

        st = small(64)
        Pst, qst, rP, mst, rR, wc = (st[:, i:i + 1] for i in range(6))
        Xv, Yv, zz1 = st[:, 6:9], st[:, 9:12], st[:, 12:13]
        C1v, C0v, Av = st[:, 13:16], st[:, 16:19], st[:, 19:20]
        tmp8, al = st[:, 20:28], st[:, 28:36]
        km, sg, al0, g0, b0 = (st[:, i:i + 1] for i in range(36, 41))
        pv, L8 = st[:, 41:49], st[:, 49:57]
        x11 = small(11)
        ex11 = small(88)
        dt = small(88)
        dt3 = dt.rearrange("p (j x) -> p j x", x=11)
        rp8 = small(8)
        Rc = small(8)
        Wst = small(8)
        sg3 = small(3)
        one8_ = K("oneh")
        V(lambda e: e.memset(Mst, 0.0))
        V(lambda e: e.memset(st, 0.0))
        V.chain(lambda e: e.memset(Pst, 1.0))
        V.chain(lambda e: e.memset(rR, 1.0))
        V(lambda e: e.memset(sg3[:, 0:1], 0.0))
        V(lambda e: e.memset(sg3[:, 1:2], 1.0))
        V(lambda e: e.memset(sg3[:, 2:3], -1.0))
        bar()

        def outer(a, n, b, m):
            return (a.rearrange("p (x y) -> p x y", y=1).broadcast_to((128, n, m)),
                    b.rearrange("p (x y) -> p x y", x=1).broadcast_to((128, n, m)))

        def prep(c):
            i = c % 2
            s = sv(i)
            lo = slice(0, 64)
            old = prep.old.get(i, [])
            p1 = P(mm(PS[:, 0, 0:128], cv(KB, c, lo), cv(EK, c, lo)), prep.b[0])
            yield
            P(mm(PS[:, 0, 128:256], cv(EK, c, lo), cv(EK, c, lo)))
            p1 = P(mm(PS[:, 0, 256:384], cv(VT, c), cv(VT, c)))
            yield
            px = None
            if c:
                px = P(mms(mm(PS[:, 5, 0:128], cv(EK, c - 1, lo), cv(KB, c, lo)),
                           mm(PS[:, 5, 128:256], cv(EK, c - 1, lo), cv(EK, c, lo))), prep.rc)
            p2 = P(mms(mm(PS[:, 1, 0:128], cv(XR, c), W("wv")),
                       mm(PS[:, 1, 128:192], cv(EK, c, lo), K("ident")[0:64, 0:64]),
                       mm(PS[:, 1, 192:193], cv(KB, c, lo), K("one")[0:64, 0:1]),
                       mm(PS[:, 1, 193:194], cv(EK, c, lo), K("mean")[0:64, 0:1]),
                       mm(PS[:, 1, 194:195], cv(VT, c), K("one")[:, 0:1])), prep.b[1])
            yield
            vv = V(tt(grm.rearrange("p (k b s) -> p k b s", k=3, b=NB),
                      PS[:, 0, 0:384].rearrange("p (k b s) -> p k b s", k=3, b=NB),
                      K("hid").rearrange("p (k b s) -> p k b s", k=1, s=1).broadcast_to((128, 3, NB, C)), MU), p1)
            prep.b[0] = [vv]
            yield
            for k_, buf in ((0, KB), (1, EK)):
                prep.kem[c] = G.chain(tt(KEM[i][:, k_, :], cv(buf, c), K("par"), MU), old)
            yield
            a1 = A(act(vch[i], PS[:, 1, 0:128], ACT.Copy), p2, old)
            yield
            a2 = A(act(SC[i][:, 0:67], PS[:, 1, 128:195], ACT.Copy), p2, old)
            prep.b[1] = [a2]
            yield
            if c:
                prep.xm = V(tt(XM, PS[:, 5, 0:256].rearrange("p (k n) -> p k n", k=2),
                               K("blk").rearrange("p (k n) -> p k n", k=1).broadcast_to((128, 2, 128)), MU), px)
            v = V(red(s["G"].rearrange("p (k s) -> p k s", k=3),
                      grm.rearrange("p (k b s) -> p k s b", k=3, b=NB)), vv, old)
            gk, gg, gv = s["G"][:, 0:8], s["G"][:, 8:16], s["G"][:, 16:24]
            g = G(tt(s["c"], s["eb"], s["vs"], MU), a2)
            g = G.chain(ts(s["c"], s["c"], 2.0 / 128, None, MU))
            g = G.chain(ts(s["kapn"], s["kap"], -1.0, None, MU))
            g = G.chain(ts(s["e1"][:, 0:8], one8_, s["c"], None, MU))
            g = G.chain(ts(s["e1"][:, 8:16], one8_, s["vs"], None, MU))
            yield
            g = G.chain(tt(s["e1"][:, 16:80].rearrange("p (x y) -> p x y", x=8), *outer(one8_, 8, gv, 8), MU), v)
            p = P(mm(PS[:, 1, 256:336], K("blk"), s["e1"]), g, a2)
            yield
            a = A(act(s["rep"], PS[:, 1, 256:336], ACT.Copy), p)
            prep.b[1] = [a]
            yield
            crep, vrep, vvr = s["rep"][:, 0:8], s["rep"][:, 8:16], s["rep"][:, 16:80]
            g = G.chain(ts(s["B"], crep, s["kap"], None, MU), a)
            g = G.chain(ts(s["nB"], s["B"], -1.0, None, MU))
            g = G.chain(tt(s["F"], gk, vrep, MU))
            g = G.chain(ts(s["t8"], s["B"], -64.0, None, MU))
            g = G.chain(tt(s["F"], s["F"], s["t8"], AD))
            yield
            x2 = lambda ap: ap.rearrange("p (x y) -> p x y", x=8)
            xq, xn, xb, xc = s["x"][:, 0:64], s["x"][:, 64:72], s["x"][:, 72:80], s["x"][:, 80:88]
            g = G.chain(tt(x2(q64), *outer(gk, 8, gk, 8), MU))
            g = G.chain(tt(q64, q64, vvr, MU))
            g = G.chain(tt(x2(q64b), *outer(s["F"], 8, s["nB"], 8), MU))
            g = G.chain(tt(q64, q64, q64b, AD))
            yield
            g = G.chain(tt(x2(q64b), *outer(s["nB"], 8, s["F"], 8), MU))
            g = G.chain(tt(q64, q64, q64b, AD))
            g = G.chain(ts(xq, q64, 2.0, None, MU))
            g = G.chain(lambda e: e.tensor_copy(xn, q64[:, 0:64:9]))
            yield
            g = G.chain(tt(s["t8"], gk, gv, MU))
            g = G.chain(ts(xb, s["nB"], s["vs"], None, MU))
            g = G.chain(tt(xb, xb, s["t8"], AD))
            g = G.chain(ts(xb, xb, -2.0, None, MU))
            g = G.chain(tt(s["t8"], gg, gv, MU))
            g = G.chain(ts(s["t8"], s["t8"], 2.0 / 8192, None, MU))
            g = G.chain(ts(xc, crep, s["c"], None, MU))
            g = G.chain(ts(xc, xc, -2.0, None, MU))
            g = G.chain(tt(xc, xc, s["t8"], AD))
            yield
            g = G.chain(tt(EXP, *outer(one8_, 8, s["x"], 88), MU), prep.b[2])
            yield
            K3 = s["K3"].rearrange("p (t x) -> p t x", x=3)
            C2 = s["C2"].rearrange("p (t x) -> p t x", x=3)
            g = G.chain(lambda e: e.tensor_copy(K3[:, 0:8, 0], K("one")[:, 0:8]))
            g = G.chain(lambda e: e.tensor_copy(K3[:, 0:7, 1], vvr[:, 9:64:9]))
            g = G.chain(ts(K3[:, 0:7, 2], vvr[:, 9:64:9], -1.0, None, MU))
            prep.ready0[c] = [g, a, v]
            yield "rest"
            e_ = EXP.rearrange("p j x -> p (j x)")
            p = None
            for h in range(2):
                p = P(mm(PS[:, 2 + h, 0:352], K("blk"), e_[:, 352 * h:352 * h + 352]), g)
            yield
            for h in range(4):
                a = A(act(RT[i].rearrange("p j x -> p (j x)")[:, 176 * h:176 * h + 176],
                          PS[:, 2 + h // 2, 176 * (h % 2):176 * (h % 2) + 176], ACT.Copy), p, old)
                yield
            prep.b[2] = [p, a]
            rf = RT[i].rearrange("p j x -> p (j x)")
            g = G.chain(ts(s["d8"], rf[:, 80:704:89], 0.5, None, MU), a)
            yield
            g = G.chain(lambda e: e.tensor_copy(s["u8"][:, 0:7], rf[:, 88 + 64:704:89]))
            g = G.chain(tt(C2[:, 0:7, :], K3[:, 0:7, :],
                           s["d8"][:, 0:7].rearrange("p (t x) -> p t x", x=1).broadcast_to((128, 7, 3)), MU))
            g = G.chain(tt(C2[:, 0:7, 1], C2[:, 0:7, 1], s["u8"][:, 0:7], AD))
            g = G.chain(tt(C2[:, 0:7, 2], C2[:, 0:7, 2], s["u8"][:, 0:7], SU))
            g = G.chain(lambda e: e.tensor_copy(C2[:, 7, 0:1], s["d8"][:, 7:8]))
            prep.ready[c] = [g, a, v]

        prep.old = {}
        prep.b = {0: [], 1: [], 2: []}
        prep.ready = {}
        prep.ready0 = {}
        prep.kem = {}
        prep.rc = []
        XM = MW[:, 6400:6656].rearrange("p (k n) -> p k n", k=2)
        for _ in prep(0):
            pass
        gM, gE, vwt, prp, pu = None, None, None, None, None

        def keys(c, done):
            kem = KEM[c % 2]
            o = PS[:, 4, 0:256].rearrange("p (k n) -> p k n", k=2)
            return P(mms(*[mm(o[:, :, 16 * a_:16 * a_ + 16], Mst[:, a_, :], kem[:, :, 16 * a_:16 * a_ + 16],
                              start=done or a_ == 0, stop=done)
                           for a_ in range(8)]), prep.kem[c], gM)

        def update():
            return [P(mms(*[mm(PS[:, 6 + h, (a_ % 4) * 128:(a_ % 4) * 128 + 128],
                               EKBL[:, a_].rearrange("p h f -> p (h f)"), vw) for a_ in range(4 * h, 4 * h + 4)]),
                      gE, vwt, V.last()) for h in range(2)]

        def added(h):
            return V(tt(Mun[:, 4 * h:4 * h + 4, :], Mst[:, 4 * h:4 * h + 4, :],
                        PS[:, 6 + h, :].rearrange("p (a d) -> p a d", a=4), AD), pu[h], gM)

        def scaled(w):
            return G(tt(Mst, Mun, Rc.rearrange("p (a d) -> p a d", d=1).broadcast_to((128, 8, 128)), MU), w)

        P_, q_ = Pst, qst
        ahead = iter(())
        for c in range(NC):
            i = c % 2
            s = sv(i)
            rest = ahead
            ahead = prep(c + 1) if c + 1 < NC else iter(())
            held = c + 1 == NC
            rdy = prep.ready0[c]
            crep, vrep, vvr = s["rep"][:, 0:8], s["rep"][:, 8:16], s["rep"][:, 16:80]
            K3 = s["K3"].rearrange("p (t x) -> p t x", x=3)
            C2 = s["C2"].rearrange("p (t x) -> p t x", x=3)
            ps4 = PS[:, 4, 0:256].rearrange("p (k n) -> p k n", k=2)
            if c == 0:
                p = keys(0, True)
            else:
                p = P(mm(PS[:, 4, 0:256], vw, XM.rearrange("p k n -> p (k n)"), start=False, stop=True), vwt, prep.xm)
            a = A(act(pT, ps4, ACT.Copy), p)
            p1 = P(mms(mm(PS[:, 6, 0:128], pT[:, 0, :], cv(VT, c)), mm(PS[:, 6, 256:257], pT[:, 0, :], K("one")[:, 0:1])), a)
            a = A(act(sqp, pT[:, 0, :], ACT.Square), a)
            p2 = P(mm(PS[:, 6, 128:256], pT[:, 1, :], cv(VT, c)))
            p3 = P(mm(PS[:, 7, 0:1], sqp, K("one")[:, 0:1]), a)
            p1 = p2
            for _ in rest:
                pass
            tables = prep.ready[c]
            v = V(tt(km, mst, s["kap"], MU), rdy, V.last())
            v = V(tt(mk.rearrange("p (b s) -> p b s", b=NB), PS[:, 6, 0:128].rearrange("p (b s) -> p b s", b=NB),
                     K("hid").rearrange("p (b s) -> p b s", s=1).broadcast_to((128, NB, C)), MU), p1)
            vk = V.chain(red(pv, mk.rearrange("p (b s) -> p s b", b=NB)))
            vg = V(ttr(mk2, PS[:, 6, 128:256], K("ident"), g0), p2)
            v = V(ts(tmp8, vrep, km, None, MU), vk)
            va = V(ts(al0, PS[:, 6, 256:257], -2.0, None, MU), p1)
            v = V(tt(pv, pv, tmp8, SU), v)
            va = V(stt(al0, km, 128.0, al0, MU, AD), va)
            vs_ = V(stt(sg, km, -128.0, PS[:, 6, 256:257], MU, AD), p1)
            vL = V(tt(L8, s["G"][:, 0:8], pv, MU), v)
            va = V(stt(al0, al0, km, PS[:, 7, 0:1], MU, AD), va, p3)
            vb = V(ttr(tmp8, pv, one8_, b0), vL)
            vL = V(stt(L8, s["nB"], sg, L8, MU, AD), vs_, vL)
            vg = V(ts(g0, g0, 1.0 / 8192, None, MU), vg)
            vx = V(ts(x11[:, 0:8], L8, 2.0, None, MU), vL)
            v = V(tt(wc, s["c"], mst, MU), rdy)
            va = V(ts(x11[:, 8:9], al0, rR, None, MU), va)
            vb = V(ts(x11[:, 9:10], b0, -2.0, None, MU), vb)
            vg = V(tt(g0, g0, wc, SU), v, vg)
            v = V(ts(mst, mst, rR, None, MU), vg)
            vg = V(ts(x11[:, 10:11], g0, 2.0, None, MU), vg)
            v = V(ts(x11, x11, rR, None, MU), vx, va, vb, vg)
            v = V.chain(tt(ex11.rearrange("p (x y) -> p x y", x=8), *outer(one8_, 8, x11, 11), MU))
            p = P(mm(PS[:, 7, 16:104], K("blk"), ex11), v)
            v = V(cp(dt, PS[:, 7, 16:104]), p)
            vF = V(tt(Yv[:, 1:2], dt[:, 8:9], vvr[:, 0:1], AD), v)
            vA = V(ts(Av, qst, 1e-5, None, AD))
            vC = V(ts(C1v, K3[:, 0, :], dt3[:, 0, 10:11], None, MU), v)
            vN = V(ts(Yv[:, 2:3], Yv[:, 1:2], -1.0, None, MU), vF)
            vD = V(ts(C0v, K3[:, 0, :], Av, None, MU), vA)
            vC = V(stt(C1v, sg3, dt3[:, 1, 0:1], C1v, MU, AD), vC)
            vz = V(tt(zz1, dt3[:, 0, 9:10], Yv[:, 2:3], MX), vN)
            vD = V(stt(C0v, sg3, dt3[:, 1, 8:9], C0v, MU, AD), vD)
            aw = A(act(Wst[:, 0:1], zz1, ACT.Sqrt, bias=Yv[:, 1:2]), vz)
            vR = v = V(ts(rp8, K("pairm"), rR, None, MU), prp)
            if c:
                prp = pr = P(mm(PS[:, 5, 256:264], K("rselA"), rp8), v)
                pu = update()
            for t in range(C):
                w_ = Wst[:, t:t + 1]
                last = t == C - 1
                m = 1 if last else 3
                vX = V(stt(Xv[:, 0:m], C2[:, t, 0:m], w_, C1v[:, 0:m], MU, AD), aw, vC, tables)
                if not last:
                    vd = V(stt(dt3[:, t + 1:8, 9:11], RT[i][:, t + 1:8, 72 + t:88:8], w_, dt3[:, t + 1:8, 9:11], MU, AD), aw)
                vY = V(stt(Yv[:, 0:m], Xv[:, 0:m], w_, C0v[:, 0:m], MU, AD), vX, vD)
                ar = A(act(rP, Yv[:, 0:1], ACT.Sqrt), vY)
                if not last:
                    va = V(stt(tmp8[:, 0:7 - t], RT[i][:, t + 1:8, 64 + t], w_, dt3[:, t + 1:8, t], MU, AD), aw)
                vq = V(stt(qst, Xv[:, 0:1], w_, qst, MU, AD), vX)
                if last:
                    break
                va = V(stt(dt3[:, t + 1:8, 8], tmp8[:, 0:7 - t], w_, dt3[:, t + 1:8, 8], MU, AD), va)
                vz = V(stt(zz1, dt3[:, t + 1, 9:10], rP, Yv[:, 2:3], MU, MX), vd, vY, ar)
                aw = A(act(Wst[:, t + 1:t + 2], zz1, ACT.Sqrt, bias=Yv[:, 1:2]), vz)
                vA = V(stt(Av, Yv[:, 0:1], 1e-5, qst, MU, AD), vY, vq)
                m = 1 if t + 1 == C - 1 else 3
                vC = V(ts(C1v[:, 0:m], K3[:, t + 1, 0:m], dt3[:, t + 1, 10:11], None, MU), vd, vX)
                if m == 3:
                    vT = V(stt(dt3[:, t + 2:8, t + 1:8], RT[i][:, t + 2:8, 8 * t + t + 1:8 * t + 8], w_,
                               dt3[:, t + 2:8, t + 1:8], MU, AD), va)
                vD = V(ts(C0v[:, 0:m], K3[:, t + 1, 0:m], Av, None, MU), vA)
                if m == 3:
                    vC = V(stt(C1v, sg3, dt3[:, t + 2, t + 1:t + 2], C1v, MU, AD), vC, vT)
                    vD = V(stt(C0v, sg3, dt3[:, t + 2, 8:9], C0v, MU, AD), vD, va)
                if c and t == 0:
                    v = V(cp(Rc, PS[:, 5, 256:264]), pr, gM)
                    prep.rc = [v]
                if c and t in (3, 4):
                    mtok = added(t - 3)
                if c and t == 4:
                    gM = scaled(mtok)
                for _ in range(3):
                    held = held or next(ahead) == "rest"
            while not held:
                held = next(ahead) == "rest"
            gE = G(tt(EKBL.rearrange("p a h f -> p (a h) f"),
                      s["ek"].rearrange("p (a f) -> p a f", a=1).broadcast_to((128, 16, 64)),
                      K("hid").rearrange("p (a f) -> p a f", f=1).broadcast_to((128, 16, 64)), MU), rdy, pu)
            if c + 1 < NC:
                keys(c + 1, False)
            v = V(ttr(rp8, Wst, one8_, wc), aw, prp)
            vwt = v = V.chain(ts(vw, vch[i], wc, None, MU))
            v = V(ttr(tmp8, Wst, crep, wc), v)
            v = V.chain(tt(mst, mst, wc, AD))
            v = V(rcp(rR, rP), ar)
            v = V.chain(tt(qst, qst, rR, MU))
            v = V.chain(tt(qst, qst, rR, MU))
            prep.old[i] = [vwt, V.last(), G.last(), P.last()]
        v = V(ts(rp8, K("pairm"), rR, None, MU), prp)
        pr = P(mm(PS[:, 5, 256:264], K("rselA"), rp8), v)
        pu = update()
        v = V(cp(Rc, PS[:, 5, 256:264]), pr, gM)
        added(0)
        mtok = added(1)
        v = V.chain(tt(Mst, Mun, Rc.rearrange("p (a d) -> p a d", d=1).broadcast_to((128, 8, 128)), MU))
        v = V.chain(ts(mst, mst, rR, None, MU))
        mtok = v
        b2 = V(ts(rp8, K("pairm"), mst, None, MU), mtok, pr)
        pr = P(mm(PS[:, 5, 256:264], K("rselA"), rp8), b2)
        v = V(cp(Rc, PS[:, 5, 256:264]), pr, gM)
        v = V.chain(tt(Mst, Mst, Rc.rearrange("p (a d) -> p a d", d=1).broadcast_to((128, 8, 128)), SU))
        bar()

        def mo_gen(b_):
            h = slice(64 * (b_ % 2), 64 * (b_ % 2) + 64)
            c0 = slice(b_ * S, (b_ + 1) * S)
            b, w = PB.get()
            p = P(mm(PS[:, b, 0:256], Mst[h, b_ // 2, :],
                     Q[h, :].rearrange("p (c b j) -> p b c j", b=NB, c=NC)[:, b_]), w)
            yield
            k, w = TB.get()
            a = A(act(TMP[:, k, 0:256], PS[:, b, 0:256], ACT.Copy), p, w)
            PB.free(b, a)
            yield
            b, w = PB.get()
            p = P(mm(PS[:, b, 0:256], W("wout"), TMP[:, k, 0:256]), a, w)
            TB.free(k, p)
            yield
            v = V(tt(BIG[0][:, c0].rearrange("p (c j) -> p c j", c=NC),
                     X[:, :].rearrange("p (c b j) -> p b c j", b=NB, c=NC)[:, b_],
                     PS[:, b, 0:256].rearrange("p (c j) -> p c j", c=NC), AD), p)
            PB.free(b, v)

        pipe((mo_gen(b_) for b_ in range(NB)), 4)
        bar()

        X = BIG[0]
        XG, XA, QF, KF, YF = BIG[2], BIG[3], BIG[4], BIG[5], BIG[6]
        XN = BIG[1]
        pipe((ln_gen(X, XN, t) for t in range(NT)), 4)
        bar()
        bst = small(6)
        agg = small(2)
        gs = small(32)
        gs2 = small(32)
        gsc = small(32)

        def group_norm(src, dst, g_, b_):
            for n in range(NB):
                V.chain(lambda e, n=n: e.bn_stats(bst, src[:, n * S:(n + 1) * S]))
                V.chain(lambda e, n=n: e.bn_aggr(agg, bst))
                V.chain(cp(gs[:, n:n + 1], agg[:, 0:1]))
                V.chain(stt(gs[:, 16 + n:17 + n], agg[:, 0:1], agg[:, 0:1], agg[:, 1:2], MU, AD))
            p = P(mm(PS[:, 0, 0:32], K("g8"), gs), V.last())
            V(cp(gs2, PS[:, 0, 0:32]), p)
            V.chain(tt(gsc[:, 0:16], gs2[:, 0:16], gs2[:, 0:16], MU))
            V.chain(tt(gsc[:, 0:16], gs2[:, 16:32], gsc[:, 0:16], SU))
            V.chain(ts(gsc[:, 0:16], gsc[:, 0:16], 0.0, None, MX))
            a = A(act(gsc[:, 0:16], gsc[:, 0:16], ACT.Sqrt, bias=K("eps5")), V.last())
            V.chain(rcp(gsc[:, 0:16], gsc[:, 0:16]), a)
            V.chain(ts(gsc[:, 0:16], gsc[:, 0:16], g_, None, MU))
            V.chain(tt(gsc[:, 16:32], gs2[:, 0:16], gsc[:, 0:16], MU))
            V.chain(ts(gsc[:, 16:32], gsc[:, 16:32], -1.0, b_, MU, AD))
            v = V.last()
            for n in range(NB):
                c0 = slice(n * S, (n + 1) * S)
                if n % 2:
                    A(act(dst[:, c0], src[:, c0], ACT.Identity, scale=gsc[:, n:n + 1], bias=gsc[:, 16 + n:17 + n]), v)
                else:
                    V(ts(dst[:, c0], src[:, c0], gsc[:, n:n + 1], gsc[:, 16 + n:17 + n], MU, AD), v)
            bar()

        group_norm(XN, XG, B("g1"), B("b1n"))

        def qk_gen(t, w, dst, dec):
            b, wt = PB.get()
            p = P(mm(PS[:, b, :], w, XG[:, sl(t)]), wt)
            yield
            k, w_ = TB.get()
            a = A(act(TMP[:, k, :], PS[:, b, :], ACT.Square), p, w_)
            yield
            res = []
            yield from rstd_gen(a, k, None, False, res, 1e-12)
            b2, p = res[0]
            v = V(tt(dst[:, sl(t)].rearrange("p (a n) -> p a n", a=2), PS[:, b, :].rearrange("p (a n) -> p a n", a=2),
                     K(dec).rearrange("p (a n) -> p a n", a=1).broadcast_to((128, 2, 256)), MU), p)
            PB.free(b, v)
            yield
            v = V.chain(tt(dst[:, sl(t)], dst[:, sl(t)], PS[:, b2, :], MU))
            PB.free(b2, v)

        pipe([g for t in range(NT) for g in (qk_gen(t, W("q1"), QF, "dq"), qk_gen(t, W("k1"), KF, "dk"))], 3)
        bar()
        AB = BIG[7]
        KM = [AB[:, 1024 * i:1024 * i + 1024].rearrange("p (r n) -> p r n", r=4) for i in range(2)]
        VM = [AB[:, 2048 + 1024 * i:3072 + 1024 * i].rearrange("p (a r n) -> p a r n", a=2, r=4) for i in range(2)]
        KT_ = [BIG[6][:, 256 * i:256 * i + 256].rearrange("p (a n) -> p a n", a=2) for i in range(2)]
        VTK = [BIG[6][:, 512 + 256 * i:768 + 256 * i].rearrange("p (a n) -> p a n", a=2) for i in range(2)]
        SBD = [BIG[6][:, 1024 + 128 * i:1152 + 128 * i] for i in range(2)]
        YT = [BIG[6][:, 1280 + 256 * i:1536 + 256 * i] for i in range(2)]
        S1 = [BIG[6][:, 1792 + 1024 * i:2816 + 1024 * i].rearrange("p (a r n) -> p a r n", a=2, r=4) for i in range(2)]
        setfree = [[], []]
        sring = Ring([0, 1])

        def ret_gen(n):
            i = n % 2
            c0 = n * S
            w0 = setfree[i]
            vs_ = []
            for r in range(4):
                vs_.append(V(ts(KM[i][:, r, :], KF[:, c0:c0 + S], K("rm", r, r + 1), None, MU), w0))
            b, wt = PB.get()
            p = P(mms(mm(PS[:, b, 0:128], XG[:, c0:c0 + 128], W("v1")),
                      mm(PS[:, b, 128:256], XG[:, c0 + 128:c0 + 256], W("v1")),
                      tr(PS[:, b, 256:384], KF[:, c0:c0 + 128])), wt)
            yield
            a = A(act(VTK[i], PS[:, b, 0:256].rearrange("p (a n) -> p a n", a=2), ACT.Copy), p, w0)
            a = A(act(KT_[i][:, 0, :], PS[:, b, 256:384], ACT.Copy), p)
            PB.free(b, a)
            yield
            gg = []
            for h in range(2):
                gg.append(G(tt(VM[i][:, h], VTK[i][:, h, :].rearrange("p (r n) -> p r n", r=1).broadcast_to((128, 4, 128)),
                               K("colr").rearrange("p (r n) -> p r n", r=4), MU), a, w0))
            b, wt = PB.get()
            p = P(mm(PS[:, b, 0:128], KT_[i][:, 0, :], VTK[i][:, 0, :]), a, wt)
            yield
            v = V(tt(SBD[i], PS[:, b, 0:128], K("bd8"), MU), p, w0)
            PB.free(b, v)
            vsb = v
            by, wy = PB.get()
            py = None
            for g_ in range(4):
                r32 = slice(32 * g_, 32 * g_ + 32)
                ks, ws = sring.get()
                done = []
                for h in range(2):
                    b, wt = PB.get()
                    cc = c0 + 128 * h
                    p = P(mms(*[mm(PS[:, b, 128 * r:128 * r + 128], KM[i][r32, r, 128 * h:128 * h + 128],
                                   QF[r32, cc:cc + 128]) for r in range(4)]), vs_, wt)
                    yield
                    v = V(tt(S1[ks][:, h], PS[:, b, :].rearrange("p (r n) -> p r n", r=4),
                             K("tri").rearrange("p (r n) -> p r n", r=1).broadcast_to((128, 4, 128)), MU), p, ws)
                    PB.free(b, v)
                    done.append(v)
                yield
                fs = []
                for h in range(2):
                    o = PS[r32, by, 128 * h:128 * h + 128]
                    if h:
                        fs.append(mm(o, SBD[i][:, r32], QF[:, c0 + 128:c0 + 256], start=True, stop=False))
                    for r in range(4):
                        fs.append(mm(o, VM[i][:, h, r, r32], S1[ks][:, h, r, :], start=(h == 0 and r == 0), stop=(r == 3)))
                py = P(mms(*fs), done, gg, vsb, wy)
                sring.free(ks, py)
            yield
            a = A(act(YT[i], PS[:, by, 0:256], ACT.Copy), py, w0)
            PB.free(by, a)
            yield
            b, wt = PB.get()
            p = P(mm(PS[:, b, 0:256], W("o1"), YT[i]), a, wt)
            yield
            v = V(stt(XA[:, c0:c0 + S], PS[:, b, 0:256], B("ob1"), XN[:, c0:c0 + S], AD, AD), p)
            PB.free(b, v)
            setfree[i] = [v, p, py]

        pipe((ret_gen(n) for n in range(NB)), 2)
        bar()
        group_norm(XA, XG, B("fg1"), B("fb1"))

        def fin1(t):
            def f(b, p):
                v = V(stt(X[:, sl(t)], PS[:, b, :], B("b12"), X[:, sl(t)], AD, AD), p)
                return V.chain(tt(X[:, sl(t)], X[:, sl(t)], XA[:, sl(t)], AD))
            return f

        pipe((ffn_gen(t, XG, lambda j: W("w11", 128 * j, 128 * j + 128), lambda j: B("b11", j, j + 1), 2, ACT.Silu,
                      lambda j: W("w12", 128 * j, 128 * j + 128), fin1(t)) for t in range(NT)), 2)
        bar()

        R = [BIG[7][:, 256 * i:256 * i + 256] for i in range(8)]

        def r3(ap, n):
            return ap[:, 0:32 * n].rearrange("p (b e) -> p b e", e=n)

        def bc(ap, n):
            return ap.rearrange("p (b e) -> p b e", e=1).broadcast_to((128, 32, n))

        def logits(wt, n, bias, dst):
            p = P(mms(*[mm(PS[:, 0, n * k:n * k + n], XN[:, 128 * k:128 * k + 128], wt) for k in range(32)]))
            if bias is None:
                V.chain(cp(dst[:, 0:32 * n], PS[:, 0, 0:32 * n]), p)
            else:
                V.chain(tt(r3(dst, n), r3(PS[:, 0, :], n),
                           bias.rearrange("p (b e) -> p b e", b=1).broadcast_to((128, 32, n)), AD), p)

        def softmax8(lg, n, tmp):
            m, z = small(32), small(32)
            V.chain(red(m, r3(lg, n), MX))
            V.chain(tt(r3(lg, n), r3(lg, n), bc(m, n), SU))
            a = A(act(lg[:, 0:32 * n], lg[:, 0:32 * n], ACT.Exp), V.last())
            V.chain(red(z, r3(lg, n)), a)
            V.chain(rcp(z, z))
            V.chain(tt(r3(lg, n), r3(lg, n), bc(z, n), MU))

        def moe(n, nh, w1, b1, func, w2, b2, wtok, waits):
            def gen(t, e_):
                b, w = PB.get()
                p = P(mms(*[mm(PS[:, b, 128 * k:128 * k + 128],
                               wtok[:, 4 * t + k, e_:e_ + 1].broadcast_to((128, 128)), K("ident")) for k in range(4)]),
                      w, waits)
                yield
                kb, w = TB.get()
                a0 = A(act(TMP[:, kb, :], PS[:, b, :], ACT.Copy), p, w)
                PB.free(b, a0)

                def fin(bo, p):
                    v = V(stt(TMP[:, kb, :], PS[:, bo, :], b2(e_), TMP[:, kb, :], AD, MU), p, a0)
                    v2 = V.chain(tt(X[:, sl(t)], X[:, sl(t)], TMP[:, kb, :], AD))
                    TB.free(kb, v2)
                    return v
                yield from ffn_gen(t, XN, lambda j: w1(e_, j), lambda j: b1(e_, j), nh, func, lambda j: w2(e_, j), fin)
            pipe((gen(t, e_) for e_ in range(n) for t in range(NT)), 2)
            bar()

        lg, wt1 = R[0], R[1]
        logits(W("gw1"), 4, B("gb1"), lg)
        ent = small(32)
        ab = small(32)
        held = PB.idle.pop([k for k, _ in PB.idle].index(7))
        for t in range(NT):
            b, w = PB.get()
            p = P(mm(PS[0:64, b, :], W("dw1"), XN[:, sl(t)]), w, V.last())
            k, w = TB.get()
            a = A(act(TMP[0:64, k, :], PS[0:64, b, :], ACT.Relu, bias=B("db1")[0:64, :]), p, w)
            PB.free(b, a)
            p = P(mms(*[mm(PS[:, 7, 4 * t + j:4 * t + j + 1], TMP[0:64, k, 128 * j:128 * j + 128], W("dw2")[0:64, :])
                        for j in range(4)]), a)
            TB.free(k, p)
        V.chain(ts(ent, PS[:, 7, 0:32], B("db2"), None, AD), p)
        PB.free(7)
        V.chain(ts(ab, ent, -1.0, None, MU))
        V.chain(tt(ab, ent, ab, MX))
        a = A(act(ab, ab, ACT.Exp, scale=-1.0), V.last())
        a = A.chain(act(ab, ab, ACT.Ln, bias=K("one")[:, 0:1]))
        V.chain(ts(ent, ent, 0.0, None, MX), a)
        V.chain(tt(ent, ent, ab, AD))
        V.chain(ts(ent, ent, -0.5, None, AD))
        V.chain(ts(ent, ent, 1.0 / 1.5, None, MU))
        V.chain(ts(ent, ent, 0.0, 1.0, MX, MN))
        V.chain(ts(ent, ent, 3.0, 1.0, MU, AD))
        V.chain(ts(ent, ent, RND, None, AD))
        V.chain(ts(ent, ent, -RND, None, AD))
        V.chain(ts(ent, ent, 1.0, 4.0, MX, MN))
        rk = R[2]
        V.chain(lambda e: e.memset(rk[:, 0:128], 0.0))
        l3, k3 = r3(lg, 4), r3(rk, 4)
        for i in range(4):
            for j in range(i + 1, 4):
                V.chain(tt(ab, l3[:, :, j], l3[:, :, i], ALU.is_gt))
                V.chain(tt(k3[:, :, i], k3[:, :, i], ab, AD))
                V.chain(ts(ab, ab, -1.0, 1.0, MU, AD))
                V.chain(tt(k3[:, :, j], k3[:, :, j], ab, AD))
        V.chain(tt(k3, k3, bc(ent, 4), ALU.is_lt))
        V.chain(red(ab, l3, MX))
        V.chain(tt(l3, l3, bc(ab, 4), SU))
        a = A(act(lg[:, 0:128], lg[:, 0:128], ACT.Exp), V.last())
        V.chain(tt(l3, l3, k3, MU), a)
        V.chain(red(ab, l3))
        V.chain(rcp(ab, ab))
        V.chain(tt(l3, l3, bc(ab, 4), MU))
        bar()
        moe(4, 2, lambda e, j: MW[:, 256 * e + 128 * j:256 * e + 128 * j + 128], lambda e, j: B("eb1", 2 * e + j, 2 * e + j + 1),
            ACT.Relu, lambda e, j: MW[:, 1024 + 256 * e + 128 * j:1024 + 256 * e + 128 * j + 128],
            lambda e: B("eb2", e, e + 1), l3, [(s_m1, 16)])
        mw_free = bar()
        SP.dma(lambda e: e.dma_start(MW[:, :], m2), (s_m2, 16), mw_free, (s_m1, 16))

        pipe((ln_gen(X, XN, t) for t in range(NT)), 4)
        bar()
        XT, X1, H1, H2, KN, DG = BIG[2], BIG[3], BIG[4], BIG[5], BIG[6], BIG[7]
        XT3 = XT[:, :].rearrange("p (b d) -> p b d", b=32)
        def xt_gen(k, dst):
            b, w = PB.get()
            p = P(mms(*[tr(PS[:, b, 128 * j:128 * j + 128], XN[:, 128 * (k + j):128 * (k + j) + 128])
                        for j in range(4)]), w)
            yield
            a = A(act(dst[:, 128 * k:128 * k + 512], PS[:, b, :], ACT.Copy), p)
            PB.free(b, a)

        pipe((xt_gen(4 * k, XT) for k in range(8)), 2)
        bar()
        d_idx = nc.dram_tensor("d_idx", (4096,), mybir.dt.uint32).ap()
        d_xt = nc.dram_tensor("d_xt", (4096, 136), F32).ap()
        d_acc = nc.dram_tensor("d_acc", (4096, 128), F32).ap()
        d_xs = nc.dram_tensor("d_xs", (5120, 128), F32).ap()
        d_ys = nc.dram_tensor("d_ys", (5120, 128), F32).ap()
        s_zx, s_sx, s_wy, s_gy = (sem(n) for n in ("d_zx", "d_sx", "d_wy", "d_gy"))
        s_lx = [sem(f"d_lx{i}") for i in range(5)]
        s_i, s_i2, s_xt, s_z = sem("d_i"), sem("d_i2"), sem("d_xt"), sem("d_z")
        s_g = [sem(f"d_g{i}") for i in range(8)]
        s_s = [sem(f"d_s{i}") for i in range(8)]
        IX = small(32).bitcast(mybir.dt.uint32)

        def views(a, n, b, m):
            return (a[:, 0:n].rearrange("p (x y) -> p x y", y=1).broadcast_to((128, n, m)),
                    b.rearrange("p (x y) -> p x y", x=1).broadcast_to((128, n, m)))

        lg, eq, sel, pre, tot = R[0], R[1], R[2], R[4], R[5]
        logits(W("gw2"), 8, None, lg)
        softmax8(lg, 8, None)
        thr, cand, cnt, one8, need = (small(8) for _ in range(5))
        p3 = r3(lg, 8)
        V.chain(lambda e: e.memset(thr, 0.0))

        def b32(ap):
            return ap.rearrange("p (b e) -> p b e", b=1).broadcast_to((128, 32, 8))

        for bit in range(29, -1, -1):
            V.chain(ts(cand.bitcast(I32), thr.bitcast(I32), 1 << bit, None, ALU.bitwise_or))
            V.chain(tt(r3(eq, 8), p3, b32(cand), ALU.is_ge))
            V.chain(red(cnt, eq[:, 0:256].rearrange("p (b e) -> p e b", e=8)))
            p = P(mm(PS[:, 0, 0:8], K("one"), cnt), V.last())
            V.chain(ts(one8.bitcast(I32), PS[:, 0, 0:8], 512.0, None, ALU.is_ge), p)
            V.chain(lambda e: e.copy_predicated(thr, one8.bitcast(I32), cand))
        V.chain(tt(r3(sel, 8), p3, b32(thr), ALU.is_gt))
        V.chain(tt(r3(eq, 8), p3, b32(thr), ALU.is_equal))

        def prefix(m, out, tmp):
            p = P(mms(mm(PS[:, 0, 0:256], K("lt"), m), mm(PS[:, 0, 256:512], K("one"), m)), V.last())
            V.chain(cp(tmp, PS[:, 0, 256:512]), p)
            x, y = tmp, out
            for sh in (1, 2, 4, 8, 16):
                V.chain(cp(y[:, 0:8 * sh], x[:, 0:8 * sh]))
                V.chain(tt(y[:, 8 * sh:256], x[:, 8 * sh:256], x[:, 0:256 - 8 * sh], AD))
                x, y = y, x
            V.chain(tt(x, x, PS[:, 0, 256:512], SU))
            V.chain(tt(out, x, PS[:, 0, 0:256], AD))

        prefix(eq, pre, tot)
        V.chain(red(cnt, sel[:, 0:256].rearrange("p (b e) -> p e b", e=8)))
        p = P(mm(PS[:, 0, 0:8], K("one"), cnt), V.last())
        V.chain(ts(need, PS[:, 0, 0:8], -1.0, 512.0, MU, AD), p)
        V.chain(tt(r3(pre, 8), r3(pre, 8), b32(need), ALU.is_lt))
        V.chain(tt(pre, pre, eq, MU))
        V.chain(tt(sel, sel, pre, AD))
        prefix(sel, pre, tot)
        V.chain(ts(pre, pre, 1.0, None, AD))
        V.chain(tt(pre, pre, sel, MU))
        V.chain(ts(pre, pre, -1.0, None, AD))
        pi, ph = tot.bitcast(I32), R[6]
        V.chain(cp(pi, pre))
        V.chain(ts(eq.bitcast(I32), pi, 4, None, ALU.arith_shift_right))
        V.chain(cp(ph, eq.bitcast(I32)))
        V.chain(ts(eq.bitcast(I32), pi, 15, None, ALU.bitwise_and))
        V.chain(cp(pre, eq.bitcast(I32)))
        OH = BIG[4][:, :].bitcast(BF16).rearrange("p (x n) -> p x n", n=32)
        OL = BIG[5][:, :].bitcast(BF16).rearrange("p (x v n) -> p x v n", v=2, n=16)
        V.chain(tt(OH, *views(ph, 256, K("i40", 0, 32), 32), ALU.is_equal))
        LO = BIG[6][:, 0:2048].bitcast(BF16).rearrange("p (x n) -> p x n", n=16)
        V.chain(tt(LO, *views(pre, 256, K("i40", 0, 16), 16), ALU.is_equal))
        V.chain(ts(OL[:, :, 0, :], LO, K("pcol"), None, MU))
        for k in range(32):
            V(ts(OL[:, 8 * k:8 * k + 8, 1, :], LO[:, 8 * k:8 * k + 8, :], K("i40", k, k + 1), None, MU))
        OHf = OH.rearrange("p x n -> p (x n)")
        OLf = OL.rearrange("p x v n -> p (x v n)")
        for hh in range(2):
            p = P(mms(*[mm(PS[:, 1 + hh, 0:256], OHf[:, 256 * k + 128 * hh:256 * k + 128 * hh + 128],
                           OLf[:, 256 * k:256 * k + 256], start=(k == 0), stop=(k == 31)) for k in range(32)]), V.last())
        idf = R[7]
        IDX = BIG[6][:, 2048:2048 + 32].bitcast(mybir.dt.uint32).rearrange("p (h l) -> p h l", h=2)
        for hh in range(2):
            a = A(act(R[6 + hh], PS[:, 1 + hh, 0:256], ACT.Copy), p)
        for hh in range(2):
            for e4 in range(4):
                q = slice(32 * e4, 32 * e4 + 32)
                c = 32 * (4 * hh + e4)
                v = V(stt(IDX[q, hh, :], R[6 + hh][q, c + 16:c + 32], 128.0, R[6 + hh][q, c:c + 16], MU, AD), a)
        SP.dma(lambda e: e.dma_start(d_idx.rearrange("(h p l) -> p h l", h=2, l=16), IDX), (s_i, 16), v)
        SP.dma(lambda e: e.dma_start(IX, d_idx.rearrange("(c p) -> p c", p=128), allow_slow_non_contiguous=True), (s_i2, 16), (s_i, 16))
        SP.dma(lambda e: e.dma_start(d_xt.rearrange("(b p) d -> p b d", p=128)[:, :, 0:128], XT3), (s_xt, 16), v)
        SP.dma(lambda e: e.dma_start(d_xt.rearrange("(b p) d -> p b d", p=128)[:, :, 128:136], r3(lg, 8)), (s_xt, 32), v)
        for e_ in (A, V, G, P):
            e_.items.append((lambda eng: None, [(s_xt, 32), (s_i2, 16)], False))
        bar()

        def fetch2():
            z = BIG[7][:, 1024:2048]
            v = V(lambda e: e.memset(z, 0.0))
            for q in range(4):
                SP.dma(lambda e, q=q: e.dma_start(
                    d_acc.rearrange("(p b) d -> p (b d)", p=128)[:, 1024 * q:1024 * q + 1024], z), (s_z, 16 * q + 16), v)
            for q in range(5):
                SP.dma(lambda e, q=q: e.dma_start(
                    d_xs.rearrange("(p b) d -> p (b d)", p=128)[:, 1024 * q:1024 * q + 1024], z), (s_zx, 16 * q + 16), v)
            for e_ in range(8):
                for q in range(4):
                    dst = gx(e_)[:, 136 * q:136 * q + 136]
                    c = 4 * e_ + q
                    G.dma(lambda e, dst=dst, c=c: e.indirect_dma_start(
                        dst, None, d_xt, bass.IndirectOffsetOnAxis(ap=IX[:, c:c + 1], axis=0)), (s_g[e_], 0),
                        (s_xt, 32), (s_i2, 16), v)

        def gx(e_):
            return BIG[3][:, 544 * e_:544 * e_ + 544] if e_ < 7 else BIG[7][:, 0:544]

        def experts2():
            YO = [BIG[5][:, 512 * i:512 * i + 512] for i in range(8)]

            def gen(e_):
                b, w = PB.get()
                p = P(mms(*[tr(PS[:, b, 128 * q:128 * q + 128], gx(e_)[:, 136 * q:136 * q + 128]) for q in range(4)]),
                      w, (s_g[e_], 64), (s_m2, 16))
                yield
                kx, w = TB.get()
                ax = A(act(TMP[:, kx, :], PS[:, b, :], ACT.Copy), p, w)
                PB.free(b, ax)
                yield
                bo, wo = PB.get()
                hs = []
                for j in range(4):
                    b, w = PB.get()
                    p = P(mm(PS[:, b, :], MW[:, 512 * e_ + 128 * j:512 * e_ + 128 * j + 128], TMP[:, kx, :]), w, ax)
                    yield
                    k, w = TB.get()
                    a = A(act(TMP[:, k, :], PS[:, b, :], ACT.Gelu_apprx_tanh, bias=B("m2b1", 4 * e_ + j, 4 * e_ + j + 1)), p, w)
                    PB.free(b, a)
                    hs.append((k, a))
                    if j:
                        kk, aa = hs[j - 1]
                        p = P(mm(PS[:, bo, :], MW[:, 4096 + 512 * e_ + 128 * (j - 1):4096 + 512 * e_ + 128 * j],
                                 TMP[:, kk, :], start=(j == 1), stop=False), aa, wo)
                        TB.free(kk, p)
                TB.free(kx, p)
                kk, aa = hs[3]
                p = P(mm(PS[:, bo, :], MW[:, 4096 + 512 * e_ + 384:4096 + 512 * e_ + 512], TMP[:, kk, :],
                         start=False, stop=True), aa)
                TB.free(kk, p)
                yield
                k, w = TB.get()
                a = A(act(TMP[:, k, :], PS[:, bo, :], ACT.Identity, bias=B("m2b2", e_, e_ + 1)), p, w)
                yield
                p = P(mms(*[tr(PS[:, bo, 128 * q:128 * q + 128], TMP[:, k, 128 * q:128 * q + 128]) for q in range(4)]), a)
                TB.free(k, p)
                yield
                for q in range(4):
                    v = V(ts(YO[e_][:, 128 * q:128 * q + 128], PS[:, bo, 128 * q:128 * q + 128],
                             gx(e_)[:, 136 * q + 128 + e_:136 * q + 129 + e_], None, MU), p)
                PB.free(bo, v)
                before = (s_s[e_ - 1], 64) if e_ else (s_z, 64)
                for q in range(4):
                    c = 4 * e_ + q
                    src = YO[e_][:, 128 * q:128 * q + 128]
                    G.dma(lambda e, src=src, c=c: e.indirect_dma_start(
                        d_acc, bass.IndirectOffsetOnAxis(ap=IX[:, c:c + 1], axis=0), src, None, compute_op=AD),
                        (s_s[e_], 0), v, before)

            pipe((gen(e_) for e_ in range(8)), 2)
            s_a = sem("d_a")
            SP.dma(lambda e: e.dma_start(BIG[6][:, :].rearrange("p (b d) -> p b d", b=32),
                                         d_acc.rearrange("(b p) d -> p b d", p=128)), (s_a, 16), (s_s[7], 64), bar())
            for k in range(8):
                b, w = PB.get()
                p = P(mms(*[tr(PS[:, b, 128 * q:128 * q + 128], BIG[6][:, 512 * k + 128 * q:512 * k + 128 * q + 128])
                            for q in range(4)]), w, (s_a, 16))
                v = V(tt(X[:, 512 * k:512 * k + 512], X[:, 512 * k:512 * k + 512], PS[:, b, :], AD), p)
                PB.free(b, v)

        XP = DG[0:32, 0:2048].rearrange("p (b d) -> p b d", b=16)
        for q_ in range(4):
            b, w = PB.get()
            p = P(mms(*[tr(PS[0:32, b, 128 * j:128 * j + 128],
                           XN[:, 256 * (4 * q_ + j) + 96:256 * (4 * q_ + j) + 128]) for j in range(4)]), w)
            a = A(act(XP[:, 4 * q_:4 * q_ + 4, :], PS[0:32, b, :].rearrange("p (b d) -> p b d", b=4), ACT.Copy), p)
            PB.free(b, a)
        bar()
        wm, wz = small(32), small(32)
        SCL = 128 ** -0.5

        def win_gen(k):
            half = k % 2
            nk = 160 if half else 128
            q0 = 128 * k
            b, w = PB.get()
            p = P(mm(PS[:, b, 0:nk], XN[:, q0:q0 + 128], XN[:, q0 + 128 - nk:q0 + 128]), w)
            yield
            kt, w = TB.get()
            sc_ = TMP[:, kt, 0:nk]
            v = V(stt(sc_, PS[:, b, 0:nk], SCL, K("band") if half else K("band0"), MU, AD), p, w)
            PB.free(b, v)
            v = V.chain(red(wm[:, k:k + 1], sc_, MX))
            v = V.chain(ts(wm[:, k:k + 1], wm[:, k:k + 1], -1.0, None, MU))
            yield
            a = A(act(sc_, sc_, ACT.Exp, bias=wm[:, k:k + 1], accum_out=wz[:, k:k + 1]), v)
            yield
            v = V(rcp(wz[:, k:k + 1], wz[:, k:k + 1]), a)
            v = V.chain(ts(sc_, sc_, wz[:, k:k + 1], None, MU))
            yield
            b, w = PB.get()
            fs = [tr(PS[:, b, 0:128], sc_[:, nk - 128:nk])]
            if half:
                fs.append(tr(PS[0:32, b, 128:256], sc_[:, 0:32]))
            p = P(mms(*fs), v, w)
            yield
            a = A(act(TMP[:, kt, 256:384], PS[:, b, 0:128], ACT.Copy), p)
            if half:
                a = A(act(TMP[0:32, kt, 384:512], PS[0:32, b, 128:256], ACT.Copy), p)
            yield
            fs = [mm(PS[:, b, 256:384], XT3[:, k, :], TMP[:, kt, 256:384], stop=not half)]
            if half:
                fs.append(mm(PS[:, b, 256:384], XP[:, k // 2, :], TMP[0:32, kt, 384:512], start=False))
            p = P(mms(*fs), a)
            TB.free(kt, p)
            yield
            v = V(tt(X1[:, q0:q0 + 128], PS[:, b, 256:384], XN[:, q0:q0 + 128], AD), p)
            PB.free(b, v)

        pipe((win_gen(k) for k in range(32)), 4)
        bar()
        pipe((ln_gen(X1, X1, t, gb=[B("g21"), B("be21")]) for t in range(NT)), 4)
        bar()

        def kn_gen(src, dst, n0, n):
            k, w = TB.get()
            a = A(act(TMP[:, k, 0:n], src[:, n0:n0 + n], ACT.Square), w)
            yield
            res = []
            yield from rstd_gen(a, k, None, False, res, 1e-12, n)
            b, p = res[0]
            v = V(tt(dst[:, n0:n0 + n], src[:, n0:n0 + n], PS[:, b, 0:n], MU), p)
            PB.free(b, v)

        pk = small(50)
        pkn, pkp, ph1, ph2, pdf = (pk[:, 10 * i:10 * i + 10] for i in range(5))
        pipe([kn_gen(XN, KN, TW * t, TW) for t in range(NT)] + [kn_gen(W("pT"), pkn, 0, 10)], 3)
        bar()
        bim = small(1)
        V(tt(bim, B("memb"), B("bi"), SU))
        bar()
        DF = DG

        def mem_gen(kn, kp, h1, h2, df, n0, n):
            s = slice(n0, n0 + n)
            b, w = PB.get()
            p = P(mm(PS[:, b, 0:n], W("wi"), kn[:, s]), w)
            yield
            k, w = TB.get()
            a = A(act(TMP[:, k, 0:n], PS[:, b, 0:n], ACT.Identity, bias=B("bi")), p, w)
            PB.free(b, a)
            yield
            b, w = PB.get()
            p = P(mm(PS[:, b, 0:n], W("wl1"), TMP[:, k, 0:n]), a, w)
            yield
            k2, w = TB.get()
            a = A(act(TMP[:, k2, 0:n], PS[:, b, 0:n], ACT.Silu, bias=B("bl1")), p, w)
            PB.free(b, a)
            yield
            b, w = PB.get()
            p = P(mm(PS[:, b, 0:n], W("wl2"), TMP[:, k2, 0:n]), a, w)
            TB.free(k2, p)
            yield
            a = A(act(h2[:, s], PS[:, b, 0:n], ACT.Silu, bias=B("bl2")), p)
            PB.free(b, a)
            yield
            b, w = PB.get()
            p = P(mm(PS[:, b, 0:n], W("memT"), h2[:, s]), a, w)
            yield
            v = V(stt(df[:, s], PS[:, b, 0:n], B("memb"), TMP[:, k, 0:n], AD, SU), p)
            PB.free(b, v)
            TB.free(k, v)

        pipe([mem_gen(KN, None, None, H2, DF, TW * t, TW) for t in range(NT)]
             + [mem_gen(pkn, None, None, ph2, pdf, 0, 10)], 3)
        bar()
        V(ts(pdf, pdf, 16.0, None, MU))
        bar()
        PB = Ring(range(7))

        def gr_gen(k, n, h2, df):
            s = slice(128 * k, 128 * k + n)
            b, w = PB.get()
            p = P(mms(tr(PS[0:n, b, 0:128], h2[:, s]),
                      tr(PS[0:n, b, 128:256], df[:, s])), w)
            yield
            kt, w = TB.get()
            a = A(act(TMP[0:n, kt, 0:256], PS[0:n, b, 0:256], ACT.Copy), p, w)
            PB.free(b, a)
            yield
            last = n != 128
            p = P(mm(PS[:, 7, 0:128], TMP[0:n, kt, 0:128], TMP[0:n, kt, 128:256], start=(k == 0 and not last), stop=last), a)
            TB.free(kt, p)

        pipe([gr_gen(k, 128, H2, DF) for k in range(32)] + [gr_gen(0, 10, ph2, pdf)], 3)
        wnew = TMP[:, 8, 0:128]
        gsx = small(2)
        bar()
        V(ts(gsx[:, 0:1], B("lrate"), 2.0 / (4256 * 128), None, MU))
        V.chain(ts(gsx[:, 1:2], B("fgate"), -1.0, 1.0, MU, AD))
        V.chain(ts(wnew, PS[:, 7, 0:128], gsx[:, 0:1], None, MU))
        V.chain(stt(wnew, W("memT"), gsx[:, 1:2], wnew, MU, AD))
        bar()
        PB = Ring(range(8))
        TB = Ring(range(8))
        MO = KN

        def mo2_gen(t):
            s = sl(t)
            b, w = PB.get()
            p = P(mm(PS[:, b, :], wnew, H2[:, s]), w)
            yield
            k, w = TB.get()
            a = A(act(TMP[:, k, :], PS[:, b, :], ACT.Identity, bias=B("memb")), p, w)
            PB.free(b, a)
            yield
            b, w = PB.get()
            p = P(mm(PS[:, b, :], W("wo2"), TMP[:, k, :]), a, w)
            yield
            a = A(act(MO[:, s], PS[:, b, :], ACT.Identity, bias=B("bo2")), p)
            PB.free(b, a)
            yield
            b, w = PB.get()
            p = P(mms(mm(PS[:, b, :], W("wg", 0, 128), X1[:, s], stop=False),
                      mm(PS[:, b, :], W("wg", 128, 256), MO[:, s], start=False)), a, w)
            yield
            a = A(act(TMP[:, k, :], PS[:, b, :], ACT.Sigmoid, bias=B("bg")), p)
            PB.free(b, a)
            yield
            v = V(tt(DG[:, s], X1[:, s], MO[:, s], SU), a)
            v = V.chain(tt(DG[:, s], DG[:, s], TMP[:, k, :], MU))
            TB.free(k, v)
            yield
            v = V.chain(tt(DG[:, s], DG[:, s], MO[:, s], AD))
            v = V.chain(tt(DG[:, s], DG[:, s], X1[:, s], AD))

        pipe((mo2_gen(t) for t in range(NT)), 3)
        bar()
        TB = Ring(range(9))
        X2 = DG
        pipe((ln_gen(DG, X2, t, gb=[B("g22"), B("be22")]) for t in range(NT)), 4)
        bar()

        def fin2(t):
            def f(b, p):
                return V(stt(H1[:, sl(t)], PS[:, b, :], B("b22"), X2[:, sl(t)], AD, AD), p)
            return f

        pipe((ffn_gen(t, X2, lambda j: W("w21", 128 * j, 128 * j + 128), lambda j: B("b21", j, j + 1), 4, ACT.Silu,
                      lambda j: W("w22", 128 * j, 128 * j + 128), fin2(t)) for t in range(NT)), 2)
        bar()
        pipe((ln_gen(H1, H1, t, gb=[B("g23"), B("be23")]) for t in range(NT)), 4)
        bar()

        fetch2()

        def fin2s(t):
            def f(b, p):
                v = V(stt(X[:, sl(t)], PS[:, b, :], B("bs2"), X[:, sl(t)], AD, AD), p)
                return V.chain(tt(X[:, sl(t)], X[:, sl(t)], H1[:, sl(t)], AD))
            return f

        pipe((ffn_gen(t, XN, lambda j: W("ws1", 128 * j, 128 * j + 128), lambda j: B("bs1", j, j + 1), 4,
                      ACT.Gelu_apprx_tanh, lambda j: W("ws2", 128 * j, 128 * j + 128), fin2s(t)) for t in range(NT)), 2)
        bar()
        experts2()
        mw_free = bar()
        SP.dma(lambda e: e.dma_start(MW[:, :], m3), (s_m3, 16), mw_free, (s_m2, 16))

        pipe((ln_gen(X, XN, t) for t in range(NT)), 4)
        bar()
        XU = BIG[5]
        XU3 = XU[:, :].rearrange("p (b d) -> p b d", b=32)
        pipe((xt_gen(4 * k, XU) for k in range(8)), 2)
        bar()
        logits(W("gw3"), 8, B("gb3"), R[0])
        softmax8(R[0], 8, None)
        m = small(32)
        p3 = r3(R[0], 8)
        V.chain(red(m, p3, MX))
        V.chain(tt(p3, p3, bc(m, 8), ALU.is_equal))
        V.chain(tt(p3, p3, K("desc").rearrange("p (b e) -> p b e", b=1).broadcast_to((128, 32, 8)), MU))
        V.chain(red(m, p3, MX))
        V.chain(tt(p3, p3, bc(m, 8), ALU.is_equal))
        SCR = BIG[7][:, 3072:4096]
        nt, e1, e2 = SCR[:, 0:8], SCR[:, 8:16], SCR[:, 16:24]
        expf, oh, ohT = SCR[:, 32:72], SCR[:, 80:400].rearrange("p (i e) -> p i e", e=8), SCR[:, 400:440]
        b1t = SCR[:, 440:600].rearrange("p (i j) -> p i j", j=4)
        EXI, IXP = SCR[:, 600:640].bitcast(I32), IX
        V.chain(red(cnt, R[0].rearrange("p (b e) -> p e b", e=8)))
        p = P(mm(PS[:, 1, 0:8], K("one"), cnt), V.last())
        V.chain(ts(e1, PS[:, 1, 0:8], 127.0, None, AD), p)
        V.chain(cp(nt.bitcast(I32), e1))
        V.chain(ts(e1.bitcast(I32), nt.bitcast(I32), 7, None, ALU.arith_shift_right))
        V.chain(cp(nt, e1.bitcast(I32)))
        V.chain(cp(e1, nt))
        x, y = e1, e2
        for sh in (1, 2, 4):
            V.chain(cp(y[:, 0:sh], x[:, 0:sh]))
            V.chain(tt(y[:, sh:8], x[:, sh:8], x[:, 0:8 - sh], AD))
            x, y = y, x
        pre, tot = R[1], R[2]
        prefix(R[0], pre, tot)
        V.chain(tt(y, x, nt, SU))
        V.chain(ts(y, y, 128.0, None, MU))
        V.chain(tt(r3(pre, 8), r3(pre, 8), b32(y), AD))
        V.chain(tt(pre, pre, R[0], MU))
        V.chain(red(m, r3(pre, 8)))
        vix = V.chain(cp(IXP, m))
        for k in range(32):
            G.dma(lambda e, k=k: e.indirect_dma_start(
                d_xs, bass.IndirectOffsetOnAxis(ap=IXP[:, k:k + 1], axis=0), XU3[:, k, :], None),
                (s_sx, 0), vix, A.last(), (s_zx, 80))
        V.chain(tt(oh, *views(K("i40"), 40, x, 8), ALU.is_ge))
        V.chain(red(expf, oh))
        V.chain(ts(expf, expf, 7.0, None, MN))
        V.chain(cp(EXI, expf))
        V.chain(tt(oh, *views(expf, 40, K("i40", 0, 8), 8), ALU.is_equal))
        V.chain(ts(ohT, expf, K("pcol"), None, ALU.is_equal))
        pr4 = TMP[:, 0:3, :].rearrange("p a n -> p (a n)")[:, 0:1280].rearrange("p (i j e) -> p i j e", j=4, e=8)
        V.chain(tt(pr4, oh.rearrange("p i (j e) -> p i j e", j=1).broadcast_to((128, 40, 4, 8)),
                   B("m3b1").rearrange("p (i e j) -> p i j e", i=1, e=8).broadcast_to((128, 40, 4, 8)), MU))
        V.chain(red(b1t, pr4))
        bar()
        XSA, XSB = BIG[6], BIG[7][:, 2048:3072]
        xs3 = d_xs.rearrange("(i p) d -> p i d", p=128)
        ys3 = d_ys.rearrange("(i p) d -> p i d", p=128)

        def tile(i):
            return XSA[:, 128 * i:128 * i + 128] if i < 32 else XSB[:, 128 * (i - 32):128 * (i - 31)]

        for g_ in range(5):
            sbv = (XSA[:, 1024 * g_:1024 * g_ + 1024] if g_ < 4 else XSB).rearrange("p (i d) -> p i d", i=8)
            SP.dma(lambda e, g_=g_, sbv=sbv: e.dma_start(sbv, xs3[:, 8 * g_:8 * g_ + 8, :]), (s_lx[g_], 16), (s_sx, 512))

        QF, KF, VF, CF = BIG[2], BIG[3], BIG[4], BIG[5]
        pipe([g for t in range(NT) for g in (lin_gen(t, QF, W("qkv", 0, 128), XN, ACT.Identity, bias=B("bqkv", 0, 1)),
                                              lin_gen(t, KF, W("qkv", 128, 256), XN, ACT.Identity, bias=B("bqkv", 1, 2)))], 4)
        VF3 = VF[:, :].rearrange("p (b d) -> p b d", b=32)

        def v3_gen(k):
            b, w = PB.get()
            p = P(mms(*[mm(PS[:, b, 128 * j:128 * j + 128], XN[:, 128 * (k + j):128 * (k + j) + 128], W("qkv", 256, 384))
                        for j in range(4)]), w)
            yield
            v = V(tt(VF3[:, k:k + 4, :], PS[:, b, :].rearrange("p (b d) -> p b d", b=4),
                     B("bv3").rearrange("p (b d) -> p b d", b=1).broadcast_to((128, 4, 128)), AD), p)
            PB.free(b, v)

        pipe((v3_gen(4 * k) for k in range(8)), 2)
        bar()
        def e3_gen(i):
            b, w = PB.get()
            p = P(tr(PS[:, b, 0:128], tile(i)), w, (s_lx[i // 8], 16), (s_m3, 16))
            yield
            k, w = TB.get()
            a = A(act(TMP[:, k, 0:128], PS[:, b, 0:128], ACT.Copy), p, w)
            yield

            def first(e, k=k, b=b):
                x = e.value_load(EXI[0:1, i:i + 1], min_val=0, max_val=7)
                return e.matmul(PS[:, b, :], TMP[:, k, 0:128], MW[:, bass.ds(x * 512, 512)], start=True, stop=True)

            p = P(first, a)
            TB.free(k, p)
            yield
            k, w = TB.get()
            v = V(cp(TMP[:, k, :], PS[:, b, :]), p, w)
            yield
            p = P(mms(*[tr(PS[:, b, 128 * j:128 * j + 128], TMP[:, k, 128 * j:128 * j + 128]) for j in range(4)]), v)
            yield
            for j in range(4):
                if j % 4 == 3:
                    v = V(ts(TMP[:, k, 384:512], PS[:, b, 384:512], b1t[:, i, 3:4], 0.0, AD, MX), p, a)
                else:
                    a = A(act(TMP[:, k, 128 * j:128 * j + 128], PS[:, b, 128 * j:128 * j + 128], ACT.Relu,
                              bias=b1t[:, i, j:j + 1]), p)
            PB.free(b, a, v)
            yield
            b, w = PB.get()

            def second(e, k=k, b=b):
                x = e.value_load(EXI[0:1, i:i + 1], min_val=0, max_val=7)
                e.matmul(PS[:, b, 0:128], ohT[:, i:i + 1].broadcast_to((128, 128)), W("b2r"), start=True, stop=False)
                for j in range(4):
                    r = e.matmul(PS[:, b, 0:128], TMP[:, k, 128 * j:128 * j + 128],
                                 MW[:, bass.ds(x * 512 + (4096 + 128 * j), 128)], start=False, stop=(j == 3))
                return r

            p = P(second, a, v, w)
            TB.free(k, p)
            yield
            v = V(cp(tile(i), PS[:, b, 0:128]), p)
            PB.free(b, v)
            if i % 8 == 7:
                g_ = i // 8
                sbv = (XSA[:, 1024 * g_:1024 * g_ + 1024] if g_ < 4 else XSB).rearrange("p (i d) -> p i d", i=8)
                SP.dma(lambda e: e.dma_start(ys3[:, 8 * g_:8 * g_ + 8, :], sbv), (s_wy, 16 * g_ + 16), v)

        pipe((e3_gen(i) for i in range(40)), 4)
        for e_ in (A, V, G, P):
            e_.items.append((lambda eng: None, [(s_wy, 80)], False))
        bar()
        YG = BIG[1][:, :].rearrange("p (b d) -> p b d", b=32)

        def y3_gather(k):
            G.dma(lambda e: e.indirect_dma_start(
                YG[:, k, :], None, d_ys, bass.IndirectOffsetOnAxis(ap=IXP[:, k:k + 1], axis=0)), (s_gy, 0), (s_wy, 80))

        EN = CF
        esum = small(8)

        def en_gen(t):
            k, w = TB.get()
            a = A(act(TMP[:, k, :], QF[:, sl(t)], ACT.Square), w)
            yield
            b, w = PB.get()
            p = P(mm(PS[:, b, :], K("s8"), TMP[:, k, :]), a, w)
            TB.free(k, p)
            yield
            a = A(act(EN[:, sl(t)], PS[:, b, :], ACT.Sqrt, accum_out=esum[:, t:t + 1]), p)
            PB.free(b, a)

        pipe((en_gen(t) for t in range(NT)), 3)
        bar()
        et = small(2)
        V(red(et[:, 0:1], esum))
        p = P(mm(PS[:, 0, 0:1], K("one"), et[:, 0:1]), V.last())
        V(ts(et[:, 1:2], PS[:, 0, 0:1], 0.1 / (128.0 * T), None, MU), p)
        V.chain(ts(EN[:, :], EN[:, :], et[:, 1:2], None, ALU.is_gt))
        V.chain(tt(KF[:, :], KF[:, :], EN[:, :], MU))
        bar()
        ISQ = float(np.float32(1.0) / np.sqrt(np.float32(8.0)))
        def half(buf, i):
            return buf[:, 2048 * i:2048 * i + 2048].bitcast(BF16).rearrange("p (h n) -> p h n", h=16)

        sets = [(half(MW, 0), half(MW, 1)), (half(MW, 2), half(MW, 3)), (half(BIG[5], 0), half(BIG[5], 1))]
        PTT = [BIG[6][:, 512 * i:512 * i + 512].rearrange("p (a n) -> p a n", a=2) for i in range(8)]
        AT = BIG[7]
        PTT += [AT[:, 3072 + 512 * i:3584 + 512 * i].rearrange("p (a n) -> p a n", a=2) for i in range(2)]
        PQ = [[AT[:, 768 * i + 384 * j:768 * i + 384 * j + 384].bitcast(BF16).rearrange("p (a n) -> p a n", a=3)
               for j in range(2)] for i in range(2)]
        V32 = [TMP[:, 5 + 2 * i:7 + 2 * i, :].rearrange("p a (h d) -> p a h d", d=32) for i in range(2)]
        RES = AT[:, 2112:2368]
        M3 = [AT[:, 2368 + 128 * i:2496 + 128 * i].bitcast(BF16) for i in range(2)]
        MXB = [AT[:, 2624 + 48 * i:2672 + 48 * i].bitcast(BF16).rearrange("p (a k h) -> p a k h", a=2, h=16)
               for i in range(2)]
        MX_ = [AT[:, 2720 + 32 * i:2752 + 32 * i].rearrange("p (a h) -> p a h", a=2) for i in range(2)]
        MXR = AT[:, 2784:2816].rearrange("p (a h) -> p a h", a=2)
        IDB = AT[:, 2816:2880].bitcast(BF16)
        ZR = [AT[:, 2880 + 32 * i:2912 + 32 * i].rearrange("p (a h) -> p a h", a=2) for i in range(2)]
        d_pt = nc.dram_tensor("d_pt", (NB, 2, 3, 128, 256), BF16).ap()
        d_mr = nc.dram_tensor("d_mr", (NB, 48, 256), BF16).ap()
        s_pw, s_st, s_mw, s_mr = ([sem(f"d_{n_}{i}") for i in range(2)] for n_ in ("pw", "st", "mw", "mr"))
        V(cp(IDB, K("ident")))
        for q_, k_ in sets:
            V(lambda e, k_=k_: e.memset(k_[32:64], 1.0))
        for i in range(2):
            V(lambda e, i=i: e.memset(V32[i][:, :, :, 8:32], 0.0))
            V.chain(lambda e, i=i: e.memset(V32[i][:, :, :, 8:9], 1.0))
        bar()
        TB = Ring(range(5))
        PB = Ring(range(6))
        ptr = Ring(range(10))
        v9free, setdone, maxtok, scored, bld = [[], []], {}, {}, {}, {}
        QROW = (0, 0, 0, 1, 1, 2)
        KROW = (0, 1, 2, 0, 1, 0)

        def build(n):
            i, st_ = n % 2, sets[n % 3]
            c0 = n * S
            k_ = n // 2
            for j, src in ((0, QF), (1, KF)):
                x_ = src[:, c0:c0 + S]
                pq = PQ[i][j]
                G.chain(cp(pq[:, 0, :], x_), *([(s_pw[i], 32 * k_)] if k_ else []))
                G.chain(tt(RES, x_, pq[:, 0, :], SU))
                G.chain(cp(pq[:, 1, :], RES))
                G.chain(tt(RES, RES, pq[:, 1, :], SU))
                g = G.chain(cp(pq[:, 2, :], RES))
                SP.dma(lambda e, j=j, pq=pq: e.dma_start(d_pt[n, j].rearrange("a p n -> p a n"), pq), (s_pw[i], 0), g)
            for j, rows in ((0, QROW), (1, KROW)):
                for t, part in enumerate(rows):
                    SP.dma(lambda e, j=j, t=t, part=part: e.dma_start(
                        st_[j][8 * t:8 * t + 8], d_pt[n, j, part].rearrange("(h d) n -> d h n", d=8)),
                        (s_st[i], 0), (s_pw[i], 32 * k_ + 32), setdone[n - 3] if n > 2 else None,
                        scored[n - 2] if n > 1 else None)
            bld[n] = (s_st[i], 192 * k_ + 192)

        def max_gen(n, h_):
            i = n % 2
            qs, ks = sets[n % 3]
            b, w = PB.get()
            p = P(mms(*[mm(PS[:, b, 256 * a_:256 * a_ + 256], qs[0:48, h_, 128 * a_:128 * a_ + 128], ks[0:48, h_, :])
                        for a_ in range(2)]), bld[n], w)
            if h_ == 15:
                scored[n] = p
            yield
            v = V(red(MX_[i][:, :, h_], PS[:, b, :].rearrange("p (h n) -> p h n", h=2), MX), p)
            PB.free(b, v)
            if h_ < 15:
                return
            yield
            V.chain(ts(MX_[i], MX_[i], -1.0, None, MU))
            V.chain(cp(MXB[i][:, :, 0, :], MX_[i]), maxtok.get(n - 2))
            V.chain(tt(MXR, MX_[i], MXB[i][:, :, 0, :], SU))
            V.chain(cp(MXB[i][:, :, 1, :], MXR))
            V.chain(tt(MXR, MXR, MXB[i][:, :, 1, :], SU))
            v = V.chain(cp(MXB[i][:, :, 2, :], MXR))
            b, w = PB.get()
            p = P(mms(*[mm(PS[0:48, b, 128 * a_:128 * a_ + 128], MXB[i][:, a_].rearrange("p k h -> p (k h)"), IDB)
                        for a_ in range(2)]), v, w)
            yield
            k_ = n // 2
            v = V(cp(M3[i][0:48, :], PS[0:48, b, 0:256]), p, *([(s_mw[i], 16 * k_)] if k_ else []))
            PB.free(b, v)
            maxtok[n] = p
            SP.dma(lambda e: e.dma_start(d_mr[n], M3[i][0:48, :]), (s_mw[i], 0), v)
            SP.dma(lambda e: e.dma_start(qs[48:51].rearrange("p h n -> p (h n)"),
                                         d_mr[n].rearrange("(k h) n -> k (h n)", k=3)),
                   (s_mr[i], 0), (s_mw[i], 16 * k_ + 16), setdone[n - 2] if n > 1 else None)

        def at_gen(n, q):
            i = n % 2
            c0 = n * S
            qs, ks = sets[n % 3]
            if q == 0:
                y3_gather(2 * n)
                y3_gather(2 * n + 1)
                con_[n] = G(cp(V32[i][:, :, :, 0:8], VF3[:, 2 * n:2 * n + 2, :].rearrange("p a (h d) -> p a h d", d=8)),
                            v9free[i])
            if q == 1 and n + 2 < NB:
                build(n + 2)
            g = con_[n]
            ex = []
            for r in range(4):
                h_ = 4 * q + r
                b, w = PB.get()
                p = P(mms(*[mm(PS[:, b, 256 * jh:256 * jh + 256], ks[0:51, h_, 128 * jh:128 * jh + 128], qs[0:51, h_, :])
                            for jh in range(2)]), (s_mr[i], 16 * (n // 2) + 16), w)
                yield
                kt, wt = ptr.get()
                a = A(act(PTT[kt], PS[:, b, :].rearrange("p (a n) -> p a n", a=2), ACT.Exp, scale=ISQ), p, wt)
                PB.free(b, a)
                ex.append((kt, a))
            yield
            py = P(mms(*[mm(PS[32 * r:32 * r + 32, 6 + q // 2, 256 * (q % 2):256 * (q % 2) + 256],
                            V32[i][:, jh, 4 * q + r, :], PTT[ex[r][0]][:, jh, :], start=(jh == 0), stop=(jh == 1))
                         for jh in range(2) for r in range(4)]), a, g, bofree[q // 2])
            for kt, _ in ex:
                ptr.free(kt, py)
            if q == 1:
                k, w = TB.get()
                a = A(act(TMP[:, k, :], PS[:, 6, :], ACT.Copy), py, w)
                bofree[0] = [a]
                con_[n, 'c'] = (k, a)
            if q < 3:
                return
            v9free[i] = [py]
            setdone[n] = py
            k2, w = TB.get()
            a = A(act(TMP[:, k2, :], PS[:, 7, :], ACT.Copy), py, w)
            bofree[1] = [a]
            yield
            k1, a1 = con_.pop((n, 'c'))
            b1, w1 = PB.get()
            b2, w2 = PB.get()
            p1 = P(mms(*[tr(PS[:, b1, 128 * x_:128 * x_ + 128], TMP[:, k1, 128 * x_:128 * x_ + 128]) for x_ in range(4)]), a1, w1)
            p2 = P(mms(*[tr(PS[:, b2, 128 * x_:128 * x_ + 128], TMP[:, k2, 128 * x_:128 * x_ + 128]) for x_ in range(4)]), a, w2)
            TB.free(k1, p1)
            TB.free(k2, p2)
            yield
            k, w = TB.get()
            for hf, b_, p_ in ((0, b1, p1), (1, b2, p2)):
                c9 = PS[:, b_, :].rearrange("p (g a r d) -> p a g r d", g=2, a=2, d=32)
                zr = ZR[i][:, :, 8 * hf:8 * hf + 8].rearrange("p a (g r) -> p a g r", g=2)
                c8 = TMP[:, k, 0:256].rearrange("p (a x g r d) -> p a x g r d", a=2, x=2, g=2, d=8)[:, :, hf]
                v = V(rcp(zr, c9[:, :, :, :, 8]), p_)
                for a_ in range(2):
                    v = V(tt(c8[:, a_], c9[:, a_, :, :, 0:8],
                             zr[:, a_].rearrange("p g (r d) -> p g r d", d=1).broadcast_to((128, 2, 4, 8)), MU), v, w)
                PB.free(b_, v)
            yield
            bo, w = PB.get()
            p = P(mms(*[tr(PS[:, bo, 128 * a_:128 * a_ + 128], TMP[:, k, 128 * a_:128 * a_ + 128]) for a_ in range(2)]), v, w)
            yield
            a = A(act(TMP[:, k, 256:512], PS[:, bo, 0:256], ACT.Copy), p)
            yield
            p = P(mm(PS[:, bo, 0:256], W("w3o"), TMP[:, k, 256:512]), a)
            TB.free(k, p)
            yield
            v = V(stt(X[:, c0:c0 + S], PS[:, bo, 0:256], B("bo3"), X[:, c0:c0 + S], AD, AD), p)
            PB.free(bo, v)

        con_ = {}
        bofree = [[], []]
        build(0)
        build(1)

        def order():
            for n in range(NB):
                for q in range(4):
                    yield at_gen(n, q)
                    if n + 1 < NB and q < 3:
                        for h_ in range((0, 6, 13)[q], (6, 13, 16)[q]):
                            yield max_gen(n + 1, h_)

        pipe((max_gen(0, h_) for h_ in range(16)), 6)
        pipe(order(), 4)
        bar()
        PB = Ring(range(8))
        TB = Ring(range(9))
        bar()
        for k in range(8):
            b, w = PB.get()
            p = P(mms(*[tr(PS[:, b, 128 * q:128 * q + 128], YG[:, 4 * k + q, :]) for q in range(4)]), w, (s_gy, 512))
            v = V(tt(X[:, 512 * k:512 * k + 512], X[:, 512 * k:512 * k + 512], PS[:, b, :], AD), p)
            PB.free(b, v)
        done = bar()
        s_o = sem("d_o")
        SP.dma(lambda e: e.dma_start(outT, X[:, :]), (s_o, 16), done)
        SP.items.append((lambda eng: None, [(s_o, 16)], False))

        block = ctx.enter_context(nc.Block())

        @block.sync
        def _(e):
            SP.play(e)

        @block.scalar
        def _(e):
            A.play(e)

        @block.vector
        def _(e):
            V.play(e)

        @block.gpsimd
        def _(e):
            G.play(e)

        @block.tensor
        def _(e):
            P.play(e)


def kernel(**inp):
    import concourse.bacc as bacc
    from concourse.bass_utils import run_bass_kernel_spmd as run

    f = {k: np.asarray(v) for k, v in inp.items()}

    def pad(a):
        out = np.zeros((128, a.shape[1]), np.float32)
        out[:a.shape[0]] = a
        return out

    def blocks(a):
        n = a.shape[0] // 128
        return a.reshape(n, 128, a.shape[1]).transpose(1, 0, 2).reshape(128, -1)

    def col(a):
        return a.reshape(-1, 128).T

    def row(a):
        return np.broadcast_to(a.reshape(1, -1), (128, a.size))

    L0, L1, L2, L3 = "L0_attn_", "L1_attn_", "L2_attn_", "L3_attn_"
    w = dict(
        wk=np.concatenate([f[L0 + "Wk"].T] * 2, 1), wq=np.concatenate([f[L0 + "Wq"].T] * 2, 1), wv=f[L0 + "Wv"].T,
        wout=f[L0 + "Wout"].T, f1=f["L0_ffn_W1"].T, f2=blocks(f["L0_ffn_W2"].T),
        q1=f[L1 + "qw"].T, k1=f[L1 + "kw"].T, v1=f[L1 + "vw"].T, o1=f[L1 + "ow"].T, w11=f[L1 + "w1"].T,
        w12=blocks(f[L1 + "w2"].T), gw1=f["L1_ffn_gate_w"], dw1=f["L1_ffn_dp_w1"], dw2=pad(f["L1_ffn_dp_w2"]),
        wi=f[L2 + "Wi"].T, wl1=f[L2 + "Wl1"].T, wl2=f[L2 + "Wl2"].T, memT=f[L2 + "mem_W"].T, wo2=f[L2 + "Wo"].T,
        wg=blocks(f[L2 + "Wg"].T), w21=f[L2 + "W1"].T, w22=blocks(f[L2 + "W2"].T), gw2=f["L2_ffn_gate"],
        ws1=f["L2_ffn_Ws1"], ws2=blocks(f["L2_ffn_Ws2"]), pT=f[L2 + "P"].T,
        qkv=f[L3 + "w_qkv"].T, w3o=f[L3 + "w_out"].T, gw3=f["L3_ffn_gate_w"],
        b2r=pad(f["L3_ffn_b2"]))
    b = dict(
        nw=col(f[L0 + "norm_weight"]), eta=np.concatenate([f[L0 + "eta"]] * 2).reshape(128, 1),
        f1b=col(f["L0_ffn_b1"]), f2b=col(f["L0_ffn_b2"]),
        g1=col(f[L1 + "norm_g"]), b1n=col(f[L1 + "norm_b"]), ob1=col(f[L1 + "ob"]), fg1=col(f[L1 + "ffn_norm_g"]),
        fb1=col(f[L1 + "ffn_norm_b"]), b11=col(f[L1 + "b1"]), b12=col(f[L1 + "b2"]),
        gb1=row(f["L1_ffn_gate_b"]), db1=pad(f["L1_ffn_dp_b1"].reshape(-1, 1)), db2=row(f["L1_ffn_dp_b2"]),
        eb1=col(f["L1_ffn_eb1"].reshape(-1)), eb2=col(f["L1_ffn_eb2"].reshape(-1)),
        memb=col(f[L2 + "mem_b"]), bi=col(f[L2 + "bi"]), bl1=col(f[L2 + "bl1"]), bl2=col(f[L2 + "bl2"]),
        bo2=col(f[L2 + "bo"]), fgate=row(f[L2 + "fgate"]), lrate=row(f[L2 + "lrate"]), bg=col(f[L2 + "bg"]),
        b21=col(f[L2 + "b1"]), b22=col(f[L2 + "b2"]), g21=col(f[L2 + "g1"]), be21=col(f[L2 + "be1"]),
        g22=col(f[L2 + "g2"]), be22=col(f[L2 + "be2"]), g23=col(f[L2 + "g3"]), be23=col(f[L2 + "be3"]),
        m2b1=col(f["L2_ffn_b1"].reshape(-1)), m2b2=col(f["L2_ffn_b2"].reshape(-1)), bs1=col(f["L2_ffn_bs1"]),
        bs2=col(f["L2_ffn_bs2"]),
        bqkv=col(f[L3 + "b_qkv"]), bo3=col(f[L3 + "b_out"]), m3b1=col(f["L3_ffn_b1"].reshape(-1)),
        gb3=row(f["L3_ffn_gate_b"]), bv3=row(f[L3 + "b_qkv"][256:384]))

    def moe(w1, w2):
        e = w1.shape[0]
        return np.concatenate([w1.transpose(1, 0, 2).reshape(128, -1),
                               w2.reshape(e, -1, 128, 128).transpose(2, 0, 1, 3).reshape(128, -1)], 1)

    c = constants()
    arrays = {
        "xT": f["L0_attn_x"].reshape(NB, NC, C, 128).transpose(3, 1, 0, 2).reshape(128, T),
        "early": np.concatenate([w[n] for n, _ in EARLY] + [c[n] for n, _ in ECONSTS], 1),
        "wts": np.concatenate([w[n] for n, _ in WEIGHTS], 1),
        "bia": np.concatenate([b[n] for n, _ in BIASES], 1),
        "con": np.concatenate([c[n] for n, _ in CONSTS], 1),
        "m1": moe(f["L1_ffn_ew1"], f["L1_ffn_ew2"]),
        "m2": moe(f["L2_ffn_W1"], f["L2_ffn_W2"]),
        "m3": moe(f["L3_ffn_w1"], f["L3_ffn_w2"]),
    }
    arrays = {k: np.ascontiguousarray(v, dtype=np.float32) for k, v in arrays.items()}
    nc = bacc.Bacc("TRN2", target_bir_lowering=False, num_devices=1)
    args = [nc.dram_tensor(k, v.shape, F32, kind="ExternalInput").ap() for k, v in arrays.items()]
    args.append(nc.dram_tensor("outT", (128, T), F32, kind="ExternalOutput").ap())
    program(nc, *args)
    r = run(nc, [arrays], core_ids=[0])
    return np.ascontiguousarray(r.results[0]["outT"].T).reshape(NB, S, 128)
```
